# Optimizing a Trainium2 kernel written in Bass

```python
import numpy as np
import jax
import jax.numpy as jnp

def _softmax(x, axis=-1):
    return jax.nn.softmax(x, axis=axis)

def _gelu(x):
    return jax.nn.gelu(x, approximate=True)

def _silu(x):
    return jax.nn.silu(x)

def _sigmoid(x):
    return jax.nn.sigmoid(x)

def _layernorm(x, axis=-1, eps=1e-05):
    m = jnp.mean(x, axis=axis, keepdims=True)
    v = jnp.var(x, axis=axis, keepdims=True)
    return (x - m) / jnp.sqrt(v + eps)

def _scatter_add(tgt, idx, src, axis=0):
    return tgt.at[idx].add(src)

def _segment_sum(src, seg, n):
    return jax.ops.segment_sum(src, seg, n)
kernel_name = 'mk_gnn_resnorm_d2_gnn_r32_424d79'

def setup_inputs(seed: int=0):
    np.random.seed(seed)
    _w = jnp.asarray

    def _rec_inputs():
        import jax
        import jax.numpy as jnp
        _gk = jax.random.key(seed)
        x = -0.000202 + 1 * jax.random.normal(jax.random.fold_in(_gk, 1), (3125, 128), jnp.float32)
        src = jax.random.randint(jax.random.fold_in(_gk, 2), (100000,), 0, 3125, jnp.int32)
        dst = jnp.minimum((3125 * jax.random.uniform(jax.random.fold_in(_gk, 3), (100000,)) ** 2.0).astype(jnp.int32), 99999)
        _o = jnp.argsort(dst, stable=True)
        src = src[_o]
        dst = dst[_o]
        edge_type_9 = jax.random.randint(jax.random.fold_in(_gk, 13), (100000,), 0, 9, jnp.int32)
        return (x, src, dst, edge_type_9)
    x, src, dst, edge_type_9 = _rec_inputs()

    def _L0_gnn_setup():
        import jax, jax.numpy as jnp
        import numpy as np
        NUM_EDGE_TYPES = 8
        HIDDEN = 128
        N_NODES = 50000
        N_EDGES = 18750

        def _gru_cell(x, h, W_ih, W_hh, b_ih, b_hh):
            H = h.shape[-1]
            gi = x @ W_ih.T + b_ih
            gh = h @ W_hh.T + b_hh
            i_r, i_z, i_n = (gi[:, :H], gi[:, H:2 * H], gi[:, 2 * H:])
            h_r, h_z, h_n = (gh[:, :H], gh[:, H:2 * H], gh[:, 2 * H:])
            r = jax.nn.sigmoid(i_r + h_r)
            z = jax.nn.sigmoid(i_z + h_z)
            n = jnp.tanh(i_n + r * h_n)
            return (1.0 - z) * n + z * h
        key = jax.random.key(seed)
        ks = jax.random.split(key, 10)
        H = HIDDEN
        h = jax.random.normal(ks[0], (N_NODES, H), dtype=jnp.float32)
        edge_index = jax.random.randint(ks[1], (2, N_EDGES), 0, N_NODES, dtype=jnp.int32)
        edge_type = jax.random.randint(ks[2], (N_EDGES,), 0, NUM_EDGE_TYPES + 1, dtype=jnp.int32)
        s = 1.0 / np.sqrt(H)
        W_msg = jax.random.uniform(ks[3], (H, H), jnp.float32, -s, s)
        b_msg = jax.random.uniform(ks[4], (H,), jnp.float32, -s, s)
        edge_embed = jax.random.normal(ks[5], (NUM_EDGE_TYPES + 1, H), dtype=jnp.float32)
        W_ih = jax.random.uniform(ks[6], (3 * H, H), jnp.float32, -s, s)
        W_hh = jax.random.uniform(ks[7], (3 * H, H), jnp.float32, -s, s)
        b_ih = jax.random.uniform(ks[8], (3 * H,), jnp.float32, -s, s)
        b_hh = jax.random.uniform(ks[9], (3 * H,), jnp.float32, -s, s)
        return {'h': h, 'edge_index': edge_index, 'edge_type': edge_type, 'num_nodes': N_NODES, 'W_msg': W_msg, 'b_msg': b_msg, 'edge_embed': edge_embed, 'W_ih': W_ih, 'W_hh': W_hh, 'b_ih': b_ih, 'b_hh': b_hh}
    _L0_gnn_all = _L0_gnn_setup()
    _L0_gnn_in = {k: v for k, v in _L0_gnn_all.items() if k in ('W_msg', 'b_msg', 'edge_embed', 'W_ih', 'W_hh', 'b_ih', 'b_hh')}
    del _L0_gnn_all

    def _L1_gnn_setup():
        import jax, jax.numpy as jnp
        import numpy as np
        N_NODES = 10000
        N_EDGES = 20000
        IN, HID, OUT = (128, 256, 128)

        def _mean_agg(h, src, dst, n_nodes):
            summed = jax.ops.segment_sum(h[src], dst, num_segments=n_nodes)
            deg = jax.ops.segment_sum(jnp.ones_like(dst, dtype=h.dtype), dst, num_segments=n_nodes)
            return summed / jnp.maximum(deg, 1.0)[:, None]

        def _sage_layer(h, src, dst, w_self, w_neigh, b):
            neigh = _mean_agg(h, src, dst, h.shape[0])
            return h @ w_self + neigh @ w_neigh + b
        key = jax.random.key(seed)
        ks = jax.random.split(key, 8)
        scale_in = 1.0 / np.sqrt(IN)
        scale_hid = 1.0 / np.sqrt(HID)
        return {'x': jax.random.normal(ks[0], (N_NODES, IN), dtype=jnp.float32), 'w_self1': jax.random.normal(ks[1], (IN, HID), dtype=jnp.float32) * scale_in, 'w_neigh1': jax.random.normal(ks[2], (IN, HID), dtype=jnp.float32) * scale_in, 'b1': jnp.zeros((HID,), dtype=jnp.float32), 'w_self2': jax.random.normal(ks[3], (HID, OUT), dtype=jnp.float32) * scale_hid, 'w_neigh2': jax.random.normal(ks[4], (HID, OUT), dtype=jnp.float32) * scale_hid, 'b2': jnp.zeros((OUT,), dtype=jnp.float32), 'src': jax.random.randint(ks[5], (N_EDGES,), 0, N_NODES, dtype=jnp.int64 if jax.config.jax_enable_x64 else jnp.int32), 'dst': jax.random.randint(ks[6], (N_EDGES,), 0, N_NODES, dtype=jnp.int64 if jax.config.jax_enable_x64 else jnp.int32)}
    _L1_gnn_all = _L1_gnn_setup()
    _L1_gnn_in = {k: v for k, v in _L1_gnn_all.items() if k in ('w_self1', 'w_neigh1', 'b1', 'w_self2', 'w_neigh2', 'b2')}
    del _L1_gnn_all
    return {'x': x, 'src': src, 'dst': dst, 'edge_type_9': edge_type_9, 'L0_gnn_W_msg': _L0_gnn_in['W_msg'], 'L0_gnn_b_msg': _L0_gnn_in['b_msg'], 'L0_gnn_edge_embed': _L0_gnn_in['edge_embed'], 'L0_gnn_W_ih': _L0_gnn_in['W_ih'], 'L0_gnn_W_hh': _L0_gnn_in['W_hh'], 'L0_gnn_b_ih': _L0_gnn_in['b_ih'], 'L0_gnn_b_hh': _L0_gnn_in['b_hh'], 'L1_gnn_w_self1': _L1_gnn_in['w_self1'], 'L1_gnn_w_neigh1': _L1_gnn_in['w_neigh1'], 'L1_gnn_b1': _L1_gnn_in['b1'], 'L1_gnn_w_self2': _L1_gnn_in['w_self2'], 'L1_gnn_w_neigh2': _L1_gnn_in['w_neigh2'], 'L1_gnn_b2': _L1_gnn_in['b2']}

def reference(x, src, dst, edge_type_9, L0_gnn_W_msg, L0_gnn_b_msg, L0_gnn_edge_embed, L0_gnn_W_ih, L0_gnn_W_hh, L0_gnn_b_ih, L0_gnn_b_hh, L1_gnn_w_self1, L1_gnn_w_neigh1, L1_gnn_b1, L1_gnn_w_self2, L1_gnn_w_neigh2, L1_gnn_b2):
    import jax
    import jax.numpy as jnp

    def _L0_gnn_ref(h, edge_index, edge_type, num_nodes, W_msg, b_msg, edge_embed, W_ih, W_hh, b_ih, b_hh):
        import jax, jax.numpy as jnp
        import numpy as np
        NUM_EDGE_TYPES = 8
        HIDDEN = 128
        N_NODES = 50000
        N_EDGES = 18750

        def _gru_cell(x, h, W_ih, W_hh, b_ih, b_hh):
            H = h.shape[-1]
            gi = x @ W_ih.T + b_ih
            gh = h @ W_hh.T + b_hh
            i_r, i_z, i_n = (gi[:, :H], gi[:, H:2 * H], gi[:, 2 * H:])
            h_r, h_z, h_n = (gh[:, :H], gh[:, H:2 * H], gh[:, 2 * H:])
            r = jax.nn.sigmoid(i_r + h_r)
            z = jax.nn.sigmoid(i_z + h_z)
            n = jnp.tanh(i_n + r * h_n)
            return (1.0 - z) * n + z * h
        src = edge_index[0]
        dst = edge_index[1]
        src_h = h[src] @ W_msg.T + b_msg
        emb = edge_embed[jnp.clip(edge_type, 0, NUM_EDGE_TYPES)]
        msg = src_h + emb
        messages = jax.ops.segment_sum(msg, dst, num_segments=num_nodes)
        h_new = _gru_cell(messages, h[:num_nodes], W_ih, W_hh, b_ih, b_hh)
        result = jnp.zeros_like(h).at[:num_nodes].set(h_new)
        return result

    def _L1_gnn_ref(x, w_self1, w_neigh1, b1, w_self2, w_neigh2, b2, src, dst):
        import jax, jax.numpy as jnp
        import numpy as np
        N_NODES = 10000
        N_EDGES = 20000
        IN, HID, OUT = (128, 256, 128)

        def _mean_agg(h, src, dst, n_nodes):
            summed = jax.ops.segment_sum(h[src], dst, num_segments=n_nodes)
            deg = jax.ops.segment_sum(jnp.ones_like(dst, dtype=h.dtype), dst, num_segments=n_nodes)
            return summed / jnp.maximum(deg, 1.0)[:, None]

        def _sage_layer(h, src, dst, w_self, w_neigh, b):
            neigh = _mean_agg(h, src, dst, h.shape[0])
            return h @ w_self + neigh @ w_neigh + b
        h = _sage_layer(x, src, dst, w_self1, w_neigh1, b1)
        h = jax.nn.relu(h)
        h = _sage_layer(h, src, dst, w_self2, w_neigh2, b2)
        return h
    edge_index = jnp.stack([src, dst])
    x = _layernorm(x + _L0_gnn_ref(x, edge_index, edge_type_9, 3125, L0_gnn_W_msg, L0_gnn_b_msg, L0_gnn_edge_embed, L0_gnn_W_ih, L0_gnn_W_hh, L0_gnn_b_ih, L0_gnn_b_hh), axis=-1)
    x = _layernorm(x + _L1_gnn_ref(x, L1_gnn_w_self1, L1_gnn_w_neigh1, L1_gnn_b1, L1_gnn_w_self2, L1_gnn_w_neigh2, L1_gnn_b2, src, dst), axis=-1)
    return x

_drawn_inputs = setup_inputs


def setup_inputs(seed=0):
    import zlib

    import numpy as np

    out = dict(_drawn_inputs(seed))
    spreads = {'L1_gnn_b1': (0.0, 0.1), 'L1_gnn_b2': (0.0, 0.1)}
    factors = {'L0_gnn_b_ih': 7.566, 'L0_gnn_b_hh': 8.0}
    for name, (base, spread) in spreads.items():
        noise = np.random.default_rng([zlib.crc32(name.encode()), seed]).standard_normal(out[name].shape)
        drawn = base * np.exp(spread * noise) if base else spread * noise
        out[name] = jnp.asarray(drawn.astype(out[name].dtype))
    for name, factor in factors.items():
        out[name] = (out[name] * factor).astype(out[name].dtype)
    return out
```

```python
import concourse.bass as bass
from concourse import mybir
from contextlib import ExitStack

N, E, F, H2, NTYPE = 3125, 100000, 128, 256, 9
P = 128
TILES = -(-N // P)
LAST = N - (TILES - 1) * P
LASTW = 64
DW = (TILES - 1) * P + LASTW
CHUNKS = -(-E // P)
FULL = E // P
TAIL = E - FULL * P
U = 4
DRING = 16
CP = CHUNKS + U
DIGITS, GROUPS = 5, 5
SPAN = GROUPS * P
PAD_DST = 4000
CENTER = N // 2
NC = TILES // 4
PARTS = 3
SCRATCH = 2048


def graph_kernel(nc, x, xT, dst_c, dst_t, src_c, src_t, typ_c, typ_t, wmsgT, bmsg, embed, wihT, whhT,
                 bgate, wself1, wneigh1, b1, wself2, wneigh2, b2, x1_dram, y_dram, res_dram, out):
    fp32, bf16, fp16 = mybir.dt.float32, mybir.dt.bfloat16, mybir.dt.float16
    i32, u32 = mybir.dt.int32, mybir.dt.uint32
    ALU, ACT, AX = mybir.AluOpType, mybir.ActivationFunctionType, mybir.AxisListType
    SIZE = {fp32: 4, i32: 4, u32: 4, bf16: 2, fp16: 2}
    ds = bass.ds
    ctx = ExitStack()

    top = [nc.sbuf_base + (-nc.sbuf_base) % 32]

    def nbytes(shape, dt):
        n = SIZE[dt]
        for s in shape[1:]:
            n *= s
        return n + (-n) % 32

    def place(region, name, shape, dt):
        t = nc.alloc_sbuf_tensor_at(name, shape, dt, offset=region[0])
        region[0] += nbytes(shape, dt)
        return t

    def region(size):
        at = top[0]
        top[0] += size + (-size) % 32
        return at

    def sb(name, shape, dt):
        return place(top, name, shape, dt)

    part_bytes = TILES * PARTS * F * 2
    AT_at = region(TILES * DW * 2)
    AT = place([AT_at], "AT", [P, TILES, DW], bf16)
    A_at, B_at, W_at = region(part_bytes), region(part_bytes), region(CP * NTYPE * 2 + SPAN * 4 + 64)

    r = [A_at]
    digits = place(r, "digits", [P, DIGITS, SPAN], i32)
    packedT = place(r, "packedT", [P, 2, SPAN], i32)
    bmsg_b, emb_s = (place(r, n, [NTYPE, F], fp32) for n in ("bmsg_b", "emb_s"))
    r = [A_at]
    raw_dst, raw_src, raw_typ = (place(r, n, [P, CP], i32) for n in ("raw_dst", "raw_src", "raw_typ"))
    first_i = place(r, "first_i", [TILES, CHUNKS], i32)
    last_i = place(r, "last_i", [TILES, CHUNKS], i32)
    r = [AT_at]
    edge_f = place(r, "edge_f", [P, CP], fp32)
    weight_a = place(r, "weight_a", [P, CP], fp32)
    weight_b = place(r, "weight_b", [P, CP], fp32)
    digit_a = place(r, "digit_a", [P, CP], fp32)
    digit_b = place(r, "digit_b", [P, CP], fp32)
    first_f = place(r, "first_f", [TILES, CHUNKS], fp32)
    last_f = place(r, "last_f", [TILES, CHUNKS], fp32)
    passed = place(r, "passed", [TILES, CHUNKS], bf16)
    r = [B_at]
    dst_f = place(r, "dst_f", [P, CP], fp32)
    src_col = place(r, "src_col", [P, CP], fp32)
    src_w = place(r, "src_w", [P, CP], fp32)
    S = place(r, "S", [P, U, SPAN], bf16)
    D_even = place(r, "D_even", [P, U // 2, P], bf16)
    D_odd = place(r, "D_odd", [P, DRING // 2, P], bf16)
    pool_off = place(r, "pool_off", [P, 1], fp32)
    pool_dst = place(r, "pool_dst", [P, U], fp32)
    assert r[0] <= B_at + part_bytes
    r = [W_at]
    T = place(r, "T", [P, CP, NTYPE], bf16)
    packed = place(r, "packed", [P, SPAN], fp32)
    x1p = place([A_at], "x1p", [P, TILES, PARTS, F], bf16)
    xp = place([B_at], "xp", [P, TILES, PARTS, F], bf16)
    xstage = place([W_at], "xstage", [P, TILES, F], fp32)
    slot = [place([W_at + 2048 * k], f"slot{k}", [P, 512], fp32) for k in range(8)]
    assert W_at + 8 * 2048 <= top[0]

    iota_h = sb("iota_h", [P, SPAN], fp16)
    iota_t = sb("iota_t", [P, P], fp16)
    dist = sb("dist", [P, 2, P], bf16)
    tile_off = sb("tile_off", [P, TILES], fp32)
    zero = sb("zero", [P, P], bf16)
    Cn = sb("Cn", [P, 4 * (NC + 1), NTYPE], fp32)
    c_stage = sb("c_stage", [P, 4, NTYPE], fp32)
    count = sb("count", [P, TILES, DIGITS], fp32)
    top_max = sb("top_max", [P, TILES], fp32)
    ident = sb("ident", [P, P], fp32)
    ones = sb("ones", [P, P], fp32)
    before = sb("before", [TILES, TILES], fp32)
    thr = sb("thr", [TILES, 2], fp32)
    tcol = sb("tcol", [TILES, 8], fp32)
    tcol_i = sb("tcol_i", [TILES, 2], i32)
    table = sb("table", [1, 3 * 32], i32)
    verdict = sb("verdict", [P, 4], fp32)
    flag = sb("flag", [1, 4], fp32)
    flag_i = sb("flag_i", [1, 4], i32)
    ideg = sb("ideg", [P, TILES], fp32)
    wmsg_s = sb("wmsg_s", [F, F], fp32)
    wih_s = sb("wih_s", [F, 3, F], fp32)
    whh_s = sb("whh_s", [F, 3, F], fp32)
    ws1 = sb("ws1", [F, 2, F], fp32)
    wn1 = sb("wn1", [F, 2, F], fp32)
    ws2 = sb("ws2", [F, 2, F], fp32)
    wn2 = sb("wn2", [F, 2, F], fp32)
    emb_b = sb("emb_b", [NTYPE, F], fp32)
    gate_b = sb("gate_b", [F, 6], fp32)
    rz_b = sb("rz_b", [F, 2], fp32)
    b1_s = sb("b1_s", [F, 2], fp32)
    b2_b = sb("b2_b", [P, F], fp32)
    stats = sb("stats", [P, 4, 6], fp32)
    meanvar = sb("meanvar", [P, 4, 2], fp32)
    sd = sb("sd", [P, 4], fp32)
    rstd = sb("rstd", [P, 4], fp32)
    eps = sb("eps", [P, 1], fp32)
    assert top[0] <= nc.sbuf_usable_end, (top[0], nc.sbuf_usable_end)

    r = [AT_at]
    g_iota = place(r, "g_iota", [P, TILES * P], fp32)
    g_onehot = place(r, "g_onehot", [P, TILES * P], fp32)
    g_src = place(r, "g_src", [P, CP], i32)
    g_dst_i = place(r, "g_dst_i", [P, CP], i32)
    g_typ_i = place(r, "g_typ_i", [P, CP], i32)
    g_dst = place(r, "g_dst", [P, CP], fp32)
    g_typ = place(r, "g_typ", [P, CP], fp32)
    g_idx = place(r, "g_idx", [P, 1], i32)
    g_rows = place(r, "g_rows", [P, F], fp32)
    g_sum = place(r, "g_sum", [P, 4 * (NC + 1), F], fp32)
    g_stage = place(r, "g_stage", [P, 4, F], fp32)
    assert r[0] <= A_at

    with ctx:
        PS = ctx.enter_context(nc.psum_tensor("PS", [P, 8, 512], fp32))
        sems = {}

        def sem(name):
            if name not in sems:
                sems[name] = ctx.enter_context(nc.semaphore(name))
            return sems[name]

        weights = [(wmsg_s[:, :], wmsgT), (wih_s[:, :, :], wihT.rearrange("k (g m) -> k g m", g=3)),
                   (whh_s[:, :, :], whhT.rearrange("k (g m) -> k g m", g=3)),
                   (ws1[:, :, :], wself1.rearrange("k (g m) -> k g m", g=2)),
                   (wn1[:, :, :], wneigh1.rearrange("k (g m) -> k g m", g=2)),
                   (ws2[:, :, :], wself2.rearrange("(g k) m -> k g m", g=2)),
                   (wn2[:, :, :], wneigh2.rearrange("(g k) m -> k g m", g=2)),
                   (emb_s[:, :], embed), (bmsg_b[:, :], bmsg.partition_broadcast(NTYPE)),
                   (gate_b[:, :], bgate), (b1_s[:, :], b1), (b2_b[:, :], b2.partition_broadcast(P))]

        def load_tile_entry(eng, t):
            lo = eng.value_load(table[0:1, ds(t, 1)], min_val=0, max_val=CHUNKS - 1)
            nb = eng.value_load(table[0:1, ds(t + 32, 1)], min_val=1, max_val=-(-CHUNKS // U))
            st = eng.value_load(table[0:1, ds(t + 64, 1)], min_val=0, max_val=TILES * -(-CHUNKS // U))
            return lo, nb, st

        def settle(eng, name):
            eng.sem_inc(sem(name), 1)

        def by_twos(q, start, end):
            return q.with_bounds(min_val=start, max_val=end - 2 + (end - start) % 2)

        def first_chunk(lo, i):
            return (lo + i * U).with_bounds(min_val=0, max_val=CP - U)

        def is_general(eng):
            return eng.value_load(flag_i[0:1, 0:1], min_val=0, max_val=1)

        def xrest(c):
            return packedT[:, c % 2, 0:512].bitcast(fp32)

        def general_rows(dve, v, general):
            def call(n):
                with dve.If(general):
                    if n == 0:
                        dve.wait_ge(sem("g_edges_in"), 96)
                        v.tensor_copy(g_dst[:, :], g_dst_i[:, :])
                        v.tensor_scalar(g_typ[:, :], g_typ_i[:, :], 0.0, float(NTYPE - 1), ALU.max, ALU.min).then_inc(sem("g_start"), 1)
                    else:
                        dve.wait_ge(sem("g_copied"), n)
                        v.memset(flag[:, 2:3], 0.0).then_inc(sem("g_start"), 1)
                    dve.wait_ge(sem("g_start"), n + 1)
                    with dve.Fori(0, CHUNKS) as c:
                        dve.wait_ge(sem("g_used"), c + n * CHUNKS)
                        v.tensor_scalar(g_onehot[:, :], g_iota[:, :], g_dst[:, ds(c, 1)], None, ALU.is_equal).then_inc(sem("g_onehot_set"), 1)
                        if n == 0:
                            v.tensor_scalar(g_rows[:, 0:NTYPE], g_iota[:, 0:NTYPE], g_typ[:, ds(c, 1)], None, ALU.is_equal).then_inc(sem("g_types_set"), 1)
                        else:
                            v.tensor_copy(g_idx[:, :], g_src[:, ds(c, 1)]).then_inc(sem("g_idx_set"), 1)
                with dve.Else():
                    dve.nop()
            return call

        block = ctx.enter_context(nc.Block())

        def is_general_after_flag(eng):
            eng.wait_ge(sem("flag_set"), 1)
            return is_general(eng)

        @block.sync
        def _(sp):
            sp.wait_ge(sem("pads_set"), 1)
            for name, ti, m, t in (("dst_in", raw_dst, dst_c, dst_t), ("src_in", raw_src, src_c, src_t),
                                   ("typ_in", raw_typ, typ_c, typ_t)):
                sp.dma_start(ti[:, 0:FULL], m).then_inc(sem(name), 16)
                sp.dma_start(ti[0:TAIL, FULL:FULL + 1], t).then_inc(sem(name), 16)
            sp.dma_start(first_i[:, 0:FULL], dst_c[0:1, :].partition_broadcast(TILES)).then_inc(sem("ends_in"), 16)
            sp.dma_start(first_i[:, FULL:CHUNKS], dst_t[0:1, :].partition_broadcast(TILES)).then_inc(sem("ends_in"), 16)
            sp.dma_start(last_i[:, 0:FULL], dst_c[P - 1:P, :].partition_broadcast(TILES)).then_inc(sem("ends_in"), 16)
            for to, of in weights:
                sp.dma_start(to, of).then_inc(sem("weights_in"), 16)
            sp.wait_ge(sem("tiles_summed"), TILES)
            for c in range(NC):
                sp.dma_start(xstage[:, 4 * c:4 * c + 4, :],
                             x[512 * c:512 * c + 512, :].rearrange("(t p) f -> p t f", p=P)).then_inc(sem(f"x_in{c}"), 16)
            sp.dma_start(xstage[0:LAST, TILES - 1, :], x[(TILES - 1) * P:N, :]).then_inc(sem(f"x_in{NC}"), 16)

            general = is_general_after_flag(sp)
            with sp.If(general):
                sp.wait_ge(sem("g_pads_set"), 1)
                for ti, m, t in ((g_dst_i, dst_c, dst_t), (g_src, src_c, src_t), (g_typ_i, typ_c, typ_t)):
                    sp.dma_start(ti[:, 0:FULL], m).then_inc(sem("g_edges_in"), 16)
                    sp.dma_start(ti[0:TAIL, FULL:FULL + 1], t).then_inc(sem("g_edges_in"), 16)
            with sp.Else():
                sp.nop()

            def pass1(q, w, cols, rows):
                if not isinstance(q, int) or q > 0:
                    sp.wait_ge(sem("p1_y"), q)
                sp.dma_start(slot[2][:, 0:cols], xT[:, ds(q * 512, cols)]).then_inc(sem("p1_xT_in"), 16)
                sp.wait_ge(sem("p1_x1"), q + 1)
                if rows == P:
                    sp.dma_start(x1_dram[ds(q * 512, 512), :].rearrange("(t p) f -> p t f", p=P),
                                 slot[5][:, :].rearrange("p (t f) -> p t f", f=F)).then_inc(sem("p1_x1_out"), 16)
                else:
                    sp.dma_start(x1_dram[ds(q * 512, LASTW), :], slot[5][0:LASTW, 0:F]).then_inc(sem("p1_x1_out"), 16)

            sp.wait_ge(sem("x_split"), 1)
            with sp.Fori(0, NC) as q:
                pass1(q, 512, 512, P)
            pass1(NC, LASTW, LAST, LASTW)

            sp.wait_ge(sem("p1_x1_out"), 16 * (NC + 1))

            def rows_dma(dram, sl, q, last, store, name):
                if last:
                    at, tile_rows = dram[ds(q * 512, LASTW), :], sl[0:LASTW, 0:F]
                else:
                    at = dram[ds(q * 512, 512), :].rearrange("(t p) f -> p t f", p=P)
                    tile_rows = sl[:, :].rearrange("p (t f) -> p t f", f=F)
                to, of = (at, tile_rows) if store else (tile_rows, at)
                sp.dma_start(to, of).then_inc(sem(name), 16)

            def pass2_store(q, last):
                sp.wait_ge(sem("p2_yf"), q + 1)
                rows_dma(y_dram, slot[4], q, last, True, "p2_y_out")
                sp.wait_ge(sem("p2_res"), q + 1)
                rows_dma(res_dram, slot[5], q, last, True, "p2_res_out")

            sp.wait_ge(sem("p1_done"), 1)
            rows_dma(x1_dram, slot[2], 0, False, False, "p2_x1_in")
            with sp.Fori(1, NC) as q:
                sp.wait_ge(sem("p2_x1T"), q)
                rows_dma(x1_dram, slot[2], q, False, False, "p2_x1_in")
                pass2_store(q - 1, False)
            sp.wait_ge(sem("p2_x1T"), NC)
            rows_dma(x1_dram, slot[2], NC, True, False, "p2_x1_in")
            pass2_store(NC - 1, False)
            pass2_store(NC, True)
            sp.wait_ge(sem("p2_res_out"), 16 * (NC + 1))
            sp.wait_ge(sem("p2_y_out"), 16 * (NC + 1))

            def rows_in(q, par, last=False):
                if not isinstance(q, int) or q >= 2:
                    sp.wait_ge(sem("p3_sum"), 3 * (q - 1))
                rows_dma(res_dram, slot[par], q, last, False, f"p3_in{par}")
                rows_dma(x1_dram, slot[2 + par], q, last, False, f"p3_in{par}")

            def rows_out(q, par):
                sp.wait_ge(sem("p3_out"), q + 1)
                rows_dma(out, slot[6 + par], q, False, True, f"p3_stored{par}")

            sp.wait_ge(sem("p2_done"), 1)
            rows_in(0, 0)
            rows_in(1, 1)
            with sp.Fori(0, NC - 2, 2) as q:
                q = by_twos(q, 0, NC - 2)
                rows_in(q + 2, 0)
                rows_out(q, 0)
                rows_in(q + 3, 1)
                rows_out(q + 1, 1)
            rows_in(NC, 0, last=True)
            rows_out(NC - 2, 0)
            rows_out(NC - 1, 1)
            sp.wait_ge(sem("p3_out"), NC + 1)
            sp.dma_start(out[NC * 512:N, :], slot[6][0:LAST, 0:F]).then_inc(sem("p3_stored0"), 16)
            sp.wait_ge(sem("p3_stored0"), 16 * (NC // 2 + 1))
            sp.wait_ge(sem("p3_stored1"), 16 * (NC // 2))

        @block.gpsimd
        def _(pool):
            g = nc.gpsimd
            g.memset(raw_dst[:, FULL:CP], PAD_DST)
            g.memset(raw_src[:, FULL:CP], 0)
            g.memset(raw_typ[:, FULL:CP], 0).then_inc(sem("pads_set"), 1)
            g.iota(iota_h[:, :], pattern=[[1, SPAN]], base=0, channel_multiplier=0, allow_small_or_imprecise_dtypes=True)
            g.iota(tile_off[:, :], pattern=[[P, TILES]], base=-CENTER, channel_multiplier=0, allow_small_or_imprecise_dtypes=True)
            g.iota(thr[:, :], pattern=[[P, 2]], base=0, channel_multiplier=P, allow_small_or_imprecise_dtypes=True)
            g.memset(zero[:, :], 0.0)
            g.memset(ones[:, :], 1.0)
            g.memset(eps[:, :], 1e-5)
            g.memset(Cn[:, TILES:, :], 0.0)
            g.memset(before[:, :], 1.0)
            g.memset(ident[:, :], 0.0).then_inc(sem("filled"), 1)
            pool.wait_ge(sem("filled"), 1)
            g.affine_select(out=before[:, :], in_=before[:, :], compare_op=ALU.is_gt, fill=0.0,
                            base=0, pattern=[[1, TILES]], channel_multiplier=-1)
            g.affine_select(out=ident[:, :], in_=ident[:, :], compare_op=ALU.not_equal, fill=1.0,
                            base=0, pattern=[[-1, P]], channel_multiplier=1).then_inc(sem("consts"), 1)

            pool.wait_ge(sem("table_set"), 1)
            with pool.Fori(0, TILES) as t:
                lo, nb, st = load_tile_entry(pool, t)
                pool.wait_ge(sem("D_pool"), st * 2)
                g.tensor_copy(pool_off[:, :], tile_off[:, ds(t, 1)]).then_inc(sem("pool_off_set"), 1)
                with pool.Fori(0, nb) as i:
                    c0 = first_chunk(lo, i)
                    pool.wait_ge(sem("pool_off_set"), t + 1)
                    pool.wait_ge(sem("D_pool"), (st + i) * 2)
                    g.tensor_copy(pool_dst[:, :], dst_f[:, ds(c0, U)]).then_inc(sem("pool_dst_set"), 1)
                    pool.wait_ge(sem("pool_dst_set"), st + i + 1)
                    for n, u in enumerate((0, 2)):
                        pool.wait_ge(sem("items_done"), (st + i) * U + (u + 1 + DRING - U))
                        settle(pool, "pool_settled")
                        g.tensor_scalar(D_even[:, n, :], iota_h[:, 0:P], pool_off[:, :], pool_dst[:, u:u + 1],
                                        ALU.add, ALU.is_equal).then_inc(sem("D_pool"), 1)

            pool.wait_ge(sem("tiles_summed"), TILES)
            g.memset(xp[:, TILES - 1, :, :], 0.0).then_inc(sem("xp_zeroed"), 1)
            pool.wait_ge(sem("digits_stored"), (TILES + 1) * DIGITS)
            g.memset(x1p[:, TILES - 1, :, :], 0.0).then_inc(sem("x1p_zeroed"), 1)

            general = is_general_after_flag(pool)
            with pool.If(general):
                g.memset(g_dst_i[:, FULL:CP], PAD_DST)
                g.memset(g_src[:, FULL:CP], 0)
                g.memset(g_typ_i[:, FULL:CP], 0)
                g.memset(g_sum[:, TILES:, :], 0.0)
                g.iota(g_iota[:, :], pattern=[[1, TILES * P]], base=0, channel_multiplier=0,
                       allow_small_or_imprecise_dtypes=True).then_inc(sem("g_pads_set"), 1)
            with pool.Else():
                pool.nop()

            def gather(call, table_dram):
                with pool.If(general):
                    with pool.Fori(0, CHUNKS) as c:
                        pool.wait_ge(sem("g_idx_set"), c + (call - 1) * CHUNKS + 1)
                        settle(pool, "pool_settled")
                        g.indirect_dma_start(g_rows[:, :], None, table_dram,
                                             bass.IndirectOffsetOnAxis(ap=g_idx[:, 0:1].bitcast(u32), axis=0)).then_inc(sem("g_rows_in"), 16)
                with pool.Else():
                    pool.nop()

            def low_parts(name, target, q, last):
                rows, k = (LASTW, 1) if last else (P, 4)
                full = slot[5 if name == "p1" else 4][0:rows, 0:k * F].rearrange("p (t f) -> p t f", f=F)
                rest = slot[6 if name == "p1" else 0][0:rows, 0:k * F].rearrange("p (t f) -> p t f", f=F)
                hi, mid, low = (target[0:rows, ds(4 * q, k), n, :] for n in range(PARTS))
                pool.wait_ge(sem(f"{name}_hi"), q + 1)
                g.tensor_tensor(rest, full, hi, ALU.subtract).then_inc(sem(f"{name}_rest"), 1)
                pool.wait_ge(sem(f"{name}_mid"), q + 1)
                g.tensor_tensor(low, rest, mid, ALU.subtract).then_inc(sem(f"{name}_low"), 1)

            gather(1, x)
            with pool.Fori(0, NC) as q:
                low_parts("p1", x1p, q, False)
            low_parts("p1", x1p, NC, True)
            with pool.If(general):
                pool.wait_ge(sem("p1_x1_out"), 16 * (NC + 1))
            with pool.Else():
                pool.nop()
            gather(2, x1_dram)
            with pool.Fori(0, NC) as q:
                low_parts("p2", xp, q, False)
            low_parts("p2", xp, NC, True)
            with pool.If(general):
                pool.wait_ge(sem("p2_y_out"), 16 * (NC + 1))
            with pool.Else():
                pool.nop()
            gather(3, y_dram)

        @block.vector
        def _(dve):
            v = nc.vector
            chain = [0]

            def then(ins):
                chain[0] += 1
                ins.then_inc(sem("dve_chain"), 1)
                dve.wait_ge(sem("dve_chain"), chain[0])

            dve.wait_ge(sem("ends_in"), 48)
            dve.wait_ge(sem("consts"), 1)
            v.tensor_copy(first_f[:, :], first_i[:, :])
            then(v.tensor_copy(last_f[:, 0:FULL], last_i[:, 0:FULL]))
            then(v.tensor_scalar(passed[:, :], first_f[:, :], thr[:, 1:2], None, ALU.is_lt, ALU.add, accum_out=tcol[:, 0:1]))
            then(v.tensor_scalar(passed[:, 0:FULL], last_f[:, 0:FULL], thr[:, 0:1], None, ALU.is_lt, ALU.add, accum_out=tcol[:, 1:2]))
            then(v.tensor_scalar(tcol[:, 2:3], tcol[:, 1:2], float(CHUNKS - 1), None, ALU.min))
            then(v.tensor_tensor(tcol[:, 3:4], tcol[:, 0:1], tcol[:, 2:3], ALU.subtract))
            then(v.tensor_scalar(tcol[:, 4:5], tcol[:, 3:4], 1.0, float(U - 1), ALU.max, ALU.add))
            then(v.tensor_copy(tcol_i[:, 0:1], tcol[:, 4:5]))
            then(v.tensor_scalar(tcol_i[:, 1:2], tcol_i[:, 0:1], U.bit_length() - 1, None, ALU.logical_shift_right))
            v.tensor_copy(tcol[:, 5:6], tcol_i[:, 1:2]).then_inc(sem("tile_columns"), 1)
            dve.wait_ge(sem("table_rows"), 1)
            v.tensor_copy(table[:, :].rearrange("a (n t) -> a n t", n=3)[:, :, 0:TILES],
                          PS[0:1, 6, 0:96].rearrange("a (n t) -> a n t", n=3)[:, :, 0:TILES]).then_inc(sem("table_copied"), 1)

            dve.wait_ge(sem("dst_in"), 32)
            v.tensor_scalar(dst_f[:, :], raw_dst[:, :], float(-CENTER), None, ALU.add)
            dve.wait_ge(sem("src_in"), 32)
            then(v.tensor_copy(edge_f[:, :], raw_src[:, :]))
            (dg, dg2), (wt, wt2) = (digit_a, digit_b), (weight_a, weight_b)
            v.tensor_scalar(dg[:, :], edge_f[:, :], float(SPAN), None, ALU.is_ge)
            then(v.tensor_scalar(wt[:, :], edge_f[:, :], float(SPAN), 15.0, ALU.is_ge, ALU.mult))
            for k in range(2, DIGITS):
                then(v.scalar_tensor_tensor(out=dg2[:, :], in0=edge_f[:, :], scalar=float(SPAN * k), in1=dg[:, :], op0=ALU.is_ge, op1=ALU.add))
                dg, dg2 = dg2, dg
                then(v.tensor_scalar(src_w[:, :], edge_f[:, :], float(SPAN * k), 15.0 * 16 ** (k - 1), ALU.is_ge, ALU.mult))
                then(v.tensor_tensor(wt2[:, :], wt[:, :], src_w[:, :], ALU.add))
                wt, wt2 = wt2, wt
            v.tensor_scalar(src_w[:, :], wt[:, :], 1.0, None, ALU.add)
            v.scalar_tensor_tensor(out=src_col[:, :], in0=dg[:, :], scalar=float(-SPAN), in1=edge_f[:, :], op0=ALU.mult, op1=ALU.add)
            dve.wait_ge(sem("weights_in"), 16 * len(weights))
            v.tensor_tensor(rz_b[:, :], gate_b[:, 0:2], gate_b[:, 3:5], ALU.add)
            v.tensor_tensor(emb_b[:, :], emb_s[:, :], bmsg_b[:, :], ALU.add)
            dve.wait_ge(sem("typ_in"), 32)
            for k in range(NTYPE):
                if k == 0:
                    ins = v.tensor_scalar(T[:, :, k], raw_typ[:, :], 0.0, None, ALU.is_le)
                elif k == NTYPE - 1:
                    ins = v.tensor_scalar(T[:, :, k], raw_typ[:, :], float(k), None, ALU.is_ge)
                else:
                    ins = v.tensor_scalar(T[:, :, k], raw_typ[:, :], float(k), None, ALU.is_equal)
            then(ins)
            v.memset(verdict[:, 2:3], 0.0).then_inc(sem("table_set"), 1)

            def take_digits(t, par):
                dve.wait_ge(sem("packedT_in"), t + 1)
                for f in range(DIGITS):
                    dve.wait_ge(sem("digits_stored"), t * DIGITS + f + 1)
                    if f == DIGITS - 1 and (not isinstance(t, int) or t > 0):
                        dve.wait_ge(sem("top_max_set"), t)
                    if f < DIGITS - 1:
                        ins = v.tensor_scalar(digits[:, f, :], packedT[:, par, :], 4 * f, 15, ALU.logical_shift_right, ALU.bitwise_and)
                    else:
                        ins = v.tensor_scalar(digits[:, f, :], packedT[:, par, :], 4 * f, None, ALU.logical_shift_right)
                    ins.then_inc(sem("digits_taken"), 1)
                dve.wait_ge(sem("digits_taken"), (t + 1) * DIGITS)
                v.tensor_reduce(top_max[:, ds(t, 1)], digits[:, DIGITS - 1, :], AX.X, ALU.max).then_inc(sem("top_max_set"), 1)

            def source_rows(t):
                lo, nb, st = load_tile_entry(dve, t)
                with dve.Fori(0, nb) as i:
                    c0 = first_chunk(lo, i)
                    for u in range(U):
                        dve.wait_ge(sem("items_done"), (st + i) * U + (u + 1 + DRING - U))
                        v.tensor_scalar(S[:, u, :], iota_h[:, :], src_col[:, ds(c0 + u, 1)], src_w[:, ds(c0 + u, 1)],
                                        ALU.is_equal, ALU.mult).then_inc(sem("S_set"), 1)

            LAG = 3
            for t in range(LAG):
                source_rows(t)
            with dve.Fori(LAG, TILES, 2) as t:
                t = by_twos(t, LAG, TILES)
                source_rows(t)
                take_digits(t - LAG, 0)
                source_rows(t + 1)
                take_digits(t + 1 - LAG, 1)
            for t in range(TILES - LAG, TILES):
                take_digits(t, t % 2)

            dve.wait_ge(sem("digits_stored"), (TILES + 1) * DIGITS)
            dve.wait_ge(sem("top_max_set"), TILES)
            v.tensor_reduce(verdict[:, 0:1], count[:, :, :], AX.XY, ALU.add)
            then(v.tensor_reduce(verdict[:, 2:3], top_max[:, :], AX.X, ALU.max))
            v.tensor_scalar(verdict[:, 1:2], verdict[:, 2:3], 255.0, None, ALU.is_gt).then_inc(sem("verdict_set"), 1)
            dve.wait_ge(sem("verdict_sum"), 1)
            then(v.tensor_scalar(flag[:, 0:1], PS[0:1, 7, 0:1], float(E), None, ALU.not_equal))
            then(v.scalar_tensor_tensor(out=flag[:, 1:2], in0=PS[0:1, 7, 1:2], scalar=0.5, in1=flag[:, 0:1], op0=ALU.is_gt, op1=ALU.max))
            v.tensor_copy(flag_i[:, 0:1], flag[:, 1:2]).then_inc(sem("flag_set"), 1)

            dve.wait_ge(sem("xp_zeroed"), 1)
            for c in range(NC + 1):
                rows, k = (P, 4) if c < NC else (LAST, 1)
                dve.wait_ge(sem("x_hi"), c + 1)
                full = xstage[0:rows, 4 * c:4 * c + k, :]
                rest = xrest(c)[0:rows, 0:k * F].rearrange("p (t f) -> p t f", f=F)
                if c >= 2:
                    dve.wait_ge(sem("x_low"), c - 1)
                v.tensor_tensor(rest, full, xp[0:rows, 4 * c:4 * c + k, 0, :], ALU.subtract).then_inc(sem("x_rest"), 1)
                dve.wait_ge(sem("x_mid"), c + 1)
                v.tensor_tensor(xp[0:rows, 4 * c:4 * c + k, 2, :], rest, xp[0:rows, 4 * c:4 * c + k, 1, :], ALU.subtract).then_inc(sem("x_low"), 1)
            dve.wait_ge(sem("x_low"), NC + 1)
            v.memset(flag[:, 3:4], 0.0).then_inc(sem("x_split"), 1)

            general = is_general(dve)
            calls = general_rows(dve, v, general)
            calls(0)
            calls(1)

            dve.wait_ge(sem("types_ready"), 1)
            then(v.tensor_reduce(ideg[:, :], Cn[:, 0:TILES, :], AX.X, ALU.add))
            then(v.tensor_scalar(ideg[:, :], ideg[:, :], 1.0, None, ALU.max))
            then(v.reciprocal(ideg[:, :], ideg[:, :]))

            def pass1(q, w, last):
                rows, k = (LASTW, 1) if last else (P, 4)
                sT, mT, x_, rr, zz, tt, nn, yy = (slot[n][:, 0:w] for n in range(8))
                dve.wait_ge(sem("p1_m_sum"), q + 1)
                v.tensor_copy(mT, PS[:, 3, 0:w]).then_inc(sem("p1_m"), 1)
                dve.wait_ge(sem("p1_gates"), q + 1)
                dve.wait_ge(sem("p1_r"), q + 1)
                dve.wait_ge(sem("p1_x1_out"), 16 * q)
                dve.wait_ge(sem("p1_low"), q)
                v.scalar_tensor_tensor(out=tt, in0=PS[:, 7, 0:w], scalar=gate_b[:, 5:6], in1=rr, op0=ALU.add, op1=ALU.mult).then_inc(sem("p1_t"), 1)
                dve.wait_ge(sem("p1_t"), 2 * q + 1)
                v.tensor_tensor(tt, tt, PS[:, 6, 0:w], ALU.add).then_inc(sem("p1_t"), 1)
                dve.wait_ge(sem("p1_n"), q + 1)
                v.tensor_tensor(rr, x_, nn, ALU.subtract).then_inc(sem("p1_e"), 1)
                v.tensor_tensor(tt, x_, nn, ALU.add).then_inc(sem("p1_e"), 1)
                dve.wait_ge(sem("p1_e"), 3 * q + 1)
                v.tensor_tensor(zz, zz, rr, ALU.mult).then_inc(sem("p1_e"), 1)
                dve.wait_ge(sem("p1_e"), 3 * q + 3)
                v.tensor_tensor(yy, zz, tt, ALU.add).then_inc(sem("p1_y"), 1)
                dve.wait_ge(sem("p1_yT"), q + 1)
                norm("p1", q, rows, k, lambda n: PS[0:rows, 3, n * F:(n + 1) * F], slot[5], "p1_x1")

            def norm(name, q, rows, k, row_of, to, done, par=None):
                for n in range(k):
                    ins = v.bn_stats(stats[0:rows, n, :], row_of(n))
                ins.then_inc(sem(f"{name}_norm"), 1)
                dve.wait_ge(sem(f"{name}_norm"), 3 * q + 1)
                dve.wait_ge(sem(done), q)
                settle(dve, "dve_settled")
                for n in range(k):
                    ins = v.bn_aggr(meanvar[0:rows, n, :], stats[0:rows, n, :])
                ins.then_inc(sem(f"{name}_norm"), 1)
                dve.wait_ge(sem(f"{name}_sd"), q + 1)
                v.reciprocal(rstd[0:rows, 0:k], sd[0:rows, 0:k]).then_inc(sem(f"{name}_norm"), 1)
                dve.wait_ge(sem(f"{name}_norm"), 3 * q + 3)
                for n in range(k):
                    ins = v.tensor_scalar(to[0:rows, n * F:(n + 1) * F], row_of(n), meanvar[0:rows, n, 0:1],
                                          rstd[0:rows, n:n + 1], ALU.subtract, ALU.mult)
                ins.then_inc(sem(done), 1)

            with dve.Fori(0, NC) as q:
                pass1(q, 512, False)
            pass1(NC, LASTW, True)
            dve.wait_ge(sem("p1_x1"), NC + 1)
            dve.wait_ge(sem("p1_hi"), NC + 1)
            dve.wait_ge(sem("p1_low"), NC + 1)
            dve.wait_ge(sem("p1_yT"), NC + 1)
            v.memset(stats[:, 0, 0:1], 0.0).then_inc(sem("p1_done"), 1)
            calls(2)

            def mean_neighbours(q, w):
                nT, dg = slot[0][:, 0:w], slot[7][:, 0:w]
                dve.wait_ge(sem("p2_deg_sum"), q + 1)
                v.tensor_scalar(dg, PS[:, 5, 0:w], 1.0, None, ALU.max).then_inc(sem("p2_deg"), 1)
                dve.wait_ge(sem("p2_deg"), 2 * q + 1)
                v.reciprocal(dg, dg).then_inc(sem("p2_deg"), 1)
                dve.wait_ge(sem("p2_deg"), 2 * q + 2)
                dve.wait_ge(sem("p2_agg"), q + 1)
                dve.wait_ge(sem("p2_low"), q)
                v.tensor_tensor(nT, PS[:, 0, 0:w], dg, ALU.mult).then_inc(sem("p2_n"), 1)

            def residual(q, last):
                rows, k = (LASTW, 1) if last else (P, 4)
                dve.wait_ge(sem("p2_y_sum"), q + 1)
                dve.wait_ge(sem("p2_res_out"), 16 * q)
                v.tensor_tensor(slot[5][0:rows, 0:k * F].rearrange("p (t f) -> p t f", f=F),
                                PS[0:rows, 4, 0:k * F].rearrange("p (t f) -> p t f", f=F),
                                b2_b[0:rows, :].unsqueeze(1).to_broadcast([rows, k, F]), ALU.add).then_inc(sem("p2_res"), 1)

            mean_neighbours(0, 512)
            with dve.Fori(1, NC) as q:
                residual(q - 1, False)
                mean_neighbours(q, 512)
            residual(NC - 1, False)
            mean_neighbours(NC, LASTW)
            residual(NC, True)
            dve.wait_ge(sem("p2_low"), NC + 1)
            dve.wait_ge(sem("p2_res"), NC + 1)
            dve.wait_ge(sem("p2_y_out"), 16 * (NC + 1))
            dve.wait_ge(sem("p2_res_out"), 16 * (NC + 1))
            v.memset(stats[:, 0, 0:1], 0.0).then_inc(sem("p2_done"), 1)
            calls(3)

            def pass3(q, par, last):
                rows, k = (LAST, 1) if last else (P, 4)
                total = slot[4 + par][0:rows, 0:k * F]
                dve.wait_ge(sem("p3_agg"), q + 1)
                dve.wait_ge(sem("p3_out"), q)
                v.tensor_reduce(total.rearrange("p (t f) -> p t f", f=F),
                                PS[0:rows, 4 * par:4 * par + k, 0:PARTS * F].rearrange("p t (s f) -> p t f s", s=PARTS),
                                AX.X, ALU.add).then_inc(sem("p3_sum"), 1)
                dve.wait_ge(sem("p3_sum"), 3 * q + 1)
                dve.wait_ge(sem(f"p3_in{par}"), (q - par) * 16 + 32)
                for n in range(k):
                    cols = slice(n * F, (n + 1) * F)
                    ins = v.scalar_tensor_tensor(out=total[:, cols], in0=total[:, cols], scalar=ideg[0:rows, ds(4 * q + n, 1)],
                                                 in1=slot[par][0:rows, cols], op0=ALU.mult, op1=ALU.add)
                ins.then_inc(sem("p3_sum"), 1)
                dve.wait_ge(sem("p3_sum"), 3 * q + 2)
                v.tensor_tensor(total, total, slot[2 + par][0:rows, 0:k * F], ALU.add).then_inc(sem("p3_sum"), 1)
                dve.wait_ge(sem("p3_sum"), 3 * q + 3)
                dve.wait_ge(sem(f"p3_stored{par}"), (q - par) * 8)
                norm("p3", q, rows, k, lambda n: total[:, n * F:(n + 1) * F], slot[6 + par], "p3_out")

            with dve.Fori(0, NC, 2) as q:
                q = by_twos(q, 0, NC)
                pass3(q, 0, False)
                pass3(q + 1, 1, False)
            pass3(NC, 0, True)

        @block.tensor
        def _(pe):
            mm = nc.tensor.matmul

            pe.wait_ge(sem("consts"), 1)
            pe.wait_ge(sem("tile_columns"), 1)
            mm(PS[0:1, 6, 0:TILES], tcol[:, 2:3], ident[0:TILES, 0:TILES], start=True, stop=True)
            mm(PS[0:1, 6, 32:32 + TILES], tcol[:, 5:6], ident[0:TILES, 0:TILES], start=True, stop=True)
            mm(PS[0:1, 6, 64:64 + TILES], tcol[:, 5:6], before[:, :], start=True, stop=True).then_inc(sem("table_rows"), 1)
            mm(PS[:, 7, 0:16], zero[:, :], zero[:, 0:16], start=True, stop=True).then_inc(sem("items_done"), DRING)

            zeros = zero[:, 0:1].to_broadcast([P, 512])
            zeros_b = zero[:, 0:1].to_broadcast([P, P + NTYPE])

            def count_tile(t, par):
                lo, nb, st = load_tile_entry(pe, t)
                if not isinstance(t, int) or t >= 2:
                    pe.wait_ge(sem("packed_out"), t - 1)
                mm(PS[:, 2 * par, :], zero[:, :], zeros, start=True, stop=False)
                mm(PS[:, 2 * par + 1, 0:P + NTYPE], zero[:, :], zeros_b, start=True, stop=False)
                with pe.Fori(0, nb) as i:
                    c0 = first_chunk(lo, i)
                    for u in range(U):
                        if u % 2:
                            rows = D_odd[:, ds(((st + i) % (DRING // U)) * (U // 2) + u // 2, 1), :].rearrange("p a m -> p (a m)")
                        else:
                            rows = D_even[:, u // 2, :]
                        pe.wait_ge(sem("D_act" if u % 2 else "D_pool"), (st + i) * 2 + u // 2 + 1)
                        pe.wait_ge(sem("S_set"), (st + i) * U + u + 1)
                        mm(PS[:, 2 * par, :], rows, S[:, u, 0:512], start=False, stop=False)
                        mm(PS[:, 2 * par + 1, 0:P], rows, S[:, u, 512:SPAN], start=False, stop=False)
                        mm(PS[:, 2 * par + 1, P:P + NTYPE], rows, T[:, ds(c0 + u, 1), :], start=False, stop=False).then_inc(sem("items_done"), 1)
                mm(PS[:, 2 * par, :], zero[:, :], zeros, start=False, stop=True)
                mm(PS[:, 2 * par + 1, 0:P + NTYPE], zero[:, :], zeros_b, start=False, stop=True).then_inc(sem("tiles_summed"), 1)

            def turn_tile(t):
                pe.wait_ge(sem("packed_out"), t + 1)
                if not isinstance(t, int) or t > 0:
                    pe.wait_ge(sem("packedT_in"), t)
                for g in range(GROUPS):
                    ins = nc.tensor.transpose(PS[:, 4 + g // 4, (g % 4) * P:(g % 4 + 1) * P], packed[:, g * P:(g + 1) * P], ident[:, :])
                ins.then_inc(sem("turned"), 1)

            pe.wait_ge(sem("table_set"), 1)
            count_tile(0, 0)
            with pe.Fori(1, TILES, 2) as t:
                t = by_twos(t, 1, TILES)
                count_tile(t, 1)
                turn_tile(t - 1)
                count_tile(t + 1, 0)
                turn_tile(t)
            turn_tile(TILES - 1)

            pe.wait_ge(sem("verdict_set"), 1)
            mm(PS[0:1, 7, 0:2], ones[:, 0:1], verdict[:, 0:2], start=True, stop=True).then_inc(sem("verdict_sum"), 1)
            general = is_general_after_flag(pe)

            def general_sum(n, width):
                with pe.If(general):
                    per = 4 * F // width * width if n else 512
                    banks = 1 if n == 0 else 7
                    pe.wait_ge(sem("g_start"), n + 1)
                    for b in range(banks):
                        mm(PS[:, b, :], zero[:, :], zeros, start=True, stop=False)
                    with pe.Fori(0, CHUNKS) as c:
                        pe.wait_ge(sem("g_onehot_set"), c + n * CHUNKS + 1)
                        if n == 0:
                            pe.wait_ge(sem("g_types_set"), c + 1)
                        else:
                            pe.wait_ge(sem("g_rows_in"), (c + (n - 1) * CHUNKS) * 16 + 16)
                        for t in range(TILES):
                            where = PS[:, 0, t * NTYPE:(t + 1) * NTYPE] if n == 0 else PS[:, t // 4, (t % 4) * F:(t % 4 + 1) * F]
                            ins = mm(where, g_onehot[:, t * P:(t + 1) * P], g_rows[:, 0:width], start=False, stop=False)
                        ins.then_inc(sem("g_used"), 1)
                    for b in range(banks):
                        ins = mm(PS[:, b, :], zero[:, :], zeros, start=False, stop=True)
                    ins.then_inc(sem("g_summed"), 1)
                    pe.wait_ge(sem("g_copied"), n + 1)
                with pe.Else():
                    pe.nop()

            general_sum(0, NTYPE)
            general_sum(1, F)

            def agg_third(name, parts, q, w, third):
                with pe.If(general):
                    if third == 2:
                        pe.wait_ge(sem(f"{name}_sum_staged"), q + 1)
                        for n in range(-(-w // P)):
                            rows = min(P, w - n * P)
                            ins = nc.tensor.transpose(PS[:, 0, n * P:n * P + rows],
                                                      g_stage[0:rows, n, :], ident[0:rows, 0:rows])
                        ins.then_inc(sem(f"{name}_agg"), 1)
                    else:
                        pe.nop()
                with pe.Else():
                    for j in range(TILES)[third * 9:third * 9 + 9]:
                        for s in range(PARTS):
                            ins = mm(PS[:, 0, 0:w], parts[:, j, s, :], AT[:, j, ds(q * 512, w)],
                                     start=(j == 0 and s == 0), stop=(j == TILES - 1 and s == PARTS - 1))
                    if third == 2:
                        ins.then_inc(sem(f"{name}_agg"), 1)
                pe.nop()

            def turn_types(name, q, w):
                pe.wait_ge(sem(f"{name}_types_staged"), q + 1)
                for n in range(-(-w // P)):
                    rows = min(P, w - n * P)
                    ins = nc.tensor.transpose(PS[0:NTYPE, 2, n * P:n * P + rows], c_stage[0:rows, n, :], ident[0:rows, 0:rows])
                ins.then_inc(sem(f"{name}_typeT"), 1)

            def messages(q, w):
                pe.wait_ge(sem("p1_s"), q + 1)
                pe.wait_ge(sem("p1_c"), q + 1)
                pe.wait_ge(sem("p1_x1"), q)
                mm(PS[:, 3, 0:w], wmsg_s[:, :], slot[0][:, 0:w], start=True, stop=False)
                mm(PS[:, 3, 0:w], emb_b[:, :], slot[7][0:NTYPE, 0:w], start=False, stop=True).then_inc(sem("p1_m_sum"), 1)

            def gates(q, w):
                pe.wait_ge(sem("p1_m"), q + 1)
                pe.wait_ge(sem("p1_xT_in"), 16 * (q + 1))
                m, x_ = slot[1][:, 0:w], slot[2][:, 0:w]
                for g in range(2):
                    mm(PS[:, 4 + g, 0:w], wih_s[:, g, :], m, start=True, stop=False)
                    mm(PS[:, 4 + g, 0:w], whh_s[:, g, :], x_, start=False, stop=True).then_inc(sem("p1_gate"), 1)
                mm(PS[:, 7, 0:w], whh_s[:, 2, :], x_, start=True, stop=True)
                mm(PS[:, 6, 0:w], wih_s[:, 2, :], m, start=True, stop=True).then_inc(sem("p1_gates"), 1)

            def rows_back(q, w):
                pe.wait_ge(sem("p1_y"), q + 1)
                for n in range(-(-w // P)):
                    rows = min(P, w - n * P)
                    ins = nc.tensor.transpose(PS[0:rows, 3, n * P:(n + 1) * P], slot[7][:, n * P:n * P + rows], ident[:, :])
                ins.then_inc(sem("p1_yT"), 1)

            def agg(name, parts, q, w, between):
                if not isinstance(q, int) or q > 0:
                    pe.wait_ge(sem("p1_s" if name == "p1" else "p2_n"), q)
                for third in range(3):
                    agg_third(name, parts, q, w, third)
                    between[third]()

            nothing = [lambda: None] * 3
            pe.wait_ge(sem("x_split"), 1)
            pe.wait_ge(sem("digits_stored"), (TILES + 1) * DIGITS)
            pe.wait_ge(sem("types_ready"), 1)
            turn_types("p1", 0, 512)
            agg("p1", xp, 0, 512, nothing)

            def p1_step(q, w, wprev):
                agg("p1", xp, q, w, [lambda: messages(q - 1, wprev), lambda: gates(q - 1, wprev),
                                     lambda: rows_back(q - 1, wprev)])
                pe.wait_ge(sem("p1_c"), q)
                turn_types("p1", q, w)

            with pe.Fori(1, NC) as q:
                p1_step(q, 512, 512)
            p1_step(NC, LASTW, 512)
            messages(NC, LASTW)
            gates(NC, LASTW)
            rows_back(NC, LASTW)

            pe.wait_ge(sem("p1_done"), 1)
            general_sum(2, F)

            def chunk_inputs(q, w):
                pe.wait_ge(sem("p2_c"), q)
                pe.wait_ge(sem("p2_x1c"), q)
                turn_types("p2", q, w)
                pe.wait_ge(sem("p2_x1_in"), 16 * (q + 1))
                for n in range(-(-w // P)):
                    rows = min(P, w - n * P)
                    ins = nc.tensor.transpose(PS[:, 1, n * P:n * P + rows], slot[2][0:rows, n * F:(n + 1) * F], ident[0:rows, 0:rows])
                ins.then_inc(sem("p2_x1T"), 1)

            def degrees(q, w):
                pe.wait_ge(sem("p2_c"), q + 1)
                mm(PS[:, 5, 0:w], ones[0:NTYPE, :], slot[7][0:NTYPE, 0:w], start=True, stop=True).then_inc(sem("p2_deg_sum"), 1)

            def hidden(q, w):
                pe.wait_ge(sem("p2_n"), q + 1)
                pe.wait_ge(sem("p2_x1c"), q + 1)
                pe.wait_ge(sem("p2_h"), 2 * q)
                for a in range(2):
                    mm(PS[:, 6 + a, 0:w], ws1[:, a, :], slot[3][:, 0:w], start=True, stop=False)
                    mm(PS[:, 6 + a, 0:w], wn1[:, a, :], slot[0][:, 0:w], start=False, stop=True).then_inc(sem("p2_h_sum"), 1)

            def second(q, w):
                pe.wait_ge(sem("p2_h"), 2 * (q + 1))
                pe.wait_ge(sem("p2_yf"), q)
                pe.wait_ge(sem("p2_res"), q)
                hid = [slot[1], slot[6]]
                for n in range(-(-w // P)):
                    rows = min(P, w - n * P)
                    for bank, wt in ((3, wn2), (4, ws2)):
                        for a in range(2):
                            ins = mm(PS[0:rows, bank, n * F:(n + 1) * F], hid[a][:, n * P:n * P + rows], wt[:, a, :],
                                     start=(a == 0), stop=(a == 1))
                ins.then_inc(sem("p2_y_sum"), 1)

            pe.wait_ge(sem("p1_low"), NC + 1)
            chunk_inputs(0, 512)
            agg("p2", x1p, 0, 512, [lambda: None, lambda: degrees(0, 512), lambda: None])

            def p2_step(q, w):
                def one():
                    hidden(q - 1, 512)
                    chunk_inputs(q, w)

                def two():
                    second(q - 1, 512)
                    degrees(q, w)

                agg("p2", x1p, q, w, [one, two, lambda: None])

            with pe.Fori(1, NC) as q:
                p2_step(q, 512)
            p2_step(NC, LASTW)
            hidden(NC, LASTW)
            second(NC, LASTW)

            pe.wait_ge(sem("p2_done"), 1)
            general_sum(3, F)

            def agg_rows(q, par, last):
                if not isinstance(q, int) or q >= 2:
                    pe.wait_ge(sem("p3_out"), q - 1)
                tiles = [(0, LAST)] if last else [(n, P) for n in range(4)]
                with pe.If(general):
                    for n, rows in tiles:
                        mm(PS[0:rows, 4 * par + n, 0:F], ident[:, 0:rows], g_sum[:, ds(4 * q + n, 1), :].rearrange("p a f -> p (a f)"), start=True, stop=True)
                        ins = mm(PS[0:rows, 4 * par + n, F:PARTS * F], zero[:, 0:rows], zero[:, 0:1].to_broadcast([P, (PARTS - 1) * F]), start=True, stop=True)
                    ins.then_inc(sem("p3_agg"), 1)
                with pe.Else():
                    for n, rows in tiles:
                        for j in range(TILES):
                            ins = mm(PS[0:rows, 4 * par + n, 0:PARTS * F], AT[:, j, ds(q * 512 + n * P, rows)],
                                     xp[:, j, :, :].rearrange("p s f -> p (s f)"), start=(j == 0), stop=(j == TILES - 1))
                    ins.then_inc(sem("p3_agg"), 1)
                pe.nop()

            agg_rows(0, 0, False)
            agg_rows(1, 1, False)
            with pe.Fori(2, NC, 2) as q:
                q = by_twos(q, 2, NC)
                agg_rows(q, 0, False)
                agg_rows(q + 1, 1, False)
            agg_rows(NC, 0, True)

        @block.scalar
        def _(act):
            a = nc.scalar

            def dest_rows(t):
                lo, nb, st = load_tile_entry(act, t)
                act.wait_ge(sem("D_act"), st * 2)
                a.activation(iota_t[:, :], iota_h[:, 0:P], ACT.Identity, bias=tile_off[:, ds(t, 1)]).then_inc(sem("iota_t_set"), 1)
                act.wait_ge(sem("iota_t_set"), t + 1)
                with act.Fori(0, nb) as i:
                    c0 = first_chunk(lo, i)
                    act.wait_ge(sem("D_act"), (st + i) * 2)
                    for n, u in enumerate((1, 3)):
                        a.activation(dist[:, n, :], iota_t[:, :], ACT.Abs, bias=dst_f[:, ds(c0 + u, 1)], scale=-1.0).then_inc(sem("dist_set"), 1)
                    for n, u in enumerate((1, 3)):
                        act.wait_ge(sem("items_done"), (st + i) * U + u + 1)
                        act.wait_ge(sem("dist_set"), (st + i) * 2 + n + 1)
                        a.activation(D_odd[:, ds(((st + i) % (DRING // U)) * (U // 2) + u // 2, 1), :].rearrange("p a m -> p (a m)"),
                                     dist[:, n, :], ACT.Relu, bias=1.0, scale=-1.0).then_inc(sem("D_act"), 1)

            def packed_out(t, par):
                act.wait_ge(sem("tiles_summed"), t + 1)
                act.wait_ge(sem("turned"), t)
                a.activation(packed[:, 0:512], PS[:, 2 * par, :], ACT.Copy)
                a.activation(packed[:, 512:SPAN], PS[:, 2 * par + 1, 0:P], ACT.Copy)
                a.activation(Cn[:, ds(t, 1), :].rearrange("p a k -> p (a k)"), PS[:, 2 * par + 1, P:P + NTYPE], ACT.Copy).then_inc(sem("packed_out"), 1)

            def packedT_in(t, par):
                act.wait_ge(sem("turned"), t + 1)
                if not isinstance(t, int) or t >= 2:
                    act.wait_ge(sem("digits_taken"), (t - 1) * DIGITS)
                a.activation(packedT[:, par, 0:512], PS[:, 4, :], ACT.Copy)
                a.activation(packedT[:, par, 512:SPAN], PS[:, 5, 0:P], ACT.Copy).then_inc(sem("packedT_in"), 1)

            def store_digits(t, w):
                for f in range(DIGITS):
                    act.wait_ge(sem("digits_taken"), t * DIGITS + f + 1)
                    a.activation(AT[:, GROUPS * f:GROUPS * f + GROUPS, ds(t * P, w)],
                                 digits[:, f, :].rearrange("p (g m) -> p g m", g=GROUPS)[:, :, 0:w], ACT.Copy,
                                 accum_out=count[:, ds(t, 1), f:f + 1].rearrange("p a b -> p (a b)")).then_inc(sem("digits_stored"), 1)

            act.sem_inc(sem("digits_stored"), DIGITS)
            act.wait_ge(sem("table_set"), 1)
            for t in range(3):
                dest_rows(t)
                if t >= 1:
                    packed_out(t - 1, (t - 1) % 2)
                if t >= 2:
                    packedT_in(t - 2, t % 2)
            with act.Fori(3, TILES, 2) as t:
                t = by_twos(t, 3, TILES)
                for k in range(2):
                    dest_rows(t + k)
                    packed_out(t + k - 1, k)
                    packedT_in(t + k - 2, 1 - k)
                    store_digits(t + k - 3, P)
            packed_out(TILES - 1, (TILES - 1) % 2)
            packedT_in(TILES - 2, (TILES - 2) % 2)
            store_digits(TILES - 3, P)
            packedT_in(TILES - 1, (TILES - 1) % 2)
            store_digits(TILES - 2, P)
            store_digits(TILES - 1, LASTW)

            for c in range(NC + 1):
                rows, k = (P, 4) if c < NC else (LAST, 1)
                act.wait_ge(sem(f"x_in{c}"), 16)
                if c == NC:
                    act.wait_ge(sem("xp_zeroed"), 1)
                a.activation(xp[0:rows, 4 * c:4 * c + k, 0, :], xstage[0:rows, 4 * c:4 * c + k, :], ACT.Copy).then_inc(sem("x_hi"), 1)
                act.wait_ge(sem("x_rest"), c + 1)
                a.activation(xp[0:rows, 4 * c:4 * c + k, 1, :], xrest(c)[0:rows, 0:k * F].rearrange("p (t f) -> p t f", f=F), ACT.Copy).then_inc(sem("x_mid"), 1)

            general = is_general_after_flag(act)

            def general_out(n):
                with act.If(general):
                    act.wait_ge(sem("g_summed"), n + 1)
                    if n == 0:
                        ins = a.activation(Cn[:, 0:TILES, :].rearrange("p t k -> p (t k)"), PS[:, 0, 0:TILES * NTYPE], ACT.Copy)
                    else:
                        for b in range(-(-TILES // 4)):
                            k = min(4, TILES - 4 * b)
                            ins = a.activation(g_sum[:, 4 * b:4 * b + k, :], PS[:, b, 0:k * F].rearrange("p (t f) -> p t f", f=F), ACT.Copy)
                    ins.then_inc(sem("g_copied"), 1)
                    act.wait_ge(sem("g_copied"), n + 1)
                with act.Else():
                    act.nop()

            general_out(0)
            act.wait_ge(sem("packed_out"), TILES)
            a.activation(sd[:, 0:1], eps[:, :], ACT.Copy).then_inc(sem("types_ready"), 1)
            general_out(1)

            def sqrt_var(name, q, rows, k):
                act.wait_ge(sem(f"{name}_norm"), 3 * q + 2)
                a.activation(sd[0:rows, 0:k], meanvar[0:rows, 0:k, 1:2].rearrange("p t a -> p (t a)"), ACT.Sqrt, bias=eps[0:rows, :]).then_inc(sem(f"{name}_sd"), 1)

            def high_parts(name, target, full, rest, q, last):
                rows, k = (LASTW, 1) if last else (P, 4)
                if last:
                    act.wait_ge(sem("x1p_zeroed" if name == "p1" else "xp_zeroed"), 1)
                a.activation(target[0:rows, ds(4 * q, k), 0, :], full[0:rows, 0:k * F].rearrange("p (t f) -> p t f", f=F), ACT.Copy).then_inc(sem(f"{name}_hi"), 1)
                act.wait_ge(sem(f"{name}_rest"), q + 1)
                a.activation(target[0:rows, ds(4 * q, k), 1, :], rest[0:rows, 0:k * F].rearrange("p (t f) -> p t f", f=F), ACT.Copy).then_inc(sem(f"{name}_mid"), 1)

            def stage_types(name, q):
                a.activation(c_stage[:, :, :], Cn[:, ds(4 * q, 4), :], ACT.Copy).then_inc(sem(f"{name}_types_staged"), 1)

            def stage_sums(name, q):
                settle(act, "act_settled")
                with act.If(general):
                    a.activation(g_stage[:, :, :], g_sum[:, ds(4 * q, 4), :], ACT.Copy).then_inc(sem(f"{name}_sum_staged"), 1)
                with act.Else():
                    act.nop()

            def sums_out(q, w):
                act.wait_ge(sem("p1_agg"), q + 1)
                act.wait_ge(sem("p1_m_sum"), q)
                a.activation(slot[0][:, 0:w], PS[:, 0, 0:w], ACT.Copy).then_inc(sem("p1_s"), 1)
                act.wait_ge(sem("p1_typeT"), q + 1)
                if not isinstance(q, int) or q < NC:
                    stage_sums("p1", q + 1)
                    stage_types("p1", q + 1)
                a.activation(slot[7][0:NTYPE, 0:w], PS[0:NTYPE, 2, 0:w], ACT.Copy).then_inc(sem("p1_c"), 1)

            def gate_functions(q, w):
                act.wait_ge(sem("p1_gates"), q + 1)
                act.wait_ge(sem("p1_y"), q)
                a.activation(slot[3][:, 0:w], PS[:, 4, 0:w], ACT.Sigmoid, bias=rz_b[:, 0:1]).then_inc(sem("p1_r"), 1)
                a.activation(slot[4][:, 0:w], PS[:, 5, 0:w], ACT.Sigmoid, bias=rz_b[:, 1:2])
                act.wait_ge(sem("p1_t"), 2 * q + 2)
                act.wait_ge(sem("p1_low"), q)
                a.activation(slot[6][:, 0:w], slot[5][:, 0:w], ACT.Tanh, bias=gate_b[:, 2:3]).then_inc(sem("p1_n"), 1)

            def normed(q, last):
                sqrt_var("p1", q, LASTW if last else P, 1 if last else 4)
                act.wait_ge(sem("p1_x1"), q + 1)
                high_parts("p1", x1p, slot[5], slot[6], q, last)

            act.wait_ge(sem("x_split"), 1)
            stage_sums("p1", 0)
            stage_types("p1", 0)
            sums_out(0, 512)
            with act.Fori(1, NC) as q:
                gate_functions(q - 1, 512)
                sums_out(q, 512)
                normed(q - 1, False)
            gate_functions(NC - 1, 512)
            sums_out(NC, LASTW)
            normed(NC - 1, False)
            gate_functions(NC, LASTW)
            normed(NC, True)

            act.wait_ge(sem("p1_done"), 1)
            general_out(2)

            def inputs_out(q, w):
                act.wait_ge(sem("p2_typeT"), q + 1)
                if not isinstance(q, int) or q < NC:
                    stage_types("p2", q + 1)
                act.wait_ge(sem("p2_n"), q)
                a.activation(slot[7][0:NTYPE, 0:w], PS[0:NTYPE, 2, 0:w], ACT.Copy).then_inc(sem("p2_c"), 1)
                act.wait_ge(sem("p2_x1T"), q + 1)
                act.wait_ge(sem("p2_h_sum"), 2 * q)
                a.activation(slot[3][:, 0:w], PS[:, 1, 0:w], ACT.Copy).then_inc(sem("p2_x1c"), 1)

            def relu_rows(q, w):
                act.wait_ge(sem("p2_y_sum"), q)
                for n, sl in enumerate((slot[1], slot[6])):
                    act.wait_ge(sem("p2_h_sum"), 2 * q + n + 1)
                    a.activation(sl[:, 0:w], PS[:, 6 + n, 0:w], ACT.Relu, bias=b1_s[:, n:n + 1]).then_inc(sem("p2_h"), 1)

            def second_out(q, last):
                rows, k = (LASTW, 1) if last else (P, 4)
                act.wait_ge(sem("p2_y_sum"), q + 1)
                act.wait_ge(sem("p2_y_out"), 16 * q)
                act.wait_ge(sem("p2_low"), q)
                a.activation(slot[4][0:rows, 0:k * F], PS[0:rows, 3, 0:k * F], ACT.Copy).then_inc(sem("p2_yf"), 1)
                act.wait_ge(sem("p2_yf"), q + 1)
                high_parts("p2", xp, slot[4], slot[0], q, last)

            stage_types("p2", 0)
            stage_sums("p2", 0)
            inputs_out(0, 512)
            with act.Fori(1, NC) as q:
                relu_rows(q - 1, 512)
                stage_sums("p2", q)
                inputs_out(q, 512)
                second_out(q - 1, False)
            relu_rows(NC - 1, 512)
            stage_sums("p2", NC)
            inputs_out(NC, LASTW)
            second_out(NC - 1, False)
            relu_rows(NC, LASTW)
            second_out(NC, True)

            act.wait_ge(sem("p2_done"), 1)
            general_out(3)
            with act.Fori(0, NC) as q:
                sqrt_var("p3", q, P, 4)
            sqrt_var("p3", NC, LAST, 1)


def kernel(**inputs):
    import numpy as np
    import concourse.bacc as bacc
    from concourse.bass_utils import run_bass_kernel_spmd

    nc = bacc.Bacc("TRN2", target_bir_lowering=False, num_devices=1, dynamic_dma_scratch_size=SCRATCH)
    a = {k: np.asarray(v) for k, v in inputs.items()}
    arrays = {
        "x": a["x"], "xT": a["x"].T,
        "dst_c": a["dst"][:FULL * P].reshape(FULL, P).T, "dst_t": a["dst"][FULL * P:].reshape(TAIL, 1),
        "src_c": a["src"][:FULL * P].reshape(FULL, P).T, "src_t": a["src"][FULL * P:].reshape(TAIL, 1),
        "typ_c": a["edge_type_9"][:FULL * P].reshape(FULL, P).T, "typ_t": a["edge_type_9"][FULL * P:].reshape(TAIL, 1),
        "wmsgT": a["L0_gnn_W_msg"].T, "bmsg": a["L0_gnn_b_msg"].reshape(1, F), "embed": a["L0_gnn_edge_embed"],
        "wihT": a["L0_gnn_W_ih"].T, "whhT": a["L0_gnn_W_hh"].T,
        "bgate": np.concatenate([a["L0_gnn_b_ih"].reshape(3, F), a["L0_gnn_b_hh"].reshape(3, F)]).T,
        "wself1": a["L1_gnn_w_self1"], "wneigh1": a["L1_gnn_w_neigh1"], "b1": a["L1_gnn_b1"].reshape(2, F).T,
        "wself2": a["L1_gnn_w_self2"], "wneigh2": a["L1_gnn_w_neigh2"], "b2": a["L1_gnn_b2"].reshape(1, F),
    }
    arrays = {k: np.ascontiguousarray(v) for k, v in arrays.items()}
    args = [nc.dram_tensor(k, v.shape, mybir.dt.from_np(v.dtype), kind="ExternalInput").ap() for k, v in arrays.items()]
    fp32 = mybir.dt.float32
    scratch = [nc.dram_tensor(k, (DW, F), fp32, kind="Internal").ap() for k in ("x1_rows", "y_rows", "res_rows")]
    out = nc.dram_tensor("out_rows", (N, F), fp32, kind="ExternalOutput").ap()
    graph_kernel(nc, *args, *scratch, out)
    return run_bass_kernel_spmd(nc, [arrays], core_ids=[0]).results[0]["out_rows"]
```

```python
import concourse.bass as bass
from concourse import mybir
from contextlib import ExitStack

N, E, F, H2, NTYPE = 3125, 100000, 128, 256, 9
P = 128
TILES = -(-N // P)
LAST = N - (TILES - 1) * P
LASTW = 64
DW = (TILES - 1) * P + LASTW
CHUNKS = -(-E // P)
FULL = E // P
TAIL = E - FULL * P
U = 6
V = U // 2
SHARES = ((0, 1), (2, 3), (4,))
LEAST = len(SHARES)
LAG = 3
DIVIDE = -(-(1 << 16) // U)
assert all(n * DIVIDE >> 16 == n // U for n in range(CHUNKS + U)) and (CHUNKS + U) * DIVIDE < 1 << 24
CP = CHUNKS + LEAST * U
DIGITS, GROUPS = 5, 5
SPAN = GROUPS * P
PAD_DST = 4000
CENTER = N // 2
NC = TILES // 4
PARTS = 3
SCRATCH = 2048


def graph_kernel(nc, x, xT, dst_c, dst_t, src_c, src_t, typ_c, typ_t, wmsgT, bmsg, embed, wihT, whhT,
                 bgate, wself1, wneigh1, b1, wself2, wneigh2, b2, x1_dram, y_dram, res_dram, out):
    fp32, bf16, fp16 = mybir.dt.float32, mybir.dt.bfloat16, mybir.dt.float16
    i32, u32 = mybir.dt.int32, mybir.dt.uint32
    ALU, ACT, AX = mybir.AluOpType, mybir.ActivationFunctionType, mybir.AxisListType
    SIZE = {fp32: 4, i32: 4, u32: 4, bf16: 2, fp16: 2}
    ds = bass.ds
    ctx = ExitStack()

    top = [nc.sbuf_base + (-nc.sbuf_base) % 32]

    def nbytes(shape, dt):
        n = SIZE[dt]
        for s in shape[1:]:
            n *= s
        return n + (-n) % 32

    def place(region, name, shape, dt):
        t = nc.alloc_sbuf_tensor_at(name, shape, dt, offset=region[0])
        region[0] += nbytes(shape, dt)
        return t

    def region(size):
        at = top[0]
        top[0] += size + (-size) % 32
        return at

    def sb(name, shape, dt):
        return place(top, name, shape, dt)

    part_bytes = TILES * PARTS * F * 2
    AT_at = region(TILES * DW * 2)
    AT = place([AT_at], "AT", [P, TILES, DW], bf16)
    A_at, B_at, W_at = region(part_bytes), region(part_bytes), region(CP * NTYPE * 2 + SPAN * 4 + 64)

    r = [A_at]
    digits = place(r, "digits", [P, DIGITS, SPAN], i32)
    packedT = place(r, "packedT", [P, SPAN], i32)
    D = place(r, "D", [P, U, P], bf16)
    bmsg_b, emb_s = (place(r, n, [NTYPE, F], fp32) for n in ("bmsg_b", "emb_s"))
    assert r[0] <= A_at + part_bytes
    r = [A_at]
    raw_dst, raw_src, raw_typ = (place(r, n, [P, CP], i32) for n in ("raw_dst", "raw_src", "raw_typ"))
    first_i = place(r, "first_i", [TILES, CHUNKS], i32)
    last_i = place(r, "last_i", [TILES, CHUNKS], i32)
    r = [AT_at]
    edge_f = place(r, "edge_f", [P, CP], fp32)
    weight_a = place(r, "weight_a", [P, CP], fp32)
    weight_b = place(r, "weight_b", [P, CP], fp32)
    digit_a = place(r, "digit_a", [P, CP], fp32)
    digit_b = place(r, "digit_b", [P, CP], fp32)
    first_f = place(r, "first_f", [TILES, CHUNKS], fp32)
    last_f = place(r, "last_f", [TILES, CHUNKS], fp32)
    passed = place(r, "passed", [TILES, CHUNKS], bf16)
    r = [B_at]
    dst_f = place(r, "dst_f", [P, CP], fp16)
    src_col = place(r, "src_col", [P, CP], fp32)
    src_w = place(r, "src_w", [P, CP], fp32)
    S = place(r, "S", [P, U, SPAN], bf16)
    diff = place(r, "diff", [P, U, P], fp16)
    dist = place(r, "dist", [P, U, P], bf16)
    T_now = place(r, "T_now", [P, U, NTYPE], bf16)
    assert r[0] <= B_at + part_bytes
    r = [W_at]
    T = place(r, "T", [P, CP, NTYPE], bf16)
    packed = place(r, "packed", [P, SPAN], fp32)
    x1p = place([A_at], "x1p", [P, TILES, PARTS, F], bf16)
    xp = place([B_at], "xp", [P, TILES, PARTS, F], bf16)
    xstage = place([W_at], "xstage", [P, TILES, F], fp32)
    slot = [place([W_at + 2048 * k], f"slot{k}", [P, 512], fp32) for k in range(8)]
    assert W_at + 8 * 2048 <= top[0]

    iota_h = sb("iota_h", [P, SPAN], fp16)
    tile_off = sb("tile_off", [P, TILES], fp32)
    off_now = sb("off_now", [P, 1], fp32)
    zero = sb("zero", [P, P], bf16)
    Cn = sb("Cn", [P, 4 * (NC + 1), NTYPE], fp32)
    c_stage = sb("c_stage", [P, 4, NTYPE], fp32)
    count = sb("count", [P, TILES, DIGITS], fp32)
    ident = sb("ident", [P, P], fp32)
    ones = sb("ones", [P, P], fp32)
    before = sb("before", [TILES, TILES], fp32)
    thr = sb("thr", [TILES, 2], fp32)
    tcol = sb("tcol", [TILES, 8], fp32)
    tcol_i = sb("tcol_i", [TILES, 2], i32)
    table = sb("table", [1, 3 * 32], i32)
    verdict = sb("verdict", [P, 1], fp32)
    flag = sb("flag", [1, 4], fp32)
    flag_i = sb("flag_i", [1, 4], i32)
    ideg = sb("ideg", [P, TILES], fp32)
    wmsg_s = sb("wmsg_s", [F, F], fp32)
    wih_s = sb("wih_s", [F, 3, F], fp32)
    whh_s = sb("whh_s", [F, 3, F], fp32)
    ws1 = sb("ws1", [F, 2, F], fp32)
    wn1 = sb("wn1", [F, 2, F], fp32)
    ws2 = sb("ws2", [F, 2, F], fp32)
    wn2 = sb("wn2", [F, 2, F], fp32)
    emb_b = sb("emb_b", [NTYPE, F], fp32)
    gate_b = sb("gate_b", [F, 6], fp32)
    rz_b = sb("rz_b", [F, 2], fp32)
    b1_s = sb("b1_s", [F, 2], fp32)
    b2_b = sb("b2_b", [P, F], fp32)
    stats = sb("stats", [P, 4, 6], fp32)
    meanvar = sb("meanvar", [P, 4, 2], fp32)
    sd = sb("sd", [P, 4], fp32)
    rstd = sb("rstd", [P, 4], fp32)
    eps = sb("eps", [P, 1], fp32)
    assert top[0] <= nc.sbuf_usable_end, (top[0], nc.sbuf_usable_end)

    r = [AT_at]
    g_iota = place(r, "g_iota", [P, TILES * P], fp32)
    g_onehot = place(r, "g_onehot", [P, TILES * P], fp32)
    g_src = place(r, "g_src", [P, CP], i32)
    g_dst_i = place(r, "g_dst_i", [P, CP], i32)
    g_typ_i = place(r, "g_typ_i", [P, CP], i32)
    g_dst = place(r, "g_dst", [P, CP], fp32)
    g_typ = place(r, "g_typ", [P, CP], fp32)
    g_idx = place(r, "g_idx", [P, 1], i32)
    g_rows = place(r, "g_rows", [P, F], fp32)
    g_sum = place(r, "g_sum", [P, 4 * (NC + 1), F], fp32)
    g_stage = place(r, "g_stage", [P, 4, F], fp32)
    assert r[0] <= A_at

    with ctx:
        PS = ctx.enter_context(nc.psum_tensor("PS", [P, 8, 512], fp32))
        sems = {}

        def sem(name):
            if name not in sems:
                sems[name] = ctx.enter_context(nc.semaphore(name))
            return sems[name]

        weights = [(wmsg_s[:, :], wmsgT), (wih_s[:, :, :], wihT.rearrange("k (g m) -> k g m", g=3)),
                   (whh_s[:, :, :], whhT.rearrange("k (g m) -> k g m", g=3)),
                   (ws1[:, :, :], wself1.rearrange("k (g m) -> k g m", g=2)),
                   (wn1[:, :, :], wneigh1.rearrange("k (g m) -> k g m", g=2)),
                   (ws2[:, :, :], wself2.rearrange("(g k) m -> k g m", g=2)),
                   (wn2[:, :, :], wneigh2.rearrange("(g k) m -> k g m", g=2)),
                   (emb_s[:, :], embed), (bmsg_b[:, :], bmsg.partition_broadcast(NTYPE)),
                   (gate_b[:, :], bgate), (b1_s[:, :], b1), (b2_b[:, :], b2.partition_broadcast(P))]

        def first_of_tile(eng, t):
            return eng.value_load(table[0:1, ds(t, 1)], min_val=0, max_val=CHUNKS - 1)

        def batches_of_tile(eng, t):
            nb = eng.value_load(table[0:1, ds(t + 32, 1)], min_val=LEAST, max_val=-(-CHUNKS // U))
            st = eng.value_load(table[0:1, ds(t + 64, 1)], min_val=0, max_val=TILES * -(-CHUNKS // U))
            return nb, st

        def settle(eng, name):
            eng.sem_inc(sem(name), 1)

        def by_twos(q, start, end):
            return q.with_bounds(min_val=start, max_val=end - 2 + (end - start) % 2)

        def first_chunk(lo, i):
            return (lo + i * U).with_bounds(min_val=0, max_val=CP - U)

        def is_general(eng):
            return eng.value_load(flag_i[0:1, 0:1], min_val=0, max_val=1)

        def xrest(c):
            return digits[:, c % 2, 0:512].bitcast(fp32)

        def general_rows(dve, v, general):
            def call(n):
                with dve.If(general):
                    if n == 0:
                        dve.wait_ge(sem("g_edges_in"), 96)
                        v.tensor_copy(g_dst[:, :], g_dst_i[:, :])
                        v.tensor_scalar(g_typ[:, :], g_typ_i[:, :], 0.0, float(NTYPE - 1), ALU.max, ALU.min).then_inc(sem("g_start"), 1)
                    else:
                        dve.wait_ge(sem("g_copied"), n)
                        v.memset(flag[:, 2:3], 0.0).then_inc(sem("g_start"), 1)
                    dve.wait_ge(sem("g_start"), n + 1)
                    with dve.Fori(0, CHUNKS) as c:
                        dve.wait_ge(sem("g_used"), c + n * CHUNKS)
                        v.tensor_scalar(g_onehot[:, :], g_iota[:, :], g_dst[:, ds(c, 1)], None, ALU.is_equal).then_inc(sem("g_onehot_set"), 1)
                        if n == 0:
                            v.tensor_scalar(g_rows[:, 0:NTYPE], g_iota[:, 0:NTYPE], g_typ[:, ds(c, 1)], None, ALU.is_equal).then_inc(sem("g_types_set"), 1)
                        else:
                            v.tensor_copy(g_idx[:, :], g_src[:, ds(c, 1)]).then_inc(sem("g_idx_set"), 1)
                with dve.Else():
                    dve.nop()
            return call

        block = ctx.enter_context(nc.Block())

        def is_general_after_flag(eng):
            eng.wait_ge(sem("flag_set"), 1)
            return is_general(eng)

        @block.sync
        def _(sp):
            sp.wait_ge(sem("pads_set"), 1)
            for name, ti, m, t in (("dst_in", raw_dst, dst_c, dst_t), ("src_in", raw_src, src_c, src_t),
                                   ("typ_in", raw_typ, typ_c, typ_t)):
                sp.dma_start(ti[:, 0:FULL], m).then_inc(sem(name), 16)
                sp.dma_start(ti[0:TAIL, FULL:FULL + 1], t).then_inc(sem(name), 16)
            sp.dma_start(first_i[:, 0:FULL], dst_c[0:1, :].partition_broadcast(TILES)).then_inc(sem("ends_in"), 16)
            sp.dma_start(first_i[:, FULL:CHUNKS], dst_t[0:1, :].partition_broadcast(TILES)).then_inc(sem("ends_in"), 16)
            sp.dma_start(last_i[:, 0:FULL], dst_c[P - 1:P, :].partition_broadcast(TILES)).then_inc(sem("ends_in"), 16)
            for to, of in weights:
                sp.dma_start(to, of).then_inc(sem("weights_in"), 16)
            sp.wait_ge(sem("tiles_summed"), TILES)
            for c in range(NC):
                sp.dma_start(xstage[:, 4 * c:4 * c + 4, :],
                             x[512 * c:512 * c + 512, :].rearrange("(t p) f -> p t f", p=P)).then_inc(sem(f"x_in{c}"), 16)
            sp.dma_start(xstage[0:LAST, TILES - 1, :], x[(TILES - 1) * P:N, :]).then_inc(sem(f"x_in{NC}"), 16)

            general = is_general_after_flag(sp)
            with sp.If(general):
                sp.wait_ge(sem("g_pads_set"), 1)
                for ti, m, t in ((g_dst_i, dst_c, dst_t), (g_src, src_c, src_t), (g_typ_i, typ_c, typ_t)):
                    sp.dma_start(ti[:, 0:FULL], m).then_inc(sem("g_edges_in"), 16)
                    sp.dma_start(ti[0:TAIL, FULL:FULL + 1], t).then_inc(sem("g_edges_in"), 16)
            with sp.Else():
                sp.nop()

            def pass1(q, w, cols, rows):
                if not isinstance(q, int) or q > 0:
                    sp.wait_ge(sem("p1_y"), q)
                sp.dma_start(slot[2][:, 0:cols], xT[:, ds(q * 512, cols)]).then_inc(sem("p1_xT_in"), 16)
                sp.wait_ge(sem("p1_x1"), q + 1)
                if rows == P:
                    sp.dma_start(x1_dram[ds(q * 512, 512), :].rearrange("(t p) f -> p t f", p=P),
                                 slot[5][:, :].rearrange("p (t f) -> p t f", f=F)).then_inc(sem("p1_x1_out"), 16)
                else:
                    sp.dma_start(x1_dram[ds(q * 512, LASTW), :], slot[5][0:LASTW, 0:F]).then_inc(sem("p1_x1_out"), 16)

            sp.wait_ge(sem("x_split"), 1)
            with sp.Fori(0, NC) as q:
                pass1(q, 512, 512, P)
            pass1(NC, LASTW, LAST, LASTW)

            sp.wait_ge(sem("p1_x1_out"), 16 * (NC + 1))

            def rows_dma(dram, sl, q, last, store, name):
                if last:
                    at, tile_rows = dram[ds(q * 512, LASTW), :], sl[0:LASTW, 0:F]
                else:
                    at = dram[ds(q * 512, 512), :].rearrange("(t p) f -> p t f", p=P)
                    tile_rows = sl[:, :].rearrange("p (t f) -> p t f", f=F)
                to, of = (at, tile_rows) if store else (tile_rows, at)
                sp.dma_start(to, of).then_inc(sem(name), 16)

            def pass2_store(q, last):
                sp.wait_ge(sem("p2_yf"), q + 1)
                rows_dma(y_dram, slot[4], q, last, True, "p2_y_out")
                sp.wait_ge(sem("p2_res"), q + 1)
                rows_dma(res_dram, slot[5], q, last, True, "p2_res_out")

            sp.wait_ge(sem("p1_done"), 1)
            rows_dma(x1_dram, slot[2], 0, False, False, "p2_x1_in")
            with sp.Fori(1, NC) as q:
                sp.wait_ge(sem("p2_x1T"), q)
                rows_dma(x1_dram, slot[2], q, False, False, "p2_x1_in")
                pass2_store(q - 1, False)
            sp.wait_ge(sem("p2_x1T"), NC)
            rows_dma(x1_dram, slot[2], NC, True, False, "p2_x1_in")
            pass2_store(NC - 1, False)
            pass2_store(NC, True)
            sp.wait_ge(sem("p2_res_out"), 16 * (NC + 1))
            sp.wait_ge(sem("p2_y_out"), 16 * (NC + 1))

            def rows_in(q, par, last=False):
                if not isinstance(q, int) or q >= 2:
                    sp.wait_ge(sem("p3_sum"), 3 * (q - 1))
                rows_dma(res_dram, slot[par], q, last, False, f"p3_in{par}")
                rows_dma(x1_dram, slot[2 + par], q, last, False, f"p3_in{par}")

            def rows_out(q, par):
                sp.wait_ge(sem("p3_out"), q + 1)
                rows_dma(out, slot[6 + par], q, False, True, f"p3_stored{par}")

            sp.wait_ge(sem("p2_done"), 1)
            rows_in(0, 0)
            rows_in(1, 1)
            with sp.Fori(0, NC - 2, 2) as q:
                q = by_twos(q, 0, NC - 2)
                rows_in(q + 2, 0)
                rows_out(q, 0)
                rows_in(q + 3, 1)
                rows_out(q + 1, 1)
            rows_in(NC, 0, last=True)
            rows_out(NC - 2, 0)
            rows_out(NC - 1, 1)
            sp.wait_ge(sem("p3_out"), NC + 1)
            sp.dma_start(out[NC * 512:N, :], slot[6][0:LAST, 0:F]).then_inc(sem("p3_stored0"), 16)
            sp.wait_ge(sem("p3_stored0"), 16 * (NC // 2 + 1))
            sp.wait_ge(sem("p3_stored1"), 16 * (NC // 2))

        @block.gpsimd
        def _(pool):
            g = nc.gpsimd
            g.memset(raw_dst[:, FULL:CP], PAD_DST)
            g.memset(raw_src[:, FULL:CP], 0)
            g.memset(raw_typ[:, FULL:CP], 0).then_inc(sem("pads_set"), 1)
            g.iota(iota_h[:, :], pattern=[[1, SPAN]], base=0, channel_multiplier=0, allow_small_or_imprecise_dtypes=True)
            g.iota(tile_off[:, :], pattern=[[P, TILES]], base=-CENTER, channel_multiplier=0, allow_small_or_imprecise_dtypes=True)
            g.iota(thr[:, :], pattern=[[P, 2]], base=0, channel_multiplier=P, allow_small_or_imprecise_dtypes=True)
            g.memset(zero[:, :], 0.0)
            g.memset(ones[:, :], 1.0)
            g.memset(eps[:, :], 1e-5)
            g.memset(Cn[:, TILES:, :], 0.0)
            g.memset(before[:, :], 1.0)
            g.memset(ident[:, :], 0.0).then_inc(sem("filled"), 1)
            pool.wait_ge(sem("filled"), 1)
            g.affine_select(out=before[:, :], in_=before[:, :], compare_op=ALU.is_gt, fill=0.0,
                            base=0, pattern=[[1, TILES]], channel_multiplier=-1)
            g.affine_select(out=ident[:, :], in_=ident[:, :], compare_op=ALU.not_equal, fill=1.0,
                            base=0, pattern=[[-1, P]], channel_multiplier=1).then_inc(sem("consts"), 1)

            pool.wait_ge(sem("table_set"), 1)
            with pool.Fori(0, TILES) as t:
                lo = first_of_tile(pool, t)
                nb, st = batches_of_tile(pool, t)
                with pool.Fori(0, nb) as i:
                    c0 = first_chunk(lo, i)
                    k = st + i
                    for h in range(2):
                        half = slice(h * V, h * V + V)
                        pool.wait_ge(sem("dist_set"), k * 2 + (h + 1))
                        g.tensor_tensor(diff[:, half, :], iota_h[:, 0:P].unsqueeze(1).to_broadcast([P, V, P]),
                                        dst_f[:, ds(c0 + h * V, V)].unsqueeze(2).to_broadcast([P, V, P]), ALU.subtract).then_inc(sem("diff_set"), 1)
                    for h in range(2):
                        half = slice(h * V, h * V + V)
                        pool.wait_ge(sem("items_done"), k * U + V * (h + 1))
                        g.tensor_copy(T_now[:, half, :], T[:, ds(c0 + h * V, V), :]).then_inc(sem("types_set"), 1)

            pool.wait_ge(sem("tiles_summed"), TILES)
            g.memset(xp[:, TILES - 1, :, :], 0.0).then_inc(sem("xp_zeroed"), 1)
            pool.wait_ge(sem("digits_stored"), (TILES + 1) * DIGITS)
            g.memset(x1p[:, TILES - 1, :, :], 0.0).then_inc(sem("x1p_zeroed"), 1)

            general = is_general_after_flag(pool)
            with pool.If(general):
                g.memset(g_dst_i[:, FULL:CP], PAD_DST)
                g.memset(g_src[:, FULL:CP], 0)
                g.memset(g_typ_i[:, FULL:CP], 0)
                g.memset(g_sum[:, TILES:, :], 0.0)
                g.iota(g_iota[:, :], pattern=[[1, TILES * P]], base=0, channel_multiplier=0,
                       allow_small_or_imprecise_dtypes=True).then_inc(sem("g_pads_set"), 1)
            with pool.Else():
                pool.nop()

            def gather(call, table_dram):
                with pool.If(general):
                    with pool.Fori(0, CHUNKS) as c:
                        pool.wait_ge(sem("g_idx_set"), c + (call - 1) * CHUNKS + 1)
                        settle(pool, "pool_settled")
                        g.indirect_dma_start(g_rows[:, :], None, table_dram,
                                             bass.IndirectOffsetOnAxis(ap=g_idx[:, 0:1].bitcast(u32), axis=0)).then_inc(sem("g_rows_in"), 16)
                with pool.Else():
                    pool.nop()

            def low_parts(name, target, q, last):
                rows, k = (LASTW, 1) if last else (P, 4)
                full = slot[5 if name == "p1" else 4][0:rows, 0:k * F].rearrange("p (t f) -> p t f", f=F)
                rest = slot[6 if name == "p1" else 0][0:rows, 0:k * F].rearrange("p (t f) -> p t f", f=F)
                hi, mid, low = (target[0:rows, ds(4 * q, k), n, :] for n in range(PARTS))
                pool.wait_ge(sem(f"{name}_hi"), q + 1)
                g.tensor_tensor(rest, full, hi, ALU.subtract).then_inc(sem(f"{name}_rest"), 1)
                pool.wait_ge(sem(f"{name}_mid"), q + 1)
                g.tensor_tensor(low, rest, mid, ALU.subtract).then_inc(sem(f"{name}_low"), 1)

            gather(1, x)
            with pool.Fori(0, NC) as q:
                low_parts("p1", x1p, q, False)
            low_parts("p1", x1p, NC, True)
            with pool.If(general):
                pool.wait_ge(sem("p1_x1_out"), 16 * (NC + 1))
            with pool.Else():
                pool.nop()
            gather(2, x1_dram)
            with pool.Fori(0, NC) as q:
                low_parts("p2", xp, q, False)
            low_parts("p2", xp, NC, True)
            with pool.If(general):
                pool.wait_ge(sem("p2_y_out"), 16 * (NC + 1))
            with pool.Else():
                pool.nop()
            gather(3, y_dram)

        @block.vector
        def _(dve):
            v = nc.vector
            chain = [0]

            def then(ins):
                chain[0] += 1
                ins.then_inc(sem("dve_chain"), 1)
                dve.wait_ge(sem("dve_chain"), chain[0])

            dve.wait_ge(sem("ends_in"), 48)
            dve.wait_ge(sem("consts"), 1)
            v.tensor_copy(first_f[:, :], first_i[:, :])
            then(v.tensor_copy(last_f[:, 0:FULL], last_i[:, 0:FULL]))
            then(v.tensor_scalar(passed[:, :], first_f[:, :], thr[:, 1:2], None, ALU.is_lt, ALU.add, accum_out=tcol[:, 0:1]))
            then(v.tensor_scalar(passed[:, 0:FULL], last_f[:, 0:FULL], thr[:, 0:1], None, ALU.is_lt, ALU.add, accum_out=tcol[:, 1:2]))
            then(v.tensor_scalar(tcol[:, 2:3], tcol[:, 1:2], float(CHUNKS - 1), None, ALU.min))
            then(v.tensor_tensor(tcol[:, 3:4], tcol[:, 0:1], tcol[:, 2:3], ALU.subtract))
            then(v.tensor_scalar(tcol[:, 4:5], tcol[:, 3:4], float((LEAST - 1) * U + 1), float(U - 1), ALU.max, ALU.add))
            then(v.tensor_scalar(tcol[:, 6:7], tcol[:, 4:5], float(DIVIDE), None, ALU.mult))
            then(v.tensor_copy(tcol_i[:, 0:1], tcol[:, 6:7]))
            then(v.tensor_scalar(tcol_i[:, 1:2], tcol_i[:, 0:1], 16, None, ALU.logical_shift_right))
            v.tensor_copy(tcol[:, 5:6], tcol_i[:, 1:2]).then_inc(sem("tile_columns"), 1)
            dve.wait_ge(sem("table_rows"), 1)
            v.tensor_copy(table[:, :].rearrange("a (n t) -> a n t", n=3)[:, :, 0:TILES],
                          PS[0:1, 6, 0:96].rearrange("a (n t) -> a n t", n=3)[:, :, 0:TILES]).then_inc(sem("table_copied"), 1)

            dve.wait_ge(sem("dst_in"), 32)
            v.tensor_scalar(dst_f[:, :], raw_dst[:, :], float(-CENTER), None, ALU.add)
            dve.wait_ge(sem("src_in"), 32)
            then(v.tensor_copy(edge_f[:, :], raw_src[:, :]))
            (dg, dg2), (wt, wt2) = (digit_a, digit_b), (weight_a, weight_b)
            v.tensor_scalar(dg[:, :], edge_f[:, :], float(SPAN), None, ALU.is_ge)
            then(v.tensor_scalar(wt[:, :], edge_f[:, :], float(SPAN), 15.0, ALU.is_ge, ALU.mult))
            for k in range(2, DIGITS):
                then(v.scalar_tensor_tensor(out=dg2[:, :], in0=edge_f[:, :], scalar=float(SPAN * k), in1=dg[:, :], op0=ALU.is_ge, op1=ALU.add))
                dg, dg2 = dg2, dg
                then(v.tensor_scalar(src_w[:, :], edge_f[:, :], float(SPAN * k), 15.0 * 16 ** (k - 1), ALU.is_ge, ALU.mult))
                then(v.tensor_tensor(wt2[:, :], wt[:, :], src_w[:, :], ALU.add))
                wt, wt2 = wt2, wt
            v.tensor_scalar(src_w[:, :], wt[:, :], 1.0, None, ALU.add)
            v.scalar_tensor_tensor(out=src_col[:, :], in0=dg[:, :], scalar=float(-SPAN), in1=edge_f[:, :], op0=ALU.mult, op1=ALU.add)
            dve.wait_ge(sem("weights_in"), 16 * len(weights))
            v.tensor_tensor(rz_b[:, :], gate_b[:, 0:2], gate_b[:, 3:5], ALU.add)
            v.tensor_tensor(emb_b[:, :], emb_s[:, :], bmsg_b[:, :], ALU.add)
            dve.wait_ge(sem("typ_in"), 32)
            for k in range(NTYPE):
                if k == 0:
                    ins = v.tensor_scalar(T[:, :, k], raw_typ[:, :], 0.0, None, ALU.is_le)
                elif k == NTYPE - 1:
                    ins = v.tensor_scalar(T[:, :, k], raw_typ[:, :], float(k), None, ALU.is_ge)
                else:
                    ins = v.tensor_scalar(T[:, :, k], raw_typ[:, :], float(k), None, ALU.is_equal)
            ins.then_inc(sem("table_set"), 1)
            dve.wait_ge(sem("table_set"), 1)

            def take_digits(t, some):
                dve.wait_ge(sem("packedT_in"), t + 1)
                for f in some:
                    dve.wait_ge(sem("digits_stored"), t * DIGITS + (f + 1))
                    v.tensor_scalar(digits[:, f, :], packedT[:, :], 4 * f, 15, ALU.logical_shift_right,
                                    ALU.bitwise_and).then_inc(sem("digits_taken"), 1)

            def source_batch(c0, k):
                for u in range(U):
                    if u % V == 0:
                        dve.wait_ge(sem("items_done"), k * U + (u + V))
                    v.tensor_scalar(S[:, u, :], iota_h[:, :], src_col[:, ds(c0 + u, 1)], src_w[:, ds(c0 + u, 1)],
                                    ALU.is_equal, ALU.mult).then_inc(sem("S_set"), 1)

            def source_rows(t, between):
                lo = first_of_tile(dve, t)
                nb, st = batches_of_tile(dve, t)
                for i in range(LEAST - 1):
                    between(i)
                    source_batch(first_chunk(lo, i), st + i)
                between(LEAST - 1)
                with dve.Fori(LEAST - 1, nb) as i:
                    source_batch(first_chunk(lo, i), st + i)

            for t in range(LAG):
                source_rows(t, lambda i: None)
            with dve.Fori(LAG, TILES, 2) as t:
                t = by_twos(t, LAG, TILES)
                for n in range(2):
                    source_rows(t + n, lambda i: take_digits(t + n - LAG, SHARES[i]))
            for t in range(TILES - LAG, TILES):
                take_digits(t, range(DIGITS))

            dve.wait_ge(sem("digits_stored"), (TILES + 1) * DIGITS)
            v.tensor_reduce(verdict[:, :], count[:, :, :], AX.XY, ALU.add).then_inc(sem("verdict_set"), 1)
            dve.wait_ge(sem("verdict_sum"), 1)
            then(v.tensor_scalar(flag[:, 0:1], PS[0:1, 7, 0:1], float(E), None, ALU.not_equal))
            v.tensor_copy(flag_i[:, 0:1], flag[:, 0:1]).then_inc(sem("flag_set"), 1)

            dve.wait_ge(sem("xp_zeroed"), 1)
            for c in range(NC + 1):
                rows, k = (P, 4) if c < NC else (LAST, 1)
                dve.wait_ge(sem("x_hi"), c + 1)
                full = xstage[0:rows, 4 * c:4 * c + k, :]
                rest = xrest(c)[0:rows, 0:k * F].rearrange("p (t f) -> p t f", f=F)
                if c >= 2:
                    dve.wait_ge(sem("x_low"), c - 1)
                v.tensor_tensor(rest, full, xp[0:rows, 4 * c:4 * c + k, 0, :], ALU.subtract).then_inc(sem("x_rest"), 1)
                dve.wait_ge(sem("x_mid"), c + 1)
                v.tensor_tensor(xp[0:rows, 4 * c:4 * c + k, 2, :], rest, xp[0:rows, 4 * c:4 * c + k, 1, :], ALU.subtract).then_inc(sem("x_low"), 1)
            dve.wait_ge(sem("x_low"), NC + 1)
            v.memset(flag[:, 3:4], 0.0).then_inc(sem("x_split"), 1)

            general = is_general(dve)
            calls = general_rows(dve, v, general)
            calls(0)
            calls(1)

            dve.wait_ge(sem("types_ready"), 1)
            then(v.tensor_reduce(ideg[:, :], Cn[:, 0:TILES, :], AX.X, ALU.add))
            then(v.tensor_scalar(ideg[:, :], ideg[:, :], 1.0, None, ALU.max))
            then(v.reciprocal(ideg[:, :], ideg[:, :]))

            def pass1(q, w, last):
                rows, k = (LASTW, 1) if last else (P, 4)
                sT, mT, x_, rr, zz, tt, nn, yy = (slot[n][:, 0:w] for n in range(8))
                dve.wait_ge(sem("p1_m_sum"), q + 1)
                v.tensor_copy(mT, PS[:, 3, 0:w]).then_inc(sem("p1_m"), 1)
                dve.wait_ge(sem("p1_gates"), q + 1)
                dve.wait_ge(sem("p1_r"), q + 1)
                dve.wait_ge(sem("p1_x1_out"), 16 * q)
                dve.wait_ge(sem("p1_low"), q)
                v.scalar_tensor_tensor(out=tt, in0=PS[:, 7, 0:w], scalar=gate_b[:, 5:6], in1=rr, op0=ALU.add, op1=ALU.mult).then_inc(sem("p1_t"), 1)
                dve.wait_ge(sem("p1_t"), 2 * q + 1)
                v.tensor_tensor(tt, tt, PS[:, 6, 0:w], ALU.add).then_inc(sem("p1_t"), 1)
                dve.wait_ge(sem("p1_n"), q + 1)
                v.tensor_tensor(rr, x_, nn, ALU.subtract).then_inc(sem("p1_e"), 1)
                v.tensor_tensor(tt, x_, nn, ALU.add).then_inc(sem("p1_e"), 1)
                dve.wait_ge(sem("p1_e"), 3 * q + 1)
                v.tensor_tensor(zz, zz, rr, ALU.mult).then_inc(sem("p1_e"), 1)
                dve.wait_ge(sem("p1_e"), 3 * q + 3)
                v.tensor_tensor(yy, zz, tt, ALU.add).then_inc(sem("p1_y"), 1)
                dve.wait_ge(sem("p1_yT"), q + 1)
                norm("p1", q, rows, k, lambda n: PS[0:rows, 3, n * F:(n + 1) * F], slot[5], "p1_x1")

            def norm(name, q, rows, k, row_of, to, done, par=None):
                for n in range(k):
                    ins = v.bn_stats(stats[0:rows, n, :], row_of(n))
                ins.then_inc(sem(f"{name}_norm"), 1)
                dve.wait_ge(sem(f"{name}_norm"), 3 * q + 1)
                dve.wait_ge(sem(done), q)
                settle(dve, "dve_settled")
                for n in range(k):
                    ins = v.bn_aggr(meanvar[0:rows, n, :], stats[0:rows, n, :])
                ins.then_inc(sem(f"{name}_norm"), 1)
                dve.wait_ge(sem(f"{name}_sd"), q + 1)
                v.reciprocal(rstd[0:rows, 0:k], sd[0:rows, 0:k]).then_inc(sem(f"{name}_norm"), 1)
                dve.wait_ge(sem(f"{name}_norm"), 3 * q + 3)
                for n in range(k):
                    ins = v.tensor_scalar(to[0:rows, n * F:(n + 1) * F], row_of(n), meanvar[0:rows, n, 0:1],
                                          rstd[0:rows, n:n + 1], ALU.subtract, ALU.mult)
                ins.then_inc(sem(done), 1)

            with dve.Fori(0, NC) as q:
                pass1(q, 512, False)
            pass1(NC, LASTW, True)
            dve.wait_ge(sem("p1_x1"), NC + 1)
            dve.wait_ge(sem("p1_hi"), NC + 1)
            dve.wait_ge(sem("p1_low"), NC + 1)
            dve.wait_ge(sem("p1_yT"), NC + 1)
            v.memset(stats[:, 0, 0:1], 0.0).then_inc(sem("p1_done"), 1)
            calls(2)

            def mean_neighbours(q, w):
                nT, dg = slot[0][:, 0:w], slot[7][:, 0:w]
                dve.wait_ge(sem("p2_deg_sum"), q + 1)
                v.tensor_scalar(dg, PS[:, 5, 0:w], 1.0, None, ALU.max).then_inc(sem("p2_deg"), 1)
                dve.wait_ge(sem("p2_deg"), 2 * q + 1)
                v.reciprocal(dg, dg).then_inc(sem("p2_deg"), 1)
                dve.wait_ge(sem("p2_deg"), 2 * q + 2)
                dve.wait_ge(sem("p2_agg"), q + 1)
                dve.wait_ge(sem("p2_low"), q)
                v.tensor_tensor(nT, PS[:, 0, 0:w], dg, ALU.mult).then_inc(sem("p2_n"), 1)

            def residual(q, last):
                rows, k = (LASTW, 1) if last else (P, 4)
                dve.wait_ge(sem("p2_y_sum"), q + 1)
                dve.wait_ge(sem("p2_res_out"), 16 * q)
                v.tensor_tensor(slot[5][0:rows, 0:k * F].rearrange("p (t f) -> p t f", f=F),
                                PS[0:rows, 4, 0:k * F].rearrange("p (t f) -> p t f", f=F),
                                b2_b[0:rows, :].unsqueeze(1).to_broadcast([rows, k, F]), ALU.add).then_inc(sem("p2_res"), 1)

            mean_neighbours(0, 512)
            with dve.Fori(1, NC) as q:
                residual(q - 1, False)
                mean_neighbours(q, 512)
            residual(NC - 1, False)
            mean_neighbours(NC, LASTW)
            residual(NC, True)
            dve.wait_ge(sem("p2_low"), NC + 1)
            dve.wait_ge(sem("p2_res"), NC + 1)
            dve.wait_ge(sem("p2_y_out"), 16 * (NC + 1))
            dve.wait_ge(sem("p2_res_out"), 16 * (NC + 1))
            v.memset(stats[:, 0, 0:1], 0.0).then_inc(sem("p2_done"), 1)
            calls(3)

            def pass3(q, par, last):
                rows, k = (LAST, 1) if last else (P, 4)
                total = slot[4 + par][0:rows, 0:k * F]
                dve.wait_ge(sem("p3_agg"), q + 1)
                dve.wait_ge(sem("p3_out"), q)
                v.tensor_reduce(total.rearrange("p (t f) -> p t f", f=F),
                                PS[0:rows, 4 * par:4 * par + k, 0:PARTS * F].rearrange("p t (s f) -> p t f s", s=PARTS),
                                AX.X, ALU.add).then_inc(sem("p3_sum"), 1)
                dve.wait_ge(sem("p3_sum"), 3 * q + 1)
                dve.wait_ge(sem(f"p3_in{par}"), (q - par) * 16 + 32)
                for n in range(k):
                    cols = slice(n * F, (n + 1) * F)
                    ins = v.scalar_tensor_tensor(out=total[:, cols], in0=total[:, cols], scalar=ideg[0:rows, ds(4 * q + n, 1)],
                                                 in1=slot[par][0:rows, cols], op0=ALU.mult, op1=ALU.add)
                ins.then_inc(sem("p3_sum"), 1)
                dve.wait_ge(sem("p3_sum"), 3 * q + 2)
                v.tensor_tensor(total, total, slot[2 + par][0:rows, 0:k * F], ALU.add).then_inc(sem("p3_sum"), 1)
                dve.wait_ge(sem("p3_sum"), 3 * q + 3)
                dve.wait_ge(sem(f"p3_stored{par}"), (q - par) * 8)
                norm("p3", q, rows, k, lambda n: total[:, n * F:(n + 1) * F], slot[6 + par], "p3_out")

            with dve.Fori(0, NC, 2) as q:
                q = by_twos(q, 0, NC)
                pass3(q, 0, False)
                pass3(q + 1, 1, False)
            pass3(NC, 0, True)

        @block.tensor
        def _(pe):
            mm = nc.tensor.matmul

            pe.wait_ge(sem("consts"), 1)
            pe.wait_ge(sem("tile_columns"), 1)
            mm(PS[0:1, 6, 0:TILES], tcol[:, 2:3], ident[0:TILES, 0:TILES], start=True, stop=True)
            mm(PS[0:1, 6, 32:32 + TILES], tcol[:, 5:6], ident[0:TILES, 0:TILES], start=True, stop=True)
            mm(PS[0:1, 6, 64:64 + TILES], tcol[:, 5:6], before[:, :], start=True, stop=True).then_inc(sem("table_rows"), 1)
            mm(PS[:, 7, 0:16], zero[:, :], zero[:, 0:16], start=True, stop=True).then_inc(sem("items_done"), U)

            zeros = zero[:, 0:1].to_broadcast([P, 512])
            zeros_b = zero[:, 0:1].to_broadcast([P, P + NTYPE])

            def count_tile(t, par):
                nb, st = batches_of_tile(pe, t)
                if not isinstance(t, int) or t >= 2:
                    pe.wait_ge(sem("packed_out"), t - 1)
                mm(PS[:, 2 * par, :], zero[:, :], zeros, start=True, stop=False)
                mm(PS[:, 2 * par + 1, 0:P + NTYPE], zero[:, :], zeros_b, start=True, stop=False)
                with pe.Fori(0, nb) as i:
                    k = st + i
                    for u in range(U):
                        if u % V == 0:
                            pe.wait_ge(sem("D_set"), k * 2 + (u // V + 3))
                            pe.wait_ge(sem("types_set"), k * 2 + (u // V + 1))
                        if u % 2 == 0:
                            pe.wait_ge(sem("S_set"), k * U + (u + 2))
                        rows = D[:, u, :]
                        mm(PS[:, 2 * par, :], rows, S[:, u, 0:512], start=False, stop=False)
                        mm(PS[:, 2 * par + 1, 0:P], rows, S[:, u, 512:SPAN], start=False, stop=False)
                        mm(PS[:, 2 * par + 1, P:P + NTYPE], rows, T_now[:, u, :], start=False, stop=False).then_inc(sem("items_done"), 1)
                mm(PS[:, 2 * par, :], zero[:, :], zeros, start=False, stop=True)
                mm(PS[:, 2 * par + 1, 0:P + NTYPE], zero[:, :], zeros_b, start=False, stop=True).then_inc(sem("tiles_summed"), 1)

            def turn_tile(t):
                pe.wait_ge(sem("packed_out"), t + 1)
                if not isinstance(t, int) or t > 0:
                    pe.wait_ge(sem("packedT_in"), t)
                for g in range(GROUPS):
                    ins = nc.tensor.transpose(PS[:, 4 + g // 4, (g % 4) * P:(g % 4 + 1) * P], packed[:, g * P:(g + 1) * P], ident[:, :])
                ins.then_inc(sem("turned"), 1)

            pe.wait_ge(sem("table_set"), 1)
            count_tile(0, 0)
            with pe.Fori(1, TILES, 2) as t:
                t = by_twos(t, 1, TILES)
                count_tile(t, 1)
                turn_tile(t - 1)
                count_tile(t + 1, 0)
                turn_tile(t)
            turn_tile(TILES - 1)

            pe.wait_ge(sem("verdict_set"), 1)
            mm(PS[0:1, 7, 0:1], ones[:, 0:1], verdict[:, :], start=True, stop=True).then_inc(sem("verdict_sum"), 1)
            general = is_general_after_flag(pe)

            def general_sum(n, width):
                with pe.If(general):
                    per = 4 * F // width * width if n else 512
                    banks = 1 if n == 0 else 7
                    pe.wait_ge(sem("g_start"), n + 1)
                    for b in range(banks):
                        mm(PS[:, b, :], zero[:, :], zeros, start=True, stop=False)
                    with pe.Fori(0, CHUNKS) as c:
                        pe.wait_ge(sem("g_onehot_set"), c + n * CHUNKS + 1)
                        if n == 0:
                            pe.wait_ge(sem("g_types_set"), c + 1)
                        else:
                            pe.wait_ge(sem("g_rows_in"), (c + (n - 1) * CHUNKS) * 16 + 16)
                        for t in range(TILES):
                            where = PS[:, 0, t * NTYPE:(t + 1) * NTYPE] if n == 0 else PS[:, t // 4, (t % 4) * F:(t % 4 + 1) * F]
                            ins = mm(where, g_onehot[:, t * P:(t + 1) * P], g_rows[:, 0:width], start=False, stop=False)
                        ins.then_inc(sem("g_used"), 1)
                    for b in range(banks):
                        ins = mm(PS[:, b, :], zero[:, :], zeros, start=False, stop=True)
                    ins.then_inc(sem("g_summed"), 1)
                    pe.wait_ge(sem("g_copied"), n + 1)
                with pe.Else():
                    pe.nop()

            general_sum(0, NTYPE)
            general_sum(1, F)

            def agg_third(name, parts, q, w, third):
                with pe.If(general):
                    if third == 2:
                        pe.wait_ge(sem(f"{name}_sum_staged"), q + 1)
                        for n in range(-(-w // P)):
                            rows = min(P, w - n * P)
                            ins = nc.tensor.transpose(PS[:, 0, n * P:n * P + rows],
                                                      g_stage[0:rows, n, :], ident[0:rows, 0:rows])
                        ins.then_inc(sem(f"{name}_agg"), 1)
                    else:
                        pe.nop()
                with pe.Else():
                    for j in range(TILES)[third * 9:third * 9 + 9]:
                        for s in range(PARTS):
                            ins = mm(PS[:, 0, 0:w], parts[:, j, s, :], AT[:, j, ds(q * 512, w)],
                                     start=(j == 0 and s == 0), stop=(j == TILES - 1 and s == PARTS - 1))
                    if third == 2:
                        ins.then_inc(sem(f"{name}_agg"), 1)
                pe.nop()

            def turn_types(name, q, w):
                pe.wait_ge(sem(f"{name}_types_staged"), q + 1)
                for n in range(-(-w // P)):
                    rows = min(P, w - n * P)
                    ins = nc.tensor.transpose(PS[0:NTYPE, 2, n * P:n * P + rows], c_stage[0:rows, n, :], ident[0:rows, 0:rows])
                ins.then_inc(sem(f"{name}_typeT"), 1)

            def messages(q, w):
                pe.wait_ge(sem("p1_s"), q + 1)
                pe.wait_ge(sem("p1_c"), q + 1)
                pe.wait_ge(sem("p1_x1"), q)
                mm(PS[:, 3, 0:w], wmsg_s[:, :], slot[0][:, 0:w], start=True, stop=False)
                mm(PS[:, 3, 0:w], emb_b[:, :], slot[7][0:NTYPE, 0:w], start=False, stop=True).then_inc(sem("p1_m_sum"), 1)

            def gates(q, w):
                pe.wait_ge(sem("p1_m"), q + 1)
                pe.wait_ge(sem("p1_xT_in"), 16 * (q + 1))
                m, x_ = slot[1][:, 0:w], slot[2][:, 0:w]
                for g in range(2):
                    mm(PS[:, 4 + g, 0:w], wih_s[:, g, :], m, start=True, stop=False)
                    mm(PS[:, 4 + g, 0:w], whh_s[:, g, :], x_, start=False, stop=True).then_inc(sem("p1_gate"), 1)
                mm(PS[:, 7, 0:w], whh_s[:, 2, :], x_, start=True, stop=True)
                mm(PS[:, 6, 0:w], wih_s[:, 2, :], m, start=True, stop=True).then_inc(sem("p1_gates"), 1)

            def rows_back(q, w):
                pe.wait_ge(sem("p1_y"), q + 1)
                for n in range(-(-w // P)):
                    rows = min(P, w - n * P)
                    ins = nc.tensor.transpose(PS[0:rows, 3, n * P:(n + 1) * P], slot[7][:, n * P:n * P + rows], ident[:, :])
                ins.then_inc(sem("p1_yT"), 1)

            def agg(name, parts, q, w, between):
                if not isinstance(q, int) or q > 0:
                    pe.wait_ge(sem("p1_s" if name == "p1" else "p2_n"), q)
                for third in range(3):
                    agg_third(name, parts, q, w, third)
                    between[third]()

            nothing = [lambda: None] * 3
            pe.wait_ge(sem("x_split"), 1)
            pe.wait_ge(sem("digits_stored"), (TILES + 1) * DIGITS)
            pe.wait_ge(sem("types_ready"), 1)
            turn_types("p1", 0, 512)
            agg("p1", xp, 0, 512, nothing)

            def p1_step(q, w, wprev):
                agg("p1", xp, q, w, [lambda: messages(q - 1, wprev), lambda: gates(q - 1, wprev),
                                     lambda: rows_back(q - 1, wprev)])
                pe.wait_ge(sem("p1_c"), q)
                turn_types("p1", q, w)

            with pe.Fori(1, NC) as q:
                p1_step(q, 512, 512)
            p1_step(NC, LASTW, 512)
            messages(NC, LASTW)
            gates(NC, LASTW)
            rows_back(NC, LASTW)

            pe.wait_ge(sem("p1_done"), 1)
            general_sum(2, F)

            def chunk_inputs(q, w):
                pe.wait_ge(sem("p2_c"), q)
                pe.wait_ge(sem("p2_x1c"), q)
                turn_types("p2", q, w)
                pe.wait_ge(sem("p2_x1_in"), 16 * (q + 1))
                for n in range(-(-w // P)):
                    rows = min(P, w - n * P)
                    ins = nc.tensor.transpose(PS[:, 1, n * P:n * P + rows], slot[2][0:rows, n * F:(n + 1) * F], ident[0:rows, 0:rows])
                ins.then_inc(sem("p2_x1T"), 1)

            def degrees(q, w):
                pe.wait_ge(sem("p2_c"), q + 1)
                mm(PS[:, 5, 0:w], ones[0:NTYPE, :], slot[7][0:NTYPE, 0:w], start=True, stop=True).then_inc(sem("p2_deg_sum"), 1)

            def hidden(q, w):
                pe.wait_ge(sem("p2_n"), q + 1)
                pe.wait_ge(sem("p2_x1c"), q + 1)
                pe.wait_ge(sem("p2_h"), 2 * q)
                for a in range(2):
                    mm(PS[:, 6 + a, 0:w], ws1[:, a, :], slot[3][:, 0:w], start=True, stop=False)
                    mm(PS[:, 6 + a, 0:w], wn1[:, a, :], slot[0][:, 0:w], start=False, stop=True).then_inc(sem("p2_h_sum"), 1)

            def second(q, w):
                pe.wait_ge(sem("p2_h"), 2 * (q + 1))
                pe.wait_ge(sem("p2_yf"), q)
                pe.wait_ge(sem("p2_res"), q)
                hid = [slot[1], slot[6]]
                for n in range(-(-w // P)):
                    rows = min(P, w - n * P)
                    for bank, wt in ((3, wn2), (4, ws2)):
                        for a in range(2):
                            ins = mm(PS[0:rows, bank, n * F:(n + 1) * F], hid[a][:, n * P:n * P + rows], wt[:, a, :],
                                     start=(a == 0), stop=(a == 1))
                ins.then_inc(sem("p2_y_sum"), 1)

            pe.wait_ge(sem("p1_low"), NC + 1)
            chunk_inputs(0, 512)
            agg("p2", x1p, 0, 512, [lambda: None, lambda: degrees(0, 512), lambda: None])

            def p2_step(q, w):
                def one():
                    hidden(q - 1, 512)
                    chunk_inputs(q, w)

                def two():
                    second(q - 1, 512)
                    degrees(q, w)

                agg("p2", x1p, q, w, [one, two, lambda: None])

            with pe.Fori(1, NC) as q:
                p2_step(q, 512)
            p2_step(NC, LASTW)
            hidden(NC, LASTW)
            second(NC, LASTW)

            pe.wait_ge(sem("p2_done"), 1)
            general_sum(3, F)

            def agg_rows(q, par, last):
                if not isinstance(q, int) or q >= 2:
                    pe.wait_ge(sem("p3_out"), q - 1)
                tiles = [(0, LAST)] if last else [(n, P) for n in range(4)]
                with pe.If(general):
                    for n, rows in tiles:
                        mm(PS[0:rows, 4 * par + n, 0:F], ident[:, 0:rows], g_sum[:, ds(4 * q + n, 1), :].rearrange("p a f -> p (a f)"), start=True, stop=True)
                        ins = mm(PS[0:rows, 4 * par + n, F:PARTS * F], zero[:, 0:rows], zero[:, 0:1].to_broadcast([P, (PARTS - 1) * F]), start=True, stop=True)
                    ins.then_inc(sem("p3_agg"), 1)
                with pe.Else():
                    for n, rows in tiles:
                        for j in range(TILES):
                            ins = mm(PS[0:rows, 4 * par + n, 0:PARTS * F], AT[:, j, ds(q * 512 + n * P, rows)],
                                     xp[:, j, :, :].rearrange("p s f -> p (s f)"), start=(j == 0), stop=(j == TILES - 1))
                    ins.then_inc(sem("p3_agg"), 1)
                pe.nop()

            agg_rows(0, 0, False)
            agg_rows(1, 1, False)
            with pe.Fori(2, NC, 2) as q:
                q = by_twos(q, 2, NC)
                agg_rows(q, 0, False)
                agg_rows(q + 1, 1, False)
            agg_rows(NC, 0, True)

        @block.scalar
        def _(act):
            a = nc.scalar

            def dest_batch(k):
                for h in range(2):
                    half = slice(h * V, h * V + V)
                    act.wait_ge(sem("D_set"), k * 2 + (h + 1))
                    act.wait_ge(sem("diff_set"), k * 2 + (h + 1))
                    a.activation(dist[:, half, :], diff[:, half, :], ACT.Abs, bias=off_now[:, :]).then_inc(sem("dist_set"), 1)
                for h in range(2):
                    half = slice(h * V, h * V + V)
                    act.wait_ge(sem("items_done"), k * U + V * (h + 1))
                    act.wait_ge(sem("dist_set"), k * 2 + (h + 3))
                    a.activation(D[:, half, :], dist[:, half, :], ACT.Relu, bias=1.0, scale=-1.0).then_inc(sem("D_set"), 1)

            def dest_rows(t, between):
                nb, st = batches_of_tile(act, t)
                act.wait_ge(sem("dist_set"), st * 2 + 2)
                a.activation(off_now[:, :], tile_off[:, ds(t, 1)], ACT.Copy).then_inc(sem("off_set"), 1)
                act.wait_ge(sem("off_set"), t + 1)
                for i in range(LEAST - 1):
                    dest_batch(st + i)
                    between(i)
                with act.Fori(LEAST - 1, nb) as i:
                    dest_batch(st + i)
                between(LEAST - 1)

            def packed_out(t, par):
                act.wait_ge(sem("tiles_summed"), t + 1)
                act.wait_ge(sem("turned"), t)
                a.activation(packed[:, 0:512], PS[:, 2 * par, :], ACT.Copy)
                a.activation(packed[:, 512:SPAN], PS[:, 2 * par + 1, 0:P], ACT.Copy)
                a.activation(Cn[:, ds(t, 1), :].rearrange("p a k -> p (a k)"), PS[:, 2 * par + 1, P:P + NTYPE], ACT.Copy).then_inc(sem("packed_out"), 1)

            def packedT_in(t):
                act.wait_ge(sem("turned"), t + 1)
                act.wait_ge(sem("digits_taken"), t * DIGITS)
                a.activation(packedT[:, 0:512], PS[:, 4, :], ACT.Copy)
                a.activation(packedT[:, 512:SPAN], PS[:, 5, 0:P], ACT.Copy).then_inc(sem("packedT_in"), 1)

            def store_digits(t, w, some=range(DIGITS)):
                for f in some:
                    act.wait_ge(sem("digits_taken"), t * DIGITS + f + 1)
                    a.activation(AT[:, GROUPS * f:GROUPS * f + GROUPS, ds(t * P, w)],
                                 digits[:, f, :].rearrange("p (g m) -> p g m", g=GROUPS)[:, :, 0:w], ACT.Copy,
                                 accum_out=count[:, ds(t, 1), f:f + 1].rearrange("p a b -> p (a b)")).then_inc(sem("digits_stored"), 1)

            act.sem_inc(sem("digits_stored"), DIGITS)
            act.sem_inc(sem("dist_set"), 2)
            act.sem_inc(sem("D_set"), 2)
            act.wait_ge(sem("table_set"), 1)
            def between_batches(t, par, i):
                if not isinstance(t, int) or t >= LAG:
                    store_digits(t - LAG, P, SHARES[i])
                if i == LEAST - 1 and (not isinstance(t, int) or t >= 1):
                    packed_out(t - 1, par)
                if i == LEAST - 1 and (not isinstance(t, int) or t >= 2):
                    packedT_in(t - 2)

            for t in range(LAG):
                dest_rows(t, lambda i: between_batches(t, (t - 1) % 2, i))
            with act.Fori(LAG, TILES, 2) as t:
                t = by_twos(t, LAG, TILES)
                for n in range(2):
                    dest_rows(t + n, lambda i: between_batches(t + n, n, i))
            packed_out(TILES - 1, (TILES - 1) % 2)
            packedT_in(TILES - 2)
            store_digits(TILES - 3, P)
            packedT_in(TILES - 1)
            store_digits(TILES - 2, P)
            store_digits(TILES - 1, LASTW)

            for c in range(NC + 1):
                rows, k = (P, 4) if c < NC else (LAST, 1)
                act.wait_ge(sem(f"x_in{c}"), 16)
                if c == NC:
                    act.wait_ge(sem("xp_zeroed"), 1)
                a.activation(xp[0:rows, 4 * c:4 * c + k, 0, :], xstage[0:rows, 4 * c:4 * c + k, :], ACT.Copy).then_inc(sem("x_hi"), 1)
                act.wait_ge(sem("x_rest"), c + 1)
                a.activation(xp[0:rows, 4 * c:4 * c + k, 1, :], xrest(c)[0:rows, 0:k * F].rearrange("p (t f) -> p t f", f=F), ACT.Copy).then_inc(sem("x_mid"), 1)

            general = is_general_after_flag(act)

            def general_out(n):
                with act.If(general):
                    act.wait_ge(sem("g_summed"), n + 1)
                    if n == 0:
                        ins = a.activation(Cn[:, 0:TILES, :].rearrange("p t k -> p (t k)"), PS[:, 0, 0:TILES * NTYPE], ACT.Copy)
                    else:
                        for b in range(-(-TILES // 4)):
                            k = min(4, TILES - 4 * b)
                            ins = a.activation(g_sum[:, 4 * b:4 * b + k, :], PS[:, b, 0:k * F].rearrange("p (t f) -> p t f", f=F), ACT.Copy)
                    ins.then_inc(sem("g_copied"), 1)
                    act.wait_ge(sem("g_copied"), n + 1)
                with act.Else():
                    act.nop()

            general_out(0)
            act.wait_ge(sem("packed_out"), TILES)
            a.activation(sd[:, 0:1], eps[:, :], ACT.Copy).then_inc(sem("types_ready"), 1)
            general_out(1)

            def sqrt_var(name, q, rows, k):
                act.wait_ge(sem(f"{name}_norm"), 3 * q + 2)
                a.activation(sd[0:rows, 0:k], meanvar[0:rows, 0:k, 1:2].rearrange("p t a -> p (t a)"), ACT.Sqrt, bias=eps[0:rows, :]).then_inc(sem(f"{name}_sd"), 1)

            def high_parts(name, target, full, rest, q, last):
                rows, k = (LASTW, 1) if last else (P, 4)
                if last:
                    act.wait_ge(sem("x1p_zeroed" if name == "p1" else "xp_zeroed"), 1)
                a.activation(target[0:rows, ds(4 * q, k), 0, :], full[0:rows, 0:k * F].rearrange("p (t f) -> p t f", f=F), ACT.Copy).then_inc(sem(f"{name}_hi"), 1)
                act.wait_ge(sem(f"{name}_rest"), q + 1)
                a.activation(target[0:rows, ds(4 * q, k), 1, :], rest[0:rows, 0:k * F].rearrange("p (t f) -> p t f", f=F), ACT.Copy).then_inc(sem(f"{name}_mid"), 1)

            def stage_types(name, q):
                a.activation(c_stage[:, :, :], Cn[:, ds(4 * q, 4), :], ACT.Copy).then_inc(sem(f"{name}_types_staged"), 1)

            def stage_sums(name, q):
                settle(act, "act_settled")
                with act.If(general):
                    a.activation(g_stage[:, :, :], g_sum[:, ds(4 * q, 4), :], ACT.Copy).then_inc(sem(f"{name}_sum_staged"), 1)
                with act.Else():
                    act.nop()

            def sums_out(q, w):
                act.wait_ge(sem("p1_agg"), q + 1)
                act.wait_ge(sem("p1_m_sum"), q)
                a.activation(slot[0][:, 0:w], PS[:, 0, 0:w], ACT.Copy).then_inc(sem("p1_s"), 1)
                act.wait_ge(sem("p1_typeT"), q + 1)
                if not isinstance(q, int) or q < NC:
                    stage_sums("p1", q + 1)
                    stage_types("p1", q + 1)
                a.activation(slot[7][0:NTYPE, 0:w], PS[0:NTYPE, 2, 0:w], ACT.Copy).then_inc(sem("p1_c"), 1)

            def gate_functions(q, w):
                act.wait_ge(sem("p1_gates"), q + 1)
                act.wait_ge(sem("p1_y"), q)
                a.activation(slot[3][:, 0:w], PS[:, 4, 0:w], ACT.Sigmoid, bias=rz_b[:, 0:1]).then_inc(sem("p1_r"), 1)
                a.activation(slot[4][:, 0:w], PS[:, 5, 0:w], ACT.Sigmoid, bias=rz_b[:, 1:2])
                act.wait_ge(sem("p1_t"), 2 * q + 2)
                act.wait_ge(sem("p1_low"), q)
                a.activation(slot[6][:, 0:w], slot[5][:, 0:w], ACT.Tanh, bias=gate_b[:, 2:3]).then_inc(sem("p1_n"), 1)

            def normed(q, last):
                sqrt_var("p1", q, LASTW if last else P, 1 if last else 4)
                act.wait_ge(sem("p1_x1"), q + 1)
                high_parts("p1", x1p, slot[5], slot[6], q, last)

            act.wait_ge(sem("x_split"), 1)
            stage_sums("p1", 0)
            stage_types("p1", 0)
            sums_out(0, 512)
            with act.Fori(1, NC) as q:
                gate_functions(q - 1, 512)
                sums_out(q, 512)
                normed(q - 1, False)
            gate_functions(NC - 1, 512)
            sums_out(NC, LASTW)
            normed(NC - 1, False)
            gate_functions(NC, LASTW)
            normed(NC, True)

            act.wait_ge(sem("p1_done"), 1)
            general_out(2)

            def inputs_out(q, w):
                act.wait_ge(sem("p2_typeT"), q + 1)
                if not isinstance(q, int) or q < NC:
                    stage_types("p2", q + 1)
                act.wait_ge(sem("p2_n"), q)
                a.activation(slot[7][0:NTYPE, 0:w], PS[0:NTYPE, 2, 0:w], ACT.Copy).then_inc(sem("p2_c"), 1)
                act.wait_ge(sem("p2_x1T"), q + 1)
                act.wait_ge(sem("p2_h_sum"), 2 * q)
                a.activation(slot[3][:, 0:w], PS[:, 1, 0:w], ACT.Copy).then_inc(sem("p2_x1c"), 1)

            def relu_rows(q, w):
                act.wait_ge(sem("p2_y_sum"), q)
                for n, sl in enumerate((slot[1], slot[6])):
                    act.wait_ge(sem("p2_h_sum"), 2 * q + n + 1)
                    a.activation(sl[:, 0:w], PS[:, 6 + n, 0:w], ACT.Relu, bias=b1_s[:, n:n + 1]).then_inc(sem("p2_h"), 1)

            def second_out(q, last):
                rows, k = (LASTW, 1) if last else (P, 4)
                act.wait_ge(sem("p2_y_sum"), q + 1)
                act.wait_ge(sem("p2_y_out"), 16 * q)
                act.wait_ge(sem("p2_low"), q)
                a.activation(slot[4][0:rows, 0:k * F], PS[0:rows, 3, 0:k * F], ACT.Copy).then_inc(sem("p2_yf"), 1)
                act.wait_ge(sem("p2_yf"), q + 1)
                high_parts("p2", xp, slot[4], slot[0], q, last)

            stage_types("p2", 0)
            stage_sums("p2", 0)
            inputs_out(0, 512)
            with act.Fori(1, NC) as q:
                relu_rows(q - 1, 512)
                stage_sums("p2", q)
                inputs_out(q, 512)
                second_out(q - 1, False)
            relu_rows(NC - 1, 512)
            stage_sums("p2", NC)
            inputs_out(NC, LASTW)
            second_out(NC - 1, False)
            relu_rows(NC, LASTW)
            second_out(NC, True)

            act.wait_ge(sem("p2_done"), 1)
            general_out(3)
            with act.Fori(0, NC) as q:
                sqrt_var("p3", q, P, 4)
            sqrt_var("p3", NC, LAST, 1)


def kernel(**inputs):
    import numpy as np
    import concourse.bacc as bacc
    from concourse.bass_utils import run_bass_kernel_spmd

    nc = bacc.Bacc("TRN2", target_bir_lowering=False, num_devices=1, dynamic_dma_scratch_size=SCRATCH)
    a = {k: np.asarray(v) for k, v in inputs.items()}
    arrays = {
        "x": a["x"], "xT": a["x"].T,
        "dst_c": a["dst"][:FULL * P].reshape(FULL, P).T, "dst_t": a["dst"][FULL * P:].reshape(TAIL, 1),
        "src_c": a["src"][:FULL * P].reshape(FULL, P).T, "src_t": a["src"][FULL * P:].reshape(TAIL, 1),
        "typ_c": a["edge_type_9"][:FULL * P].reshape(FULL, P).T, "typ_t": a["edge_type_9"][FULL * P:].reshape(TAIL, 1),
        "wmsgT": a["L0_gnn_W_msg"].T, "bmsg": a["L0_gnn_b_msg"].reshape(1, F), "embed": a["L0_gnn_edge_embed"],
        "wihT": a["L0_gnn_W_ih"].T, "whhT": a["L0_gnn_W_hh"].T,
        "bgate": np.concatenate([a["L0_gnn_b_ih"].reshape(3, F), a["L0_gnn_b_hh"].reshape(3, F)]).T,
        "wself1": a["L1_gnn_w_self1"], "wneigh1": a["L1_gnn_w_neigh1"], "b1": a["L1_gnn_b1"].reshape(2, F).T,
        "wself2": a["L1_gnn_w_self2"], "wneigh2": a["L1_gnn_w_neigh2"], "b2": a["L1_gnn_b2"].reshape(1, F),
    }
    arrays = {k: np.ascontiguousarray(v) for k, v in arrays.items()}
    args = [nc.dram_tensor(k, v.shape, mybir.dt.from_np(v.dtype), kind="ExternalInput").ap() for k, v in arrays.items()]
    fp32 = mybir.dt.float32
    scratch = [nc.dram_tensor(k, (DW, F), fp32, kind="Internal").ap() for k in ("x1_rows", "y_rows", "res_rows")]
    out = nc.dram_tensor("out_rows", (N, F), fp32, kind="ExternalOutput").ap()
    graph_kernel(nc, *args, *scratch, out)
    return run_bass_kernel_spmd(nc, [arrays], core_ids=[0]).results[0]["out_rows"]
```

```python
import concourse.bass as bass
from concourse import mybir
from contextlib import ExitStack

N, E, F, H2, NTYPE = 3125, 100000, 128, 256, 9
P = 128
TILES = -(-N // P)
LAST = N - (TILES - 1) * P
LASTW = 64
DW = (TILES - 1) * P + LASTW
CHUNKS = -(-E // P)
FULL = E // P
TAIL = E - FULL * P
U = 6
V = U // 2
SHARES = ((0, 1), (2, 3), (4,))
LEAST = len(SHARES)
assert CHUNKS < 1 << 10 and -(-CHUNKS // U) < 1 << 8 and TILES * -(-CHUNKS // U) < 1 << 12
LAG = 3
DIVIDE = -(-(1 << 16) // U)
assert all(n * DIVIDE >> 16 == n // U for n in range(CHUNKS + U)) and (CHUNKS + U) * DIVIDE < 1 << 24
CP = CHUNKS + LEAST * U
DIGITS, GROUPS = 5, 5
SPAN = GROUPS * P
DIGIT_OF_TILE = 13
assert all(j * DIGIT_OF_TILE // 64 == j // GROUPS for j in range(TILES))
PAD_DST = 4000
CENTER = N // 2
NC = TILES // 4
PARTS = 3
CUTS = {"early": (0, 14, 22, TILES), "p1": (0, 7, 12, TILES), "p2": (0, 9, 18, TILES)}
SCRATCH = 2048


def graph_kernel(nc, x, xT, dst_c, dst_t, src_c, src_t, typ_c, typ_t, wmsgT, bmsg, embed, wihT, whhT,
                 bgate, wself1, wneigh1, b1, wself2, wneigh2, b2, x1_dram, y_dram, res_dram, out):
    fp32, bf16, fp16 = mybir.dt.float32, mybir.dt.bfloat16, mybir.dt.float16
    i32, u32 = mybir.dt.int32, mybir.dt.uint32
    ALU, ACT, AX = mybir.AluOpType, mybir.ActivationFunctionType, mybir.AxisListType
    SIZE = {fp32: 4, i32: 4, u32: 4, bf16: 2, fp16: 2}
    ds = bass.ds
    ctx = ExitStack()

    top = [nc.sbuf_base + (-nc.sbuf_base) % 32]

    def nbytes(shape, dt):
        n = SIZE[dt]
        for s in shape[1:]:
            n *= s
        return n + (-n) % 32

    def place(region, name, shape, dt):
        t = nc.alloc_sbuf_tensor_at(name, shape, dt, offset=region[0])
        region[0] += nbytes(shape, dt)
        return t

    def region(size):
        at = top[0]
        top[0] += size + (-size) % 32
        return at

    def sb(name, shape, dt):
        return place(top, name, shape, dt)

    part_bytes = TILES * PARTS * F * 2
    AT_at = region(TILES * DW * 2)
    AT = place([AT_at], "AT", [P, TILES, DW], bf16)
    A_at, B_at, W_at = region(part_bytes), region(part_bytes), region(CP * NTYPE * 2 + SPAN * 4 + 64)

    r = [A_at]
    digits = place(r, "digits", [P, DIGITS, SPAN], i32)
    packedT = place(r, "packedT", [P, SPAN], i32)
    D = place(r, "D", [P, U, P], bf16)
    bmsg_b, emb_s = (place(r, n, [NTYPE, F], fp32) for n in ("bmsg_b", "emb_s"))
    assert r[0] <= A_at + part_bytes
    r = [A_at]
    raw_dst, raw_src, raw_typ = (place(r, n, [P, CP], i32) for n in ("raw_dst", "raw_src", "raw_typ"))
    first_i = place(r, "first_i", [TILES, CHUNKS], i32)
    last_i = place(r, "last_i", [TILES, CHUNKS], i32)
    r = [AT_at]
    src_tile = place(r, "src_tile", [P, CP], i32)
    src_digit = place(r, "src_digit", [P, CP], i32)
    passed = place(r, "passed", [TILES, CHUNKS], bf16)
    r = [B_at]
    dst_f = place(r, "dst_f", [P, CP], fp16)
    src_col = place(r, "src_col", [P, CP], fp32)
    src_w = place(r, "src_w", [P, CP], fp32)
    S = place(r, "S", [P, U, SPAN], bf16)
    diff = place(r, "diff", [P, U, P], fp16)
    dist = place(r, "dist", [P, U, P], bf16)
    assert r[0] <= B_at + part_bytes
    r = [W_at]
    T = place(r, "T", [P, CP, NTYPE], bf16)
    packed = place(r, "packed", [P, SPAN], fp32)
    x1p = place([A_at], "x1p", [P, TILES, PARTS, F], bf16)
    xp = place([B_at], "xp", [P, TILES, PARTS, F], bf16)
    xstage = place([W_at], "xstage", [P, TILES, F], fp32)
    slot = [place([W_at + 2048 * k], f"slot{k}", [P, 512], fp32) for k in range(8)]
    assert W_at + 8 * 2048 <= top[0]

    iota_h = sb("iota_h", [P, SPAN], fp16)
    tile_off = sb("tile_off", [P, TILES], fp32)
    iota_t = sb("iota_t", [P, P], fp16)
    zero = sb("zero", [P, P], bf16)
    Cn = sb("Cn", [P, 4 * (NC + 1), NTYPE], fp32)
    c_stage = sb("c_stage", [P, 4, NTYPE], fp32)
    count = sb("count", [P, TILES, DIGITS], fp32)
    ident = sb("ident", [P, P], fp32)
    ones = sb("ones", [P, P], fp32)
    before = sb("before", [TILES, TILES], fp32)
    thr = sb("thr", [TILES, 2], fp32)
    tcol = sb("tcol", [TILES, 8], fp32)
    tcol_i = sb("tcol_i", [TILES, 2], i32)
    table = sb("table", [1, 3 * 32], i32)
    shifted = sb("shifted", [1, 2 * 32], i32)
    entries = sb("entries", [1, 32], i32)
    verdict = sb("verdict", [P, 1], fp32)
    flag = sb("flag", [1, 4], fp32)
    flag_i = sb("flag_i", [1, 4], i32)
    ideg = sb("ideg", [P, TILES], fp32)
    wmsg_s = sb("wmsg_s", [F, F], fp32)
    wih_s = sb("wih_s", [F, 3, F], fp32)
    whh_s = sb("whh_s", [F, 3, F], fp32)
    ws1 = sb("ws1", [F, 2, F], fp32)
    wn1 = sb("wn1", [F, 2, F], fp32)
    ws2 = sb("ws2", [F, 2, F], fp32)
    wn2 = sb("wn2", [F, 2, F], fp32)
    emb_b = sb("emb_b", [NTYPE, F], fp32)
    gate_b = sb("gate_b", [F, 6], fp32)
    rz_b = sb("rz_b", [F, 2], fp32)
    b1_s = sb("b1_s", [F, 2], fp32)
    b2_b = sb("b2_b", [P, F], fp32)
    stats = sb("stats", [P, 4, 6], fp32)
    meanvar = sb("meanvar", [P, 4, 2], fp32)
    sd = sb("sd", [P, 4], fp32)
    rstd = sb("rstd", [P, 4], fp32)
    eps = sb("eps", [P, 1], fp32)
    assert top[0] <= nc.sbuf_usable_end, (top[0], nc.sbuf_usable_end)

    r = [AT_at]
    g_iota = place(r, "g_iota", [P, TILES * P], fp32)
    g_onehot = place(r, "g_onehot", [P, TILES * P], fp32)
    g_src = place(r, "g_src", [P, CP], i32)
    g_dst_i = place(r, "g_dst_i", [P, CP], i32)
    g_typ_i = place(r, "g_typ_i", [P, CP], i32)
    g_dst = place(r, "g_dst", [P, CP], fp32)
    g_typ = place(r, "g_typ", [P, CP], fp32)
    g_idx = place(r, "g_idx", [P, 1], i32)
    g_rows = place(r, "g_rows", [P, F], fp32)
    g_sum = place(r, "g_sum", [P, 4 * (NC + 1), F], fp32)
    g_stage = place(r, "g_stage", [P, 4, F], fp32)
    assert r[0] <= A_at

    with ctx:
        PS = ctx.enter_context(nc.psum_tensor("PS", [P, 8, 512], fp32))
        sems = {}

        def sem(name):
            if name not in sems:
                sems[name] = ctx.enter_context(nc.semaphore(name))
            return sems[name]

        weights = [(wmsg_s[:, :], wmsgT), (wih_s[:, :, :], wihT.rearrange("k (g m) -> k g m", g=3)),
                   (whh_s[:, :, :], whhT.rearrange("k (g m) -> k g m", g=3)),
                   (ws1[:, :, :], wself1.rearrange("k (g m) -> k g m", g=2)),
                   (wn1[:, :, :], wneigh1.rearrange("k (g m) -> k g m", g=2)),
                   (ws2[:, :, :], wself2.rearrange("(g k) m -> k g m", g=2)),
                   (wn2[:, :, :], wneigh2.rearrange("(g k) m -> k g m", g=2)),
                   (emb_s[:, :], embed), (bmsg_b[:, :], bmsg.partition_broadcast(NTYPE)),
                   (gate_b[:, :], bgate), (b1_s[:, :], b1), (b2_b[:, :], b2.partition_broadcast(P))]

        def tile_entry(eng, t):
            entry = eng.value_load(entries[0:1, ds(t, 1)], min_val=0, max_val=(1 << 30) - 1)
            lo = (entry & 1023).with_bounds(min_val=0, max_val=CHUNKS - 1)
            nb = ((entry >> 10) & 255).with_bounds(min_val=LEAST, max_val=-(-CHUNKS // U))
            st = (entry >> 18).with_bounds(min_val=0, max_val=TILES * -(-CHUNKS // U))
            return lo, nb, st

        def settle(eng, name):
            eng.sem_inc(sem(name), 1)

        def by_twos(q, start, end):
            return q.with_bounds(min_val=start, max_val=end - 2 + (end - start) % 2)

        def first_chunk(lo, i):
            return (lo + i * U).with_bounds(min_val=0, max_val=CP - U)

        def is_general(eng):
            return eng.value_load(flag_i[0:1, 0:1], min_val=0, max_val=1)

        def general_rows(dve, v, general):
            def call(n):
                with dve.If(general):
                    if n == 0:
                        dve.wait_ge(sem("g_edges_in"), 96)
                        v.tensor_copy(g_dst[:, :], g_dst_i[:, :])
                        v.tensor_scalar(g_typ[:, :], g_typ_i[:, :], 0.0, float(NTYPE - 1), ALU.max, ALU.min).then_inc(sem("g_start"), 1)
                    else:
                        dve.wait_ge(sem("g_copied"), n)
                        v.memset(flag[:, 2:3], 0.0).then_inc(sem("g_start"), 1)
                    dve.wait_ge(sem("g_start"), n + 1)
                    with dve.Fori(0, CHUNKS) as c:
                        dve.wait_ge(sem("g_used"), c + n * CHUNKS)
                        v.tensor_scalar(g_onehot[:, :], g_iota[:, :], g_dst[:, ds(c, 1)], None, ALU.is_equal).then_inc(sem("g_onehot_set"), 1)
                        if n == 0:
                            v.tensor_scalar(g_rows[:, 0:NTYPE], g_iota[:, 0:NTYPE], g_typ[:, ds(c, 1)], None, ALU.is_equal).then_inc(sem("g_types_set"), 1)
                        else:
                            v.tensor_copy(g_idx[:, :], g_src[:, ds(c, 1)]).then_inc(sem("g_idx_set"), 1)
                with dve.Else():
                    dve.nop()
            return call

        block = ctx.enter_context(nc.Block())

        def is_general_after_flag(eng):
            eng.wait_ge(sem("flag_set"), 1)
            return is_general(eng)

        @block.sync
        def _(sp):
            sp.wait_ge(sem("pads_set"), 1)
            for name, ti, m, t in (("dst_in", raw_dst, dst_c, dst_t), ("src_in", raw_src, src_c, src_t),
                                   ("typ_in", raw_typ, typ_c, typ_t)):
                sp.dma_start(ti[:, 0:FULL], m).then_inc(sem(name), 16)
                sp.dma_start(ti[0:TAIL, FULL:FULL + 1], t).then_inc(sem(name), 16)
            sp.dma_start(first_i[:, 0:FULL], dst_c[0:1, :].partition_broadcast(TILES)).then_inc(sem("ends_in"), 16)
            sp.dma_start(first_i[:, FULL:CHUNKS], dst_t[0:1, :].partition_broadcast(TILES)).then_inc(sem("ends_in"), 16)
            sp.dma_start(last_i[:, 0:FULL], dst_c[P - 1:P, :].partition_broadcast(TILES)).then_inc(sem("ends_in"), 16)
            for to, of in weights:
                sp.dma_start(to, of).then_inc(sem("weights_in"), 16)
            sp.wait_ge(sem("tiles_summed"), TILES)
            for c in range(NC):
                sp.dma_start(xstage[:, 4 * c:4 * c + 4, :],
                             x[512 * c:512 * c + 512, :].rearrange("(t p) f -> p t f", p=P)).then_inc(sem(f"x_in{c}"), 16)
            sp.dma_start(xstage[0:LAST, TILES - 1, :], x[(TILES - 1) * P:N, :]).then_inc(sem(f"x_in{NC}"), 16)

            general = is_general_after_flag(sp)
            with sp.If(general):
                sp.wait_ge(sem("g_pads_set"), 1)
                for ti, m, t in ((g_dst_i, dst_c, dst_t), (g_src, src_c, src_t), (g_typ_i, typ_c, typ_t)):
                    sp.dma_start(ti[:, 0:FULL], m).then_inc(sem("g_edges_in"), 16)
                    sp.dma_start(ti[0:TAIL, FULL:FULL + 1], t).then_inc(sem("g_edges_in"), 16)
            with sp.Else():
                sp.nop()

            def pass1(q, w, cols, rows):
                if not isinstance(q, int) or q > 0:
                    sp.wait_ge(sem("p1_y"), q)
                sp.dma_start(slot[2][:, 0:cols], xT[:, ds(q * 512, cols)]).then_inc(sem("p1_xT_in"), 16)
                sp.wait_ge(sem("p1_x1"), q + 1)
                if rows == P:
                    sp.dma_start(x1_dram[ds(q * 512, 512), :].rearrange("(t p) f -> p t f", p=P),
                                 slot[5][:, :].rearrange("p (t f) -> p t f", f=F)).then_inc(sem("p1_x1_out"), 16)
                else:
                    sp.dma_start(x1_dram[ds(q * 512, LASTW), :], slot[5][0:LASTW, 0:F]).then_inc(sem("p1_x1_out"), 16)

            sp.wait_ge(sem("x_split"), NC + 1)
            with sp.Fori(0, NC) as q:
                pass1(q, 512, 512, P)
            pass1(NC, LASTW, LAST, LASTW)

            sp.wait_ge(sem("p1_x1_out"), 16 * (NC + 1))

            def rows_dma(dram, sl, q, last, store, name):
                if last:
                    at, tile_rows = dram[ds(q * 512, LASTW), :], sl[0:LASTW, 0:F]
                else:
                    at = dram[ds(q * 512, 512), :].rearrange("(t p) f -> p t f", p=P)
                    tile_rows = sl[:, :].rearrange("p (t f) -> p t f", f=F)
                to, of = (at, tile_rows) if store else (tile_rows, at)
                sp.dma_start(to, of).then_inc(sem(name), 16)

            def pass2_store(q, last):
                sp.wait_ge(sem("p2_yf"), q + 1)
                rows_dma(y_dram, slot[4], q, last, True, "p2_y_out")
                sp.wait_ge(sem("p2_res"), q + 1)
                rows_dma(res_dram, slot[5], q, last, True, "p2_res_out")

            sp.wait_ge(sem("p1_done"), 1)
            rows_dma(x1_dram, slot[2], 0, False, False, "p2_x1_in")
            with sp.Fori(1, NC) as q:
                sp.wait_ge(sem("p2_x1T"), q)
                rows_dma(x1_dram, slot[2], q, False, False, "p2_x1_in")
                pass2_store(q - 1, False)
            sp.wait_ge(sem("p2_x1T"), NC)
            rows_dma(x1_dram, slot[2], NC, True, False, "p2_x1_in")
            pass2_store(NC - 1, False)
            pass2_store(NC, True)
            sp.wait_ge(sem("p2_res_out"), 16 * (NC + 1))
            sp.wait_ge(sem("p2_y_out"), 16 * (NC + 1))

            def rows_in(q, par, last=False):
                if not isinstance(q, int) or q >= 2:
                    sp.wait_ge(sem("p3_sum"), 3 * (q - 1))
                rows_dma(res_dram, slot[par], q, last, False, f"p3_in{par}")
                rows_dma(x1_dram, slot[2 + par], q, last, False, f"p3_in{par}")

            def rows_out(q, par):
                sp.wait_ge(sem("p3_out"), q + 1)
                rows_dma(out, slot[6 + par], q, False, True, f"p3_stored{par}")

            sp.wait_ge(sem("p2_done"), 1)
            rows_in(0, 0)
            rows_in(1, 1)
            with sp.Fori(0, NC - 2, 2) as q:
                q = by_twos(q, 0, NC - 2)
                rows_in(q + 2, 0)
                rows_out(q, 0)
                rows_in(q + 3, 1)
                rows_out(q + 1, 1)
            rows_in(NC, 0, last=True)
            rows_out(NC - 2, 0)
            rows_out(NC - 1, 1)
            sp.wait_ge(sem("p3_out"), NC + 1)
            sp.dma_start(out[NC * 512:N, :], slot[6][0:LAST, 0:F]).then_inc(sem("p3_stored0"), 16)
            sp.wait_ge(sem("p3_stored0"), 16 * (NC // 2 + 1))
            sp.wait_ge(sem("p3_stored1"), 16 * (NC // 2))

        @block.gpsimd
        def _(pool):
            g = nc.gpsimd
            g.memset(raw_dst[:, FULL:CP], PAD_DST)
            g.memset(raw_src[:, FULL:CP], 0)
            g.memset(raw_typ[:, FULL:CP], 0).then_inc(sem("pads_set"), 1)
            g.iota(iota_h[:, :], pattern=[[1, SPAN]], base=0, channel_multiplier=0, allow_small_or_imprecise_dtypes=True)
            g.iota(tile_off[:, :], pattern=[[P, TILES]], base=-CENTER, channel_multiplier=0, allow_small_or_imprecise_dtypes=True)
            g.iota(thr[:, :], pattern=[[P, 2]], base=0, channel_multiplier=P, allow_small_or_imprecise_dtypes=True)
            g.memset(zero[:, :], 0.0)
            g.memset(ones[:, :], 1.0)
            g.memset(eps[:, :], 1e-5)
            g.memset(Cn[:, TILES:, :], 0.0)
            g.memset(before[:, :], 1.0)
            g.memset(ident[:, :], 0.0).then_inc(sem("filled"), 1)
            pool.wait_ge(sem("filled"), 1)
            g.affine_select(out=before[:, :], in_=before[:, :], compare_op=ALU.is_gt, fill=0.0,
                            base=0, pattern=[[1, TILES]], channel_multiplier=-1)
            g.affine_select(out=ident[:, :], in_=ident[:, :], compare_op=ALU.not_equal, fill=1.0,
                            base=0, pattern=[[-1, P]], channel_multiplier=1).then_inc(sem("consts"), 1)

            pool.wait_ge(sem("entries_set"), 1)
            pool.sem_inc(sem("diff_set"), 1)
            with pool.Fori(0, TILES) as t:
                lo, nb, st = tile_entry(pool, t)
                pool.wait_ge(sem("diff_set"), st * 2 + 1)
                g.tensor_tensor(iota_t[:, :], iota_h[:, 0:P], tile_off[:, ds(t, 1)].to_broadcast([P, P]), ALU.add).then_inc(sem("iota_t_set"), 1)
                pool.wait_ge(sem("iota_t_set"), t + 1)
                settle(pool, "pool_settled")
                with pool.Fori(0, nb) as i:
                    c0 = first_chunk(lo, i)
                    k = st + i
                    for h in range(2):
                        half = slice(h * V, h * V + V)
                        pool.wait_ge(sem("dist_set"), k * 2 + (h + 1))
                        g.tensor_tensor(diff[:, half, :], iota_t[:, :].unsqueeze(1).to_broadcast([P, V, P]),
                                        dst_f[:, ds(c0 + h * V, V)].unsqueeze(2).to_broadcast([P, V, P]), ALU.subtract).then_inc(sem("diff_set"), 1)

            pool.wait_ge(sem("tiles_summed"), TILES)
            g.memset(xp[:, TILES - 1, :, :], 0.0).then_inc(sem("xp_zeroed"), 1)
            pool.wait_ge(sem("digits_stored"), (TILES + 1) * DIGITS)
            g.memset(x1p[:, TILES - 1, :, :], 0.0).then_inc(sem("x1p_zeroed"), 1)

            general = is_general_after_flag(pool)
            with pool.If(general):
                pool.wait_ge(sem("early_sums"), 1)
                g.memset(g_dst_i[:, FULL:CP], PAD_DST)
                g.memset(g_src[:, FULL:CP], 0)
                g.memset(g_typ_i[:, FULL:CP], 0)
                g.memset(g_sum[:, TILES:, :], 0.0)
                g.iota(g_iota[:, :], pattern=[[1, TILES * P]], base=0, channel_multiplier=0,
                       allow_small_or_imprecise_dtypes=True).then_inc(sem("g_pads_set"), 1)
            with pool.Else():
                pool.nop()

            def gather(call, table_dram):
                with pool.If(general):
                    with pool.Fori(0, CHUNKS) as c:
                        pool.wait_ge(sem("g_idx_set"), c + (call - 1) * CHUNKS + 1)
                        settle(pool, "pool_settled")
                        g.indirect_dma_start(g_rows[:, :], None, table_dram,
                                             bass.IndirectOffsetOnAxis(ap=g_idx[:, 0:1].bitcast(u32), axis=0)).then_inc(sem("g_rows_in"), 16)
                with pool.Else():
                    pool.nop()

            def low_parts(name, target, q, last):
                rows, k = (LASTW, 1) if last else (P, 4)
                full = slot[5 if name == "p1" else 4][0:rows, 0:k * F].rearrange("p (t f) -> p t f", f=F)
                rest = slot[6 if name == "p1" else 7][0:rows, 0:k * F].rearrange("p (t f) -> p t f", f=F)
                hi, mid, low = (target[0:rows, ds(4 * q, k), n, :] for n in range(PARTS))
                pool.wait_ge(sem(f"{name}_hi"), q + 1)
                g.tensor_tensor(rest, full, hi, ALU.subtract).then_inc(sem(f"{name}_rest"), 1)
                pool.wait_ge(sem(f"{name}_mid"), q + 1)
                g.tensor_tensor(low, rest, mid, ALU.subtract).then_inc(sem(f"{name}_low"), 1)

            gather(1, x)
            with pool.Fori(0, NC) as q:
                low_parts("p1", x1p, q, False)
            low_parts("p1", x1p, NC, True)
            with pool.If(general):
                pool.wait_ge(sem("p1_x1_out"), 16 * (NC + 1))
            with pool.Else():
                pool.nop()
            gather(2, x1_dram)
            with pool.Fori(0, NC) as q:
                low_parts("p2", xp, q, False)
            low_parts("p2", xp, NC, True)
            with pool.If(general):
                pool.wait_ge(sem("p2_y_out"), 16 * (NC + 1))
            with pool.Else():
                pool.nop()
            gather(3, y_dram)

        @block.vector
        def _(dve):
            v = nc.vector
            chain = [0]

            def then(ins):
                chain[0] += 1
                ins.then_inc(sem("dve_chain"), 1)
                dve.wait_ge(sem("dve_chain"), chain[0])

            dve.wait_ge(sem("ends_in"), 48)
            dve.wait_ge(sem("consts"), 1)
            then(v.tensor_scalar(passed[:, :], first_i[:, :], thr[:, 1:2], None, ALU.is_lt, ALU.add, accum_out=tcol[:, 0:1]))
            then(v.tensor_scalar(passed[:, 0:FULL], last_i[:, 0:FULL], thr[:, 0:1], None, ALU.is_lt, ALU.add, accum_out=tcol[:, 1:2]))
            then(v.tensor_scalar(tcol[:, 2:3], tcol[:, 1:2], float(CHUNKS - 1), None, ALU.min))
            then(v.tensor_tensor(tcol[:, 3:4], tcol[:, 0:1], tcol[:, 2:3], ALU.subtract))
            then(v.tensor_scalar(tcol[:, 4:5], tcol[:, 3:4], float((LEAST - 1) * U + 1), float(U - 1), ALU.max, ALU.add))
            then(v.tensor_scalar(tcol[:, 6:7], tcol[:, 4:5], float(DIVIDE), None, ALU.mult))
            then(v.tensor_copy(tcol_i[:, 0:1], tcol[:, 6:7]))
            then(v.tensor_scalar(tcol_i[:, 1:2], tcol_i[:, 0:1], 16, None, ALU.logical_shift_right))
            v.tensor_copy(tcol[:, 5:6], tcol_i[:, 1:2]).then_inc(sem("tile_columns"), 1)
            dve.wait_ge(sem("table_rows"), 1)
            then(v.tensor_copy(table[:, :].rearrange("a (n t) -> a n t", n=3)[:, :, 0:TILES],
                               PS[0:1, 6, 0:96].rearrange("a (n t) -> a n t", n=3)[:, :, 0:TILES]))
            v.tensor_scalar(shifted[:, 0:TILES], table[:, 32:32 + TILES], 10, None, ALU.logical_shift_left)
            then(v.tensor_scalar(shifted[:, 32:32 + TILES], table[:, 64:64 + TILES], 18, None, ALU.logical_shift_left))
            then(v.tensor_tensor(shifted[:, 0:TILES], shifted[:, 0:TILES], shifted[:, 32:32 + TILES], ALU.bitwise_or))
            v.tensor_tensor(entries[:, 0:TILES], table[:, 0:TILES], shifted[:, 0:TILES], ALU.bitwise_or)

            dve.wait_ge(sem("dst_in"), 32)
            v.tensor_scalar(dst_f[:, :], raw_dst[:, :], float(-CENTER), None, ALU.add).then_inc(sem("entries_set"), 1)
            dve.wait_ge(sem("src_in"), 32)
            then(v.tensor_scalar(src_tile[:, :], raw_src[:, :], 7, None, ALU.logical_shift_right))
            then(v.tensor_scalar(src_tile[:, :], src_tile[:, :], float(DIGIT_OF_TILE), None, ALU.mult))
            then(v.tensor_scalar(src_digit[:, :], src_tile[:, :], 6, None, ALU.logical_shift_right))
            v.tensor_scalar(src_w[:, :].bitcast(i32), src_digit[:, :], float(4 << 23), float(127 << 23), ALU.mult, ALU.add)
            v.scalar_tensor_tensor(out=src_col[:, :], in0=src_digit[:, :], scalar=float(-SPAN), in1=raw_src[:, :], op0=ALU.mult, op1=ALU.add)
            dve.wait_ge(sem("weights_in"), 16 * len(weights))
            v.tensor_tensor(rz_b[:, :], gate_b[:, 0:2], gate_b[:, 3:5], ALU.add)
            v.tensor_tensor(emb_b[:, :], emb_s[:, :], bmsg_b[:, :], ALU.add)
            dve.wait_ge(sem("typ_in"), 32)
            for k in range(NTYPE):
                if k == 0:
                    ins = v.tensor_scalar(T[:, :, k], raw_typ[:, :], 0.0, None, ALU.is_le)
                elif k == NTYPE - 1:
                    ins = v.tensor_scalar(T[:, :, k], raw_typ[:, :], float(k), None, ALU.is_ge)
                else:
                    ins = v.tensor_scalar(T[:, :, k], raw_typ[:, :], float(k), None, ALU.is_equal)
            ins.then_inc(sem("edges_set"), 1)
            dve.wait_ge(sem("edges_set"), 1)

            def take_digits(t, some):
                dve.wait_ge(sem("packedT_in"), t + 1)
                for f in some:
                    dve.wait_ge(sem("digits_stored"), t * DIGITS + (f + 1))
                    v.tensor_scalar(digits[:, f, :], packedT[:, :], 4 * f, 15, ALU.logical_shift_right,
                                    ALU.bitwise_and).then_inc(sem("digits_taken"), 1)

            def source_batch(c0, k, between_halves=lambda: None):
                for u in range(U):
                    if u == V:
                        between_halves()
                    if u % V == 0:
                        dve.wait_ge(sem("items_done"), k * U + (u + V))
                    v.tensor_scalar(S[:, u, :], iota_h[:, :], src_col[:, ds(c0 + u, 1)], src_w[:, ds(c0 + u, 1)],
                                    ALU.is_equal, ALU.mult).then_inc(sem("S_set"), 1)

            def source_rows(t, between):
                lo, nb, st = tile_entry(dve, t)
                for i in range(LEAST - 1):
                    source_batch(first_chunk(lo, i), st + i, lambda: between(i))
                between(LEAST - 1)
                with dve.Fori(LEAST - 1, nb) as i:
                    source_batch(first_chunk(lo, i), st + i)

            for t in range(LAG):
                source_rows(t, lambda i: None)
            with dve.Fori(LAG, TILES, 2) as t:
                t = by_twos(t, LAG, TILES)
                for n in range(2):
                    source_rows(t + n, lambda i: take_digits(t + n - LAG, SHARES[i]))

            def x_rest(c):
                dve.wait_ge(sem("x_hi"), c + 1)
                rows, k = (P, 4) if c < NC else (LAST, 1)
                staged = xstage[0:rows, 4 * c:4 * c + k, :]
                v.tensor_tensor(staged, staged, xp[0:rows, 4 * c:4 * c + k, 0, :], ALU.subtract).then_inc(sem("x_rest"), 1)

            x_rest(0)
            for c in range(NC + 1):
                rows, k = (P, 4) if c < NC else (LAST, 1)
                if c < NC:
                    x_rest(c + 1)
                else:
                    dve.wait_ge(sem("xp_zeroed"), 1)
                rest = xstage[0:rows, 4 * c:4 * c + k, :]
                mid, low = (xp[0:rows, 4 * c:4 * c + k, n, :] for n in (1, 2))
                dve.wait_ge(sem("x_rest"), c + 1)
                v.tensor_copy(mid, rest).then_inc(sem("x_mid"), 1)
                dve.wait_ge(sem("x_mid"), c + 1)
                v.tensor_tensor(low, rest, mid, ALU.subtract).then_inc(sem("x_split"), 1)

            for t in range(TILES - LAG, TILES):
                take_digits(t, range(DIGITS))

            dve.wait_ge(sem("digits_stored"), (TILES + 1) * DIGITS)
            v.tensor_reduce(verdict[:, :], count[:, :, :], AX.XY, ALU.add).then_inc(sem("verdict_set"), 1)
            dve.wait_ge(sem("verdict_sum"), 1)
            then(v.tensor_scalar(flag[:, 0:1], PS[0:1, 7, 0:1], float(E), None, ALU.not_equal))
            v.tensor_copy(flag_i[:, 0:1], flag[:, 0:1]).then_inc(sem("flag_set"), 1)

            general = is_general_after_flag(dve)
            calls = general_rows(dve, v, general)
            calls(0)
            calls(1)

            dve.wait_ge(sem("types_ready"), 1)
            then(v.tensor_reduce(ideg[:, :], Cn[:, 0:TILES, :], AX.X, ALU.add))
            then(v.tensor_scalar(ideg[:, :], ideg[:, :], 1.0, None, ALU.max))
            then(v.reciprocal(ideg[:, :], ideg[:, :]))

            def inverse_degrees(q, w):
                if not isinstance(q, int) or q > 0:
                    dve.wait_ge(sem("p2_deg_sum"), q)
                    dve.wait_ge(sem("p2_low"), q - 1)
                for n in range(-(-w // P)):
                    ins = v.tensor_copy(slot[7][:, n * P:(n + 1) * P], ideg[:, ds(4 * q + n, 1)].to_broadcast([P, P]))
                ins.then_inc(sem("p2_deg_rows"), 1)

            def pass1(q, w, last):
                rows, k = (LASTW, 1) if last else (P, 4)
                sT, mT, x_, rr, zz, tt, nn = (slot[n][:, 0:w] for n in range(7))
                dve.wait_ge(sem("p1_m_sum"), q + 1)
                v.tensor_copy(mT, PS[:, 3, 0:w]).then_inc(sem("p1_m"), 1)
                dve.wait_ge(sem("p1_gates"), q + 1)
                dve.wait_ge(sem("p1_r"), q + 1)
                dve.wait_ge(sem("p1_x1_out"), 16 * q)
                dve.wait_ge(sem("p1_low"), q)
                v.scalar_tensor_tensor(out=tt, in0=PS[:, 7, 0:w], scalar=gate_b[:, 5:6], in1=rr, op0=ALU.add, op1=ALU.mult).then_inc(sem("p1_t"), 1)
                dve.wait_ge(sem("p1_t"), 2 * q + 1)
                v.tensor_tensor(tt, tt, PS[:, 6, 0:w], ALU.add).then_inc(sem("p1_t"), 1)
                dve.wait_ge(sem("p1_n"), q + 1)
                v.tensor_tensor(rr, x_, nn, ALU.subtract).then_inc(sem("p1_e"), 1)
                v.tensor_tensor(tt, x_, nn, ALU.add).then_inc(sem("p1_e"), 1)
                dve.wait_ge(sem("p1_e"), 3 * q + 1)
                v.tensor_tensor(zz, zz, rr, ALU.mult).then_inc(sem("p1_e"), 1)
                dve.wait_ge(sem("p1_e"), 3 * q + 3)
                v.tensor_tensor(zz, zz, tt, ALU.add).then_inc(sem("p1_y"), 1)
                dve.wait_ge(sem("p1_yT"), q + 1)
                norm("p1", q, rows, k, lambda n: PS[0:rows, 3, n * F:(n + 1) * F], slot[5], "p1_x1")

            def norm(name, q, rows, k, row_of, to, done, par=None):
                for n in range(k):
                    ins = v.bn_stats(stats[0:rows, n, :], row_of(n))
                ins.then_inc(sem(f"{name}_norm"), 1)
                dve.wait_ge(sem(f"{name}_norm"), 3 * q + 1)
                dve.wait_ge(sem(done), q)
                settle(dve, "dve_settled")
                for n in range(k):
                    ins = v.bn_aggr(meanvar[0:rows, n, :], stats[0:rows, n, :])
                ins.then_inc(sem(f"{name}_norm"), 1)
                dve.wait_ge(sem(f"{name}_sd"), q + 1)
                v.reciprocal(rstd[0:rows, 0:k], sd[0:rows, 0:k]).then_inc(sem(f"{name}_norm"), 1)
                dve.wait_ge(sem(f"{name}_norm"), 3 * q + 3)
                for n in range(k):
                    ins = v.tensor_scalar(to[0:rows, n * F:(n + 1) * F], row_of(n), meanvar[0:rows, n, 0:1],
                                          rstd[0:rows, n:n + 1], ALU.subtract, ALU.mult)
                ins.then_inc(sem(done), 1)

            with dve.Fori(0, NC) as q:
                pass1(q, 512, False)
            pass1(NC, LASTW, True)
            inverse_degrees(0, 512)
            dve.wait_ge(sem("p1_x1"), NC + 1)
            dve.wait_ge(sem("p1_hi"), NC + 1)
            dve.wait_ge(sem("p1_low"), NC + 1)
            dve.wait_ge(sem("p1_yT"), NC + 1)
            v.memset(stats[:, 0, 0:1], 0.0).then_inc(sem("p1_done"), 1)
            calls(2)

            def mean_neighbours(q, w):
                nT = slot[0][:, 0:w]
                dve.wait_ge(sem("p2_deg_sum"), q + 1)
                v.tensor_copy(nT, PS[:, 5, 0:w]).then_inc(sem("p2_deg"), 1)
                dve.wait_ge(sem("p2_deg"), q + 1)
                dve.wait_ge(sem("p2_agg"), q + 1)
                v.tensor_tensor(nT, nT, PS[:, 1 if isinstance(q, int) and q == 0 else 0, 0:w], ALU.mult).then_inc(sem("p2_n"), 1)

            def residual(q, last):
                rows, k = (LASTW, 1) if last else (P, 4)
                dve.wait_ge(sem("p2_y_sum"), q + 1)
                dve.wait_ge(sem("p2_res_out"), 16 * q)
                v.tensor_tensor(slot[5][0:rows, 0:k * F].rearrange("p (t f) -> p t f", f=F),
                                PS[0:rows, 4, 0:k * F].rearrange("p (t f) -> p t f", f=F),
                                b2_b[0:rows, :].unsqueeze(1).to_broadcast([rows, k, F]), ALU.add).then_inc(sem("p2_res"), 1)

            mean_neighbours(0, 512)
            with dve.Fori(1, NC) as q:
                inverse_degrees(q, 512)
                mean_neighbours(q, 512)
                residual(q - 1, False)
            inverse_degrees(NC, LASTW)
            mean_neighbours(NC, LASTW)
            residual(NC - 1, False)
            residual(NC, True)
            dve.wait_ge(sem("p2_low"), NC + 1)
            dve.wait_ge(sem("p2_res"), NC + 1)
            dve.wait_ge(sem("p2_y_out"), 16 * (NC + 1))
            dve.wait_ge(sem("p2_res_out"), 16 * (NC + 1))
            v.memset(stats[:, 0, 0:1], 0.0).then_inc(sem("p2_done"), 1)
            calls(3)

            def pass3(q, par, last):
                rows, k = (LAST, 1) if last else (P, 4)
                total = slot[4 + par][0:rows, 0:k * F]
                dve.wait_ge(sem("p3_agg"), q + 1)
                dve.wait_ge(sem("p3_out"), q)
                v.tensor_reduce(total.rearrange("p (t f) -> p t f", f=F),
                                PS[0:rows, 4 * par:4 * par + k, 0:PARTS * F].rearrange("p t (s f) -> p t f s", s=PARTS),
                                AX.X, ALU.add).then_inc(sem("p3_sum"), 1)
                dve.wait_ge(sem("p3_sum"), 3 * q + 1)
                dve.wait_ge(sem(f"p3_in{par}"), (q - par) * 16 + 32)
                for n in range(k):
                    cols = slice(n * F, (n + 1) * F)
                    ins = v.scalar_tensor_tensor(out=total[:, cols], in0=total[:, cols], scalar=ideg[0:rows, ds(4 * q + n, 1)],
                                                 in1=slot[par][0:rows, cols], op0=ALU.mult, op1=ALU.add)
                ins.then_inc(sem("p3_sum"), 1)
                dve.wait_ge(sem("p3_sum"), 3 * q + 2)
                v.tensor_tensor(total, total, slot[2 + par][0:rows, 0:k * F], ALU.add).then_inc(sem("p3_sum"), 1)
                dve.wait_ge(sem("p3_sum"), 3 * q + 3)
                dve.wait_ge(sem(f"p3_stored{par}"), (q - par) * 8)
                norm("p3", q, rows, k, lambda n: total[:, n * F:(n + 1) * F], slot[6 + par], "p3_out")

            with dve.Fori(0, NC, 2) as q:
                q = by_twos(q, 0, NC)
                pass3(q, 0, False)
                pass3(q + 1, 1, False)
            pass3(NC, 0, True)

        @block.tensor
        def _(pe):
            mm = nc.tensor.matmul

            pe.wait_ge(sem("consts"), 1)
            pe.wait_ge(sem("tile_columns"), 1)
            mm(PS[0:1, 6, 0:TILES], tcol[:, 2:3], ident[0:TILES, 0:TILES], start=True, stop=True)
            mm(PS[0:1, 6, 32:32 + TILES], tcol[:, 5:6], ident[0:TILES, 0:TILES], start=True, stop=True)
            mm(PS[0:1, 6, 64:64 + TILES], tcol[:, 5:6], before[:, :], start=True, stop=True).then_inc(sem("table_rows"), 1)
            mm(PS[:, 7, 0:16], zero[:, :], zero[:, 0:16], start=True, stop=True).then_inc(sem("items_done"), U)

            zeros = zero[:, 0:1].to_broadcast([P, 512])
            zeros_b = zero[:, 0:1].to_broadcast([P, P + NTYPE])

            def count_tile(t, par):
                lo, nb, st = tile_entry(pe, t)
                if not isinstance(t, int) or t >= 2:
                    pe.wait_ge(sem("packed_out"), t - 1)
                mm(PS[:, 2 * par, :], zero[:, :], zeros, start=True, stop=False)
                mm(PS[:, 2 * par + 1, 0:P + NTYPE], zero[:, :], zeros_b, start=True, stop=False)
                with pe.Fori(0, nb) as i:
                    k = st + i
                    c0 = first_chunk(lo, i)
                    for u in range(U):
                        if u % V == 0:
                            pe.wait_ge(sem("D_set"), k * 2 + (u // V + 3))
                        if u % 2 == 0:
                            pe.wait_ge(sem("S_set"), k * U + (u + 2))
                        rows = D[:, u, :]
                        mm(PS[:, 2 * par, :], rows, S[:, u, 0:512], start=False, stop=False)
                        mm(PS[:, 2 * par + 1, 0:P], rows, S[:, u, 512:SPAN], start=False, stop=False)
                        mm(PS[:, 2 * par + 1, P:P + NTYPE], rows, T[:, ds(c0 + u, 1), :], start=False, stop=False).then_inc(sem("items_done"), 1)
                mm(PS[:, 2 * par, :], zero[:, :], zeros, start=False, stop=True)
                mm(PS[:, 2 * par + 1, 0:P + NTYPE], zero[:, :], zeros_b, start=False, stop=True).then_inc(sem("tiles_summed"), 1)

            def turn_tile(t):
                pe.wait_ge(sem("packed_out"), t + 1)
                if not isinstance(t, int) or t > 0:
                    pe.wait_ge(sem("packedT_in"), t)
                for g in range(GROUPS):
                    ins = nc.tensor.transpose(PS[:, 4 + g // 4, (g % 4) * P:(g % 4 + 1) * P], packed[:, g * P:(g + 1) * P], ident[:, :])
                ins.then_inc(sem("turned"), 1)

            pe.wait_ge(sem("entries_set"), 1)
            count_tile(0, 0)
            with pe.Fori(1, TILES, 2) as t:
                t = by_twos(t, 1, TILES)
                count_tile(t, 1)
                turn_tile(t - 1)
                count_tile(t + 1, 0)
                turn_tile(t)

            def early_share(share):
                for j in range(CUTS["early"][share], CUTS["early"][share + 1]):
                    if j % 4 == 0:
                        pe.wait_ge(sem("x_split"), j // 4 + 1)
                    for s in range(PARTS):
                        ins = mm(PS[:, 0, :], xp[:, j, s, :], AT[:, j, 0:512],
                                 start=(j == 0 and s == 0), stop=(j == TILES - 1 and s == PARTS - 1))
                return ins

            pe.wait_ge(sem("packed_out"), TILES)
            pe.wait_ge(sem("digits_stored"), (4 + 1) * DIGITS)
            early_share(0)
            turn_tile(TILES - 1)
            early_share(1)
            pe.wait_ge(sem("verdict_set"), 1)
            mm(PS[0:1, 7, 0:1], ones[:, 0:1], verdict[:, :], start=True, stop=True).then_inc(sem("verdict_sum"), 1)
            early_share(2).then_inc(sem("early_sums"), 1)
            general = is_general_after_flag(pe)

            def general_sum(n, width):
                with pe.If(general):
                    per = 4 * F // width * width if n else 512
                    banks = 1 if n == 0 else 7
                    pe.wait_ge(sem("g_start"), n + 1)
                    for b in range(banks):
                        mm(PS[:, b, :], zero[:, :], zeros, start=True, stop=False)
                    with pe.Fori(0, CHUNKS) as c:
                        pe.wait_ge(sem("g_onehot_set"), c + n * CHUNKS + 1)
                        if n == 0:
                            pe.wait_ge(sem("g_types_set"), c + 1)
                        else:
                            pe.wait_ge(sem("g_rows_in"), (c + (n - 1) * CHUNKS) * 16 + 16)
                        for t in range(TILES):
                            where = PS[:, 0, t * NTYPE:(t + 1) * NTYPE] if n == 0 else PS[:, t // 4, (t % 4) * F:(t % 4 + 1) * F]
                            ins = mm(where, g_onehot[:, t * P:(t + 1) * P], g_rows[:, 0:width], start=False, stop=False)
                        ins.then_inc(sem("g_used"), 1)
                    for b in range(banks):
                        ins = mm(PS[:, b, :], zero[:, :], zeros, start=False, stop=True)
                    ins.then_inc(sem("g_summed"), 1)
                    pe.wait_ge(sem("g_copied"), n + 1)
                with pe.Else():
                    pe.nop()

            general_sum(0, NTYPE)
            general_sum(1, F)

            def agg_staged(name, q, w, bank=0):
                pe.wait_ge(sem(f"{name}_sum_staged"), q + 1)
                for n in range(-(-w // P)):
                    rows = min(P, w - n * P)
                    ins = nc.tensor.transpose(PS[:, bank, n * P:n * P + rows], g_stage[0:rows, n, :], ident[0:rows, 0:rows])
                ins.then_inc(sem(f"{name}_agg"), 1)

            def agg_share(name, parts, q, w, share):
                with pe.If(general):
                    if share == 2:
                        agg_staged(name, q, w)
                    else:
                        pe.nop()
                with pe.Else():
                    for j in range(CUTS[name][share], CUTS[name][share + 1]):
                        for s in range(PARTS):
                            ins = mm(PS[:, 0, 0:w], parts[:, j, s, :], AT[:, j, ds(q * 512, w)],
                                     start=(j == 0 and s == 0), stop=(j == TILES - 1 and s == PARTS - 1))
                    if share == 2:
                        ins.then_inc(sem(f"{name}_agg"), 1)
                pe.nop()

            def turn_types(name, q, w):
                pe.wait_ge(sem(f"{name}_types_staged"), q + 1)
                for n in range(-(-w // P)):
                    rows = min(P, w - n * P)
                    ins = nc.tensor.transpose(PS[0:NTYPE, 2, n * P:n * P + rows], c_stage[0:rows, n, :], ident[0:rows, 0:rows])
                ins.then_inc(sem(f"{name}_typeT"), 1)

            def messages(q, w):
                pe.wait_ge(sem("p1_s"), q + 1)
                pe.wait_ge(sem("p1_c"), q + 1)
                pe.wait_ge(sem("p1_x1"), q)
                mm(PS[:, 3, 0:w], wmsg_s[:, :], slot[0][:, 0:w], start=True, stop=False)
                mm(PS[:, 3, 0:w], emb_b[:, :], slot[7][0:NTYPE, 0:w], start=False, stop=True).then_inc(sem("p1_m_sum"), 1)

            def gates(q, w):
                pe.wait_ge(sem("p1_m"), q + 1)
                pe.wait_ge(sem("p1_xT_in"), 16 * (q + 1))
                m, x_ = slot[1][:, 0:w], slot[2][:, 0:w]
                for g in range(2):
                    mm(PS[:, 4 + g, 0:w], wih_s[:, g, :], m, start=True, stop=False)
                    mm(PS[:, 4 + g, 0:w], whh_s[:, g, :], x_, start=False, stop=True)
                mm(PS[:, 7, 0:w], whh_s[:, 2, :], x_, start=True, stop=True)
                mm(PS[:, 6, 0:w], wih_s[:, 2, :], m, start=True, stop=True).then_inc(sem("p1_gates"), 1)

            def rows_back(q, w):
                pe.wait_ge(sem("p1_y"), q + 1)
                for n in range(-(-w // P)):
                    rows = min(P, w - n * P)
                    ins = nc.tensor.transpose(PS[0:rows, 3, n * P:(n + 1) * P], slot[4][:, n * P:n * P + rows], ident[:, :])
                ins.then_inc(sem("p1_yT"), 1)

            def agg(name, parts, q, w, between):
                if name == "p1":
                    pe.wait_ge(sem("p1_s"), q)
                elif not isinstance(q, int) or q > 1:
                    pe.wait_ge(sem("p2_n"), q)
                for share in range(3):
                    agg_share(name, parts, q, w, share)
                    between[share]()

            pe.wait_ge(sem("digits_stored"), (TILES + 1) * DIGITS)
            pe.wait_ge(sem("types_ready"), 1)
            turn_types("p1", 0, 512)
            with pe.If(general):
                agg_staged("p1", 0, 512)
            with pe.Else():
                mm(PS[:, 1, 0:16], zero[:, :], zero[:, 0:16], start=True, stop=True).then_inc(sem("p1_agg"), 1)
            pe.nop()

            def p1_step(q, w, wprev):
                agg("p1", xp, q, w, [lambda: messages(q - 1, wprev), lambda: gates(q - 1, wprev),
                                     lambda: rows_back(q - 1, wprev)])
                pe.wait_ge(sem("p1_c"), q)
                turn_types("p1", q, w)

            with pe.Fori(1, NC) as q:
                p1_step(q, 512, 512)
            def p2_first(j0, j1):
                pe.wait_ge(sem("p1_low"), -(-j1 // 4))
                with pe.If(general):
                    pe.nop()
                with pe.Else():
                    for j in range(j0, j1):
                        for s in range(PARTS):
                            mm(PS[:, 1, :], x1p[:, j, s, :], AT[:, j, 0:512], start=(j == 0 and s == 0), stop=False)
                pe.nop()

            def messages_first():
                p2_first(0, 5)
                messages(NC - 1, 512)
                p2_first(5, 6)

            def gates_first():
                gates(NC - 1, 512)
                p2_first(6, 13)

            agg("p1", xp, NC, LASTW, [messages_first, gates_first, lambda: None])
            pe.wait_ge(sem("p1_c"), NC)
            turn_types("p1", NC, LASTW)
            rows_back(NC - 1, 512)
            p2_first(13, 18)
            messages(NC, LASTW)
            p2_first(18, 19)
            gates(NC, LASTW)
            p2_first(19, 20)
            rows_back(NC, LASTW)
            p2_first(20, TILES - 1)

            pe.wait_ge(sem("p1_done"), 1)
            general_sum(2, F)

            def chunk_inputs(q, w):
                bank = 2 if isinstance(q, int) and q == 0 else 1
                if bank == 1:
                    pe.wait_ge(sem("p2_n"), q)
                    pe.wait_ge(sem("p2_x1c"), q)
                pe.wait_ge(sem("p2_x1_in"), 16 * (q + 1))
                for n in range(-(-w // P)):
                    rows = min(P, w - n * P)
                    ins = nc.tensor.transpose(PS[:, bank, n * P:n * P + rows], slot[2][0:rows, n * F:(n + 1) * F], ident[0:rows, 0:rows])
                ins.then_inc(sem("p2_x1T"), 1)

            def degrees(q, w):
                pe.wait_ge(sem("p2_deg_rows"), q + 1)
                if not isinstance(q, int) or q > 0:
                    pe.wait_ge(sem("p2_deg"), q)
                for n in range(-(-w // P)):
                    rows = min(P, w - n * P)
                    ins = nc.tensor.transpose(PS[:, 5, n * P:n * P + rows], slot[7][0:rows, n * P:(n + 1) * P], ident[0:rows, 0:rows])
                ins.then_inc(sem("p2_deg_sum"), 1)

            def hidden(q, w):
                pe.wait_ge(sem("p2_n"), q + 1)
                pe.wait_ge(sem("p2_x1c"), q + 1)
                pe.wait_ge(sem("p2_h"), 2 * q)
                for a in range(2):
                    mm(PS[:, 6 + a, 0:w], ws1[:, a, :], slot[3][:, 0:w], start=True, stop=False)
                    mm(PS[:, 6 + a, 0:w], wn1[:, a, :], slot[0][:, 0:w], start=False, stop=True).then_inc(sem("p2_h_sum"), 1)

            def second(q, w):
                pe.wait_ge(sem("p2_h"), 2 * (q + 1))
                pe.wait_ge(sem("p2_yf"), q)
                pe.wait_ge(sem("p2_res"), q)
                hid = [slot[1], slot[6]]
                for n in range(-(-w // P)):
                    rows = min(P, w - n * P)
                    for bank, wt in ((3, wn2), (4, ws2)):
                        for a in range(2):
                            ins = mm(PS[0:rows, bank, n * F:(n + 1) * F], hid[a][:, n * P:n * P + rows], wt[:, a, :],
                                     start=(a == 0), stop=(a == 1))
                ins.then_inc(sem("p2_y_sum"), 1)

            pe.wait_ge(sem("p1_low"), NC + 1)
            with pe.If(general):
                agg_staged("p2", 0, 512, 1)
            with pe.Else():
                for s in range(PARTS):
                    ins = mm(PS[:, 1, :], x1p[:, TILES - 1, s, :], AT[:, TILES - 1, 0:512], start=False, stop=(s == PARTS - 1))
                ins.then_inc(sem("p2_agg"), 1)
            pe.nop()
            degrees(0, 512)
            chunk_inputs(0, 512)

            def p2_step(q, w):
                def inputs():
                    hidden(q - 1, 512)
                    chunk_inputs(q, w)

                agg("p2", x1p, q, w, [inputs, lambda: degrees(q, w), lambda: second(q - 1, 512)])

            p2_step(1, 512)
            with pe.Fori(2, NC) as q:
                p2_step(q, 512)
            p2_step(NC, LASTW)

            def p3_first(n, j0, j1):
                pe.wait_ge(sem("p2_low"), -(-j1 // 4))
                with pe.If(general):
                    pe.nop()
                with pe.Else():
                    for j in range(j0, j1):
                        mm(PS[:, n, 0:PARTS * F], AT[:, j, n * P:n * P + P], xp[:, j, :, :].rearrange("p s f -> p (s f)"),
                           start=(j == 0), stop=False)
                pe.nop()

            pe.wait_ge(sem("p2_x1c"), NC + 1)
            p3_first(1, 0, 20)
            hidden(NC, LASTW)
            p3_first(2, 0, 20)
            second(NC, LASTW)
            p3_first(0, 0, 20)
            pe.wait_ge(sem("p2_yf"), NC + 1)
            p3_first(3, 0, 20)
            begun = 20

            pe.wait_ge(sem("p2_done"), 1)
            general_sum(3, F)

            def rows_staged(n, rows, q, par, done):
                mm(PS[0:rows, 4 * par + n, 0:F], ident[:, 0:rows], g_sum[:, ds(4 * q + n, 1), :].rearrange("p a f -> p (a f)"), start=True, stop=True)
                ins = mm(PS[0:rows, 4 * par + n, F:PARTS * F], zero[:, 0:rows], zero[:, 0:1].to_broadcast([P, (PARTS - 1) * F]), start=True, stop=True)
                if done:
                    ins.then_inc(sem("p3_agg"), 1)

            def agg_rows(q, par, last):
                if not isinstance(q, int) or q >= 2:
                    pe.wait_ge(sem("p3_out"), q - 1)
                tiles = [(0, LAST)] if last else [(n, P) for n in range(4)]
                with pe.If(general):
                    for n, rows in tiles:
                        rows_staged(n, rows, q, par, n == tiles[-1][0])
                with pe.Else():
                    for n, rows in tiles:
                        for j in range(TILES):
                            ins = mm(PS[0:rows, 4 * par + n, 0:PARTS * F], AT[:, j, ds(q * 512 + n * P, rows)],
                                     xp[:, j, :, :].rearrange("p s f -> p (s f)"), start=(j == 0), stop=(j == TILES - 1))
                    ins.then_inc(sem("p3_agg"), 1)
                pe.nop()

            with pe.If(general):
                for n in range(4):
                    rows_staged(n, P, 0, 0, n == 3)
            with pe.Else():
                for n in range(4):
                    for j in range(begun, TILES):
                        ins = mm(PS[:, n, 0:PARTS * F], AT[:, j, n * P:n * P + P], xp[:, j, :, :].rearrange("p s f -> p (s f)"),
                                 start=False, stop=(j == TILES - 1))
                ins.then_inc(sem("p3_agg"), 1)
            pe.nop()
            agg_rows(1, 1, False)
            with pe.Fori(2, NC, 2) as q:
                q = by_twos(q, 2, NC)
                agg_rows(q, 0, False)
                agg_rows(q + 1, 1, False)
            agg_rows(NC, 0, True)

        @block.scalar
        def _(act):
            a = nc.scalar

            def dest_batch(k):
                for h in range(2):
                    half = slice(h * V, h * V + V)
                    act.wait_ge(sem("D_set"), k * 2 + (h + 1))
                    act.wait_ge(sem("diff_set"), k * 2 + (h + 2))
                    a.activation(dist[:, half, :], diff[:, half, :], ACT.Abs).then_inc(sem("dist_set"), 1)
                for h in range(2):
                    half = slice(h * V, h * V + V)
                    act.wait_ge(sem("items_done"), k * U + V * (h + 1))
                    act.wait_ge(sem("dist_set"), k * 2 + (h + 3))
                    a.activation(D[:, half, :], dist[:, half, :], ACT.Relu, bias=1.0, scale=-1.0).then_inc(sem("D_set"), 1)

            def dest_rows(t, between):
                _, nb, st = tile_entry(act, t)
                for i in range(LEAST - 1):
                    dest_batch(st + i)
                    between(i)
                with act.Fori(LEAST - 1, nb) as i:
                    dest_batch(st + i)
                between(LEAST - 1)

            def packed_out(t, par):
                act.wait_ge(sem("tiles_summed"), t + 1)
                act.wait_ge(sem("turned"), t)
                a.activation(packed[:, 0:512], PS[:, 2 * par, :], ACT.Copy)
                a.activation(packed[:, 512:SPAN], PS[:, 2 * par + 1, 0:P], ACT.Copy)
                a.activation(Cn[:, ds(t, 1), :].rearrange("p a k -> p (a k)"), PS[:, 2 * par + 1, P:P + NTYPE], ACT.Copy).then_inc(sem("packed_out"), 1)

            def packedT_in(t):
                act.wait_ge(sem("turned"), t + 1)
                act.wait_ge(sem("digits_taken"), t * DIGITS)
                a.activation(packedT[:, 0:512], PS[:, 4, :], ACT.Copy)
                a.activation(packedT[:, 512:SPAN], PS[:, 5, 0:P], ACT.Copy).then_inc(sem("packedT_in"), 1)

            def store_digits(t, w, some=range(DIGITS)):
                for f in some:
                    act.wait_ge(sem("digits_taken"), t * DIGITS + f + 1)
                    a.activation(AT[:, GROUPS * f:GROUPS * f + GROUPS, ds(t * P, w)],
                                 digits[:, f, :].rearrange("p (g m) -> p g m", g=GROUPS)[:, :, 0:w], ACT.Copy,
                                 accum_out=count[:, ds(t, 1), f:f + 1].rearrange("p a b -> p (a b)")).then_inc(sem("digits_stored"), 1)

            act.sem_inc(sem("digits_stored"), DIGITS)
            act.sem_inc(sem("dist_set"), 2)
            act.sem_inc(sem("D_set"), 2)
            act.wait_ge(sem("entries_set"), 1)
            def between_batches(t, par, i):
                if not isinstance(t, int) or t >= LAG:
                    store_digits(t - LAG, P, SHARES[i])
                if i == LEAST - 1 and (not isinstance(t, int) or t >= 1):
                    packed_out(t - 1, par)
                if i == LEAST - 1 and (not isinstance(t, int) or t >= 2):
                    packedT_in(t - 2)

            for t in range(LAG):
                dest_rows(t, lambda i: between_batches(t, (t - 1) % 2, i))
            with act.Fori(LAG, TILES, 2) as t:
                t = by_twos(t, LAG, TILES)
                for n in range(2):
                    dest_rows(t + n, lambda i: between_batches(t + n, n, i))
            packed_out(TILES - 1, (TILES - 1) % 2)
            for c in range(NC + 1):
                rows, k = (P, 4) if c < NC else (LAST, 1)
                act.wait_ge(sem(f"x_in{c}"), 16)
                if c == NC:
                    act.wait_ge(sem("xp_zeroed"), 1)
                a.activation(xp[0:rows, 4 * c:4 * c + k, 0, :], xstage[0:rows, 4 * c:4 * c + k, :], ACT.Copy).then_inc(sem("x_hi"), 1)
            store_digits(TILES - 3, P)
            packedT_in(TILES - 2)
            store_digits(TILES - 2, P)
            packedT_in(TILES - 1)
            store_digits(TILES - 1, LASTW)

            general = is_general_after_flag(act)

            def general_out(n):
                with act.If(general):
                    act.wait_ge(sem("g_summed"), n + 1)
                    if n == 0:
                        ins = a.activation(Cn[:, 0:TILES, :].rearrange("p t k -> p (t k)"), PS[:, 0, 0:TILES * NTYPE], ACT.Copy)
                    else:
                        for b in range(-(-TILES // 4)):
                            k = min(4, TILES - 4 * b)
                            ins = a.activation(g_sum[:, 4 * b:4 * b + k, :], PS[:, b, 0:k * F].rearrange("p (t f) -> p t f", f=F), ACT.Copy)
                    ins.then_inc(sem("g_copied"), 1)
                    act.wait_ge(sem("g_copied"), n + 1)
                with act.Else():
                    act.nop()

            general_out(0)
            act.wait_ge(sem("packed_out"), TILES)
            a.activation(sd[:, 0:1], eps[:, :], ACT.Copy).then_inc(sem("types_ready"), 1)
            general_out(1)

            def sqrt_var(name, q, rows, k):
                act.wait_ge(sem(f"{name}_norm"), 3 * q + 2)
                a.activation(sd[0:rows, 0:k], meanvar[0:rows, 0:k, 1:2].rearrange("p t a -> p (t a)"), ACT.Sqrt, bias=eps[0:rows, :]).then_inc(sem(f"{name}_sd"), 1)

            def high_parts(name, target, full, rest, q, last):
                rows, k = (LASTW, 1) if last else (P, 4)
                if last:
                    act.wait_ge(sem("x1p_zeroed" if name == "p1" else "xp_zeroed"), 1)
                a.activation(target[0:rows, ds(4 * q, k), 0, :], full[0:rows, 0:k * F].rearrange("p (t f) -> p t f", f=F), ACT.Copy).then_inc(sem(f"{name}_hi"), 1)
                act.wait_ge(sem(f"{name}_rest"), q + 1)
                a.activation(target[0:rows, ds(4 * q, k), 1, :], rest[0:rows, 0:k * F].rearrange("p (t f) -> p t f", f=F), ACT.Copy).then_inc(sem(f"{name}_mid"), 1)

            def stage_types(name, q):
                a.activation(c_stage[:, :, :], Cn[:, ds(4 * q, 4), :], ACT.Copy).then_inc(sem(f"{name}_types_staged"), 1)

            def stage_sums(name, q):
                settle(act, "act_settled")
                with act.If(general):
                    a.activation(g_stage[:, :, :], g_sum[:, ds(4 * q, 4), :], ACT.Copy).then_inc(sem(f"{name}_sum_staged"), 1)
                with act.Else():
                    act.nop()

            def sums_out(q, w):
                act.wait_ge(sem("p1_agg"), q + 1)
                act.wait_ge(sem("p1_m_sum"), q)
                a.activation(slot[0][:, 0:w], PS[:, 0, 0:w], ACT.Copy).then_inc(sem("p1_s"), 1)
                act.wait_ge(sem("p1_typeT"), q + 1)
                if not isinstance(q, int) or q < NC:
                    stage_sums("p1", q + 1)
                    stage_types("p1", q + 1)
                a.activation(slot[7][0:NTYPE, 0:w], PS[0:NTYPE, 2, 0:w], ACT.Copy).then_inc(sem("p1_c"), 1)

            def gate_functions(q, w):
                act.wait_ge(sem("p1_gates"), q + 1)
                act.wait_ge(sem("p1_y"), q)
                a.activation(slot[3][:, 0:w], PS[:, 4, 0:w], ACT.Sigmoid, bias=rz_b[:, 0:1]).then_inc(sem("p1_r"), 1)
                act.wait_ge(sem("p1_yT"), q)
                a.activation(slot[4][:, 0:w], PS[:, 5, 0:w], ACT.Sigmoid, bias=rz_b[:, 1:2])
                act.wait_ge(sem("p1_t"), 2 * q + 2)
                act.wait_ge(sem("p1_low"), q)
                a.activation(slot[6][:, 0:w], slot[5][:, 0:w], ACT.Tanh, bias=gate_b[:, 2:3]).then_inc(sem("p1_n"), 1)

            def normed(q, last):
                sqrt_var("p1", q, LASTW if last else P, 1 if last else 4)
                act.wait_ge(sem("p1_x1"), q + 1)
                high_parts("p1", x1p, slot[5], slot[6], q, last)

            act.wait_ge(sem("x_split"), NC + 1)
            stage_sums("p1", 0)
            stage_types("p1", 0)
            sums_out(0, 512)
            with act.Fori(1, NC) as q:
                gate_functions(q - 1, 512)
                sums_out(q, 512)
                normed(q - 1, False)
            gate_functions(NC - 1, 512)
            sums_out(NC, LASTW)
            normed(NC - 1, False)
            gate_functions(NC, LASTW)
            normed(NC, True)

            act.wait_ge(sem("p1_done"), 1)
            general_out(2)

            def inputs_out(q, w):
                act.wait_ge(sem("p2_x1T"), q + 1)
                act.wait_ge(sem("p2_h_sum"), 2 * q)
                a.activation(slot[3][:, 0:w], PS[:, 2 if isinstance(q, int) and q == 0 else 1, 0:w], ACT.Copy).then_inc(sem("p2_x1c"), 1)

            def relu_rows(q, w):
                act.wait_ge(sem("p2_y_sum"), q)
                for n, sl in enumerate((slot[1], slot[6])):
                    act.wait_ge(sem("p2_h_sum"), 2 * q + n + 1)
                    a.activation(sl[:, 0:w], PS[:, 6 + n, 0:w], ACT.Relu, bias=b1_s[:, n:n + 1]).then_inc(sem("p2_h"), 1)

            def second_out(q, last):
                rows, k = (LASTW, 1) if last else (P, 4)
                act.wait_ge(sem("p2_y_sum"), q + 1)
                act.wait_ge(sem("p2_y_out"), 16 * q)
                act.wait_ge(sem("p2_low"), q)
                a.activation(slot[4][0:rows, 0:k * F], PS[0:rows, 3, 0:k * F], ACT.Copy).then_inc(sem("p2_yf"), 1)
                act.wait_ge(sem("p2_yf"), q + 1)
                high_parts("p2", xp, slot[4], slot[7], q, last)

            stage_sums("p2", 0)
            inputs_out(0, 512)
            with act.Fori(1, NC) as q:
                relu_rows(q - 1, 512)
                stage_sums("p2", q)
                inputs_out(q, 512)
                second_out(q - 1, False)
            relu_rows(NC - 1, 512)
            stage_sums("p2", NC)
            inputs_out(NC, LASTW)
            second_out(NC - 1, False)
            relu_rows(NC, LASTW)
            second_out(NC, True)

            act.wait_ge(sem("p2_done"), 1)
            general_out(3)
            with act.Fori(0, NC) as q:
                sqrt_var("p3", q, P, 4)
            sqrt_var("p3", NC, LAST, 1)


def kernel(**inputs):
    import numpy as np
    import concourse.bacc as bacc
    from concourse.bass_utils import run_bass_kernel_spmd

    nc = bacc.Bacc("TRN2", target_bir_lowering=False, num_devices=1, dynamic_dma_scratch_size=SCRATCH)
    a = {k: np.asarray(v) for k, v in inputs.items()}
    arrays = {
        "x": a["x"], "xT": a["x"].T,
        "dst_c": a["dst"][:FULL * P].reshape(FULL, P).T, "dst_t": a["dst"][FULL * P:].reshape(TAIL, 1),
        "src_c": a["src"][:FULL * P].reshape(FULL, P).T, "src_t": a["src"][FULL * P:].reshape(TAIL, 1),
        "typ_c": a["edge_type_9"][:FULL * P].reshape(FULL, P).T, "typ_t": a["edge_type_9"][FULL * P:].reshape(TAIL, 1),
        "wmsgT": a["L0_gnn_W_msg"].T, "bmsg": a["L0_gnn_b_msg"].reshape(1, F), "embed": a["L0_gnn_edge_embed"],
        "wihT": a["L0_gnn_W_ih"].T, "whhT": a["L0_gnn_W_hh"].T,
        "bgate": np.concatenate([a["L0_gnn_b_ih"].reshape(3, F), a["L0_gnn_b_hh"].reshape(3, F)]).T,
        "wself1": a["L1_gnn_w_self1"], "wneigh1": a["L1_gnn_w_neigh1"], "b1": a["L1_gnn_b1"].reshape(2, F).T,
        "wself2": a["L1_gnn_w_self2"], "wneigh2": a["L1_gnn_w_neigh2"], "b2": a["L1_gnn_b2"].reshape(1, F),
    }
    arrays = {k: np.ascontiguousarray(v) for k, v in arrays.items()}
    args = [nc.dram_tensor(k, v.shape, mybir.dt.from_np(v.dtype), kind="ExternalInput").ap() for k, v in arrays.items()]
    fp32 = mybir.dt.float32
    scratch = [nc.dram_tensor(k, (DW, F), fp32, kind="Internal").ap() for k in ("x1_rows", "y_rows", "res_rows")]
    out = nc.dram_tensor("out_rows", (N, F), fp32, kind="ExternalOutput").ap()
    graph_kernel(nc, *args, *scratch, out)
    return run_bass_kernel_spmd(nc, [arrays], core_ids=[0]).results[0]["out_rows"]
```
